# Optimizing a Trainium2 kernel written in Bass

```python
import numpy as np
import jax
import jax.numpy as jnp

def _softmax(x, axis=-1):
    return jax.nn.softmax(x, axis=axis)

def _gelu(x):
    return jax.nn.gelu(x, approximate=True)

def _silu(x):
    return jax.nn.silu(x)

def _sigmoid(x):
    return jax.nn.sigmoid(x)

def _layernorm(x, axis=-1, eps=1e-05):
    m = jnp.mean(x, axis=axis, keepdims=True)
    v = jnp.var(x, axis=axis, keepdims=True)
    return (x - m) / jnp.sqrt(v + eps)

def _scatter_add(tgt, idx, src, axis=0):
    return tgt.at[idx].add(src)

def _segment_sum(src, seg, n):
    return jax.ops.segment_sum(src, seg, n)
kernel_name = 'mk_flamingo_gated_d2_seqx_r4_4cceda'

def setup_inputs(seed: int=0):
    np.random.seed(seed)
    _w = jnp.asarray

    def _rec_inputs():
        import jax
        import jax.numpy as jnp
        _rk = jax.random.key(seed)
        x = -0.0005207 + 1.001 * jax.random.normal(jax.random.fold_in(_rk, 1), (8, 512, 256), jnp.float32)
        _lenS = 512 - jax.random.randint(jax.random.fold_in(_rk, 7), (8,), 0, max(1, 512 // 4) + 1, jnp.int32)
        _lenS2 = 1024 - jax.random.randint(jax.random.fold_in(_rk, 8), (8,), 0, max(1, 1024 // 4) + 1, jnp.int32)
        _ctx_1024P = jax.random.normal(jax.random.fold_in(_rk, 11), (8, 16, 256), jnp.float32)
        _ctx_1024c = jax.random.dirichlet(jax.random.fold_in(_rk, 511), 0.3 * jnp.ones((16,), jnp.float32), (8, 1024))
        _ctx_1024t = jnp.einsum('bsk,bkd->bsd', _ctx_1024c, _ctx_1024P)
        _ctx_1024t = _ctx_1024t * jax.lax.rsqrt(jnp.mean(jnp.square(_ctx_1024t)) + 1e-12) * 0.953939
        ctx_1024 = -1.52775e-05 + 0.999936 * (_ctx_1024t + 0.3 * jax.random.normal(jax.random.fold_in(_rk, 611), (8, 1024, 256), jnp.float32))
        _validS = jnp.arange(512)[None, :] < _lenS[:, None]
        _validS2 = jnp.arange(1024)[None, :] < _lenS2[:, None]
        _causal = jnp.tril(jnp.ones((512, 512), dtype=bool))
        mask_1xSxS2_ff0 = jnp.where(jnp.ones((1, 512, 1024), dtype=bool), 0.0, -1000000000.0).astype(jnp.float32)
        _g = jax.random.normal(jax.random.fold_in(_rk, 9001), (2, 2), jnp.float32)
        _g = jnp.sign(_g) * jnp.maximum(jnp.abs(_g), 1.0) + (_g == 0) * 1.0
        g_xattn = _g[0]
        g_ffn = _g[1]
        return (x, ctx_1024, mask_1xSxS2_ff0, g_xattn, g_ffn)
    x, ctx_1024, mask_1xSxS2_ff0, g_xattn, g_ffn = _rec_inputs()

    def _L0_xattn_setup():
        import jax, jax.numpy as jnp
        import numpy as np
        DIM = 256
        HEADS = 16
        DHEAD = 64
        INNER = HEADS * DHEAD
        EPS = 1e-05

        def layer_norm(x, g, b):
            mu = jnp.mean(x, axis=-1, keepdims=True)
            var = jnp.mean(jnp.square(x - mu), axis=-1, keepdims=True)
            return (x - mu) * jax.lax.rsqrt(var + EPS) * g + b

        def apply_rope(x, cos, sin):
            d2 = x.shape[-1] // 2
            x1, x2 = (x[..., :d2], x[..., d2:])
            return jnp.concatenate([x1 * cos - x2 * sin, x2 * cos + x1 * sin], axis=-1)
        key = jax.random.key(seed)
        ks = jax.random.split(key, 10)
        B, N, S = (8, 64, 1024)
        latents = jax.random.normal(ks[0], (B, N, DIM), dtype=jnp.float32)
        context = jax.random.normal(ks[1], (B, S, DIM), dtype=jnp.float32)
        cos = jax.random.uniform(ks[2], (S, DHEAD // 2), dtype=jnp.float32)
        sin = jax.random.uniform(ks[3], (S, DHEAD // 2), dtype=jnp.float32)
        init = lambda k, shp, fan_in: jax.random.normal(k, shp, dtype=jnp.float32) / np.sqrt(fan_in)
        return {'latents': latents, 'context': context, 'cos': cos, 'sin': sin, 'ln_lat_g': jnp.ones((DIM,), jnp.float32), 'ln_lat_b': jnp.zeros((DIM,), jnp.float32), 'ln_ctx_g': jnp.ones((DIM,), jnp.float32), 'ln_ctx_b': jnp.zeros((DIM,), jnp.float32), 'Wq': init(ks[4], (DIM, INNER), DIM), 'Wkv': init(ks[5], (DIM, 2 * INNER), DIM), 'Wo': init(ks[6], (INNER, DIM), INNER), 'bo': jnp.zeros((DIM,), jnp.float32)}
    _L0_xattn_all = _L0_xattn_setup()
    _L0_xattn_in = {k: v for k, v in _L0_xattn_all.items() if k in ('cos', 'sin', 'ln_lat_g', 'ln_lat_b', 'ln_ctx_g', 'ln_ctx_b', 'Wq', 'Wkv', 'Wo', 'bo')}
    del _L0_xattn_all

    def _L0_ffn_setup():
        import jax, jax.numpy as jnp
        import numpy as np
        D_MODEL = 256
        D_QUERY = 64
        NUM_HEADS = 4
        NUM_EXPERTS = 4096
        NUM_SUB = 128
        TOP_K = 8
        D_LATENT = 64
        D_HIDDEN = 128
        BATCH, SEQ = (4, 512)
        BN_EPS = 1e-05

        def _gelu(v):
            return jax.nn.gelu(v, approximate=False)
        key = jax.random.key(seed)
        ks = jax.random.split(key, 10)

        def rn(k, shape, scale=1.0):
            return jax.random.normal(k, shape, dtype=jnp.float32) * scale
        x = rn(ks[0], (BATCH, SEQ, D_MODEL))
        Wq = rn(ks[1], (NUM_HEADS, D_QUERY, D_MODEL), 1.0 / np.sqrt(D_MODEL))
        bq = rn(ks[2], (NUM_HEADS, D_QUERY), 0.01)
        gamma = 1.0 + rn(ks[3], (NUM_HEADS, D_QUERY), 0.1)
        beta = rn(ks[4], (NUM_HEADS, D_QUERY), 0.1)
        sk1 = rn(ks[5], (NUM_SUB, D_QUERY // 2), 1.0 / np.sqrt(D_QUERY // 2))
        sk2 = rn(ks[6], (NUM_SUB, D_QUERY // 2), 1.0 / np.sqrt(D_QUERY // 2))
        latents = rn(ks[7], (NUM_EXPERTS, D_LATENT))
        W1 = rn(ks[8], (D_LATENT, D_HIDDEN), 1.0 / np.sqrt(D_LATENT))
        W2 = rn(ks[9], (D_HIDDEN, 2 * D_MODEL), 1.0 / np.sqrt(D_HIDDEN))
        return {'x': x, 'Wq': Wq, 'bq': bq, 'gamma': gamma, 'beta': beta, 'sk1': sk1, 'sk2': sk2, 'latents': latents, 'W1': W1, 'W2': W2}
    _L0_ffn_all = _L0_ffn_setup()
    _L0_ffn_in = {k: v for k, v in _L0_ffn_all.items() if k in ('Wq', 'bq', 'gamma', 'beta', 'sk1', 'sk2', 'latents', 'W1', 'W2')}
    del _L0_ffn_all

    def _L1_xattn_setup():
        import jax, jax.numpy as jnp
        import numpy as np
        B, S, D_IN, D_MODEL = (4, 512, 256, 256)
        key = jax.random.key(seed)
        ks = jax.random.split(key, 8)
        glorot = np.sqrt(6.0 / (D_IN + D_MODEL))
        inp = {'q': jax.random.normal(ks[0], (B, S, D_IN), dtype=jnp.float32), 'k': jax.random.normal(ks[1], (B, S, D_IN), dtype=jnp.float32), 'v': jax.random.normal(ks[2], (B, S, D_IN), dtype=jnp.float32), 'mask': jnp.zeros((1, S, S), dtype=jnp.float32), 'kernel_q': jax.random.uniform(ks[3], (1, 1, D_IN, D_MODEL), jnp.float32, -glorot, glorot), 'kernel_k': jax.random.uniform(ks[4], (1, 1, D_IN, D_MODEL), jnp.float32, -glorot, glorot), 'kernel_v': jax.random.uniform(ks[5], (1, 1, D_IN, D_MODEL), jnp.float32, -glorot, glorot), 'bias_q': 0.05 * jax.random.normal(ks[6], (D_MODEL,), dtype=jnp.float32), 'bias_k': 0.05 * jax.random.normal(ks[7], (D_MODEL,), dtype=jnp.float32), 'bias_v': 0.05 * jax.random.normal(jax.random.fold_in(key, 7), (D_MODEL,), dtype=jnp.float32)}
        return inp
    _L1_xattn_all = _L1_xattn_setup()
    _L1_xattn_in = {k: v for k, v in _L1_xattn_all.items() if k in ('kernel_q', 'kernel_k', 'kernel_v', 'bias_q', 'bias_k', 'bias_v')}
    del _L1_xattn_all

    def _L1_ffn_setup():
        import jax, jax.numpy as jnp
        import numpy as np
        TOP_K = 2
        E = 8
        D = 256
        F = 512
        B, S = (2, 256)
        key = jax.random.key(seed)
        ks = jax.random.split(key, 8)
        sc = 0.02
        return {'x_bsD': jax.random.normal(ks[0], (B, S, D), dtype=jnp.float32), 'router_DE': jax.random.normal(ks[1], (D, E), dtype=jnp.float32) * sc, 'w_in_shared_FD': jax.random.normal(ks[2], (F, D), dtype=jnp.float32) * sc, 'w_out_shared_DF': jax.random.normal(ks[3], (D, F), dtype=jnp.float32) * sc, 'w_swiglu_FD': jax.random.normal(ks[4], (F, D), dtype=jnp.float32) * sc, 'w_in_eDF': jax.random.normal(ks[5], (E, D, F), dtype=jnp.float32) * sc, 'w_swiglu_eDF': jax.random.normal(ks[6], (E, D, F), dtype=jnp.float32) * sc, 'w_out_eFD': jax.random.normal(ks[7], (E, F, D), dtype=jnp.float32) * sc}
    _L1_ffn_all = _L1_ffn_setup()
    _L1_ffn_in = {k: v for k, v in _L1_ffn_all.items() if k in ('router_DE', 'w_in_shared_FD', 'w_out_shared_DF', 'w_swiglu_FD', 'w_in_eDF', 'w_swiglu_eDF', 'w_out_eFD')}
    del _L1_ffn_all
    return {'x': x, 'ctx_1024': ctx_1024, 'mask_1xSxS2_ff0': mask_1xSxS2_ff0, 'g_xattn': g_xattn, 'g_ffn': g_ffn, 'L0_xattn_cos': _L0_xattn_in['cos'], 'L0_xattn_sin': _L0_xattn_in['sin'], 'L0_xattn_ln_lat_g': _L0_xattn_in['ln_lat_g'], 'L0_xattn_ln_lat_b': _L0_xattn_in['ln_lat_b'], 'L0_xattn_ln_ctx_g': _L0_xattn_in['ln_ctx_g'], 'L0_xattn_ln_ctx_b': _L0_xattn_in['ln_ctx_b'], 'L0_xattn_Wq': _L0_xattn_in['Wq'], 'L0_xattn_Wkv': _L0_xattn_in['Wkv'], 'L0_xattn_Wo': _L0_xattn_in['Wo'], 'L0_xattn_bo': _L0_xattn_in['bo'], 'L0_ffn_Wq': _L0_ffn_in['Wq'], 'L0_ffn_bq': _L0_ffn_in['bq'], 'L0_ffn_gamma': _L0_ffn_in['gamma'], 'L0_ffn_beta': _L0_ffn_in['beta'], 'L0_ffn_sk1': _L0_ffn_in['sk1'], 'L0_ffn_sk2': _L0_ffn_in['sk2'], 'L0_ffn_latents': _L0_ffn_in['latents'], 'L0_ffn_W1': _L0_ffn_in['W1'], 'L0_ffn_W2': _L0_ffn_in['W2'], 'L1_xattn_kernel_q': _L1_xattn_in['kernel_q'], 'L1_xattn_kernel_k': _L1_xattn_in['kernel_k'], 'L1_xattn_kernel_v': _L1_xattn_in['kernel_v'], 'L1_xattn_bias_q': _L1_xattn_in['bias_q'], 'L1_xattn_bias_k': _L1_xattn_in['bias_k'], 'L1_xattn_bias_v': _L1_xattn_in['bias_v'], 'L1_ffn_router_DE': _L1_ffn_in['router_DE'], 'L1_ffn_w_in_shared_FD': _L1_ffn_in['w_in_shared_FD'], 'L1_ffn_w_out_shared_DF': _L1_ffn_in['w_out_shared_DF'], 'L1_ffn_w_swiglu_FD': _L1_ffn_in['w_swiglu_FD'], 'L1_ffn_w_in_eDF': _L1_ffn_in['w_in_eDF'], 'L1_ffn_w_swiglu_eDF': _L1_ffn_in['w_swiglu_eDF'], 'L1_ffn_w_out_eFD': _L1_ffn_in['w_out_eFD']}

def reference(x, ctx_1024, mask_1xSxS2_ff0, g_xattn, g_ffn, L0_xattn_cos, L0_xattn_sin, L0_xattn_ln_lat_g, L0_xattn_ln_lat_b, L0_xattn_ln_ctx_g, L0_xattn_ln_ctx_b, L0_xattn_Wq, L0_xattn_Wkv, L0_xattn_Wo, L0_xattn_bo, L0_ffn_Wq, L0_ffn_bq, L0_ffn_gamma, L0_ffn_beta, L0_ffn_sk1, L0_ffn_sk2, L0_ffn_latents, L0_ffn_W1, L0_ffn_W2, L1_xattn_kernel_q, L1_xattn_kernel_k, L1_xattn_kernel_v, L1_xattn_bias_q, L1_xattn_bias_k, L1_xattn_bias_v, L1_ffn_router_DE, L1_ffn_w_in_shared_FD, L1_ffn_w_out_shared_DF, L1_ffn_w_swiglu_FD, L1_ffn_w_in_eDF, L1_ffn_w_swiglu_eDF, L1_ffn_w_out_eFD):
    import jax
    import jax.numpy as jnp

    def _L0_xattn_ref(latents, context, cos, sin, ln_lat_g, ln_lat_b, ln_ctx_g, ln_ctx_b, Wq, Wkv, Wo, bo):
        import jax, jax.numpy as jnp
        import numpy as np
        DIM = 256
        HEADS = 16
        DHEAD = 64
        INNER = HEADS * DHEAD
        EPS = 1e-05

        def layer_norm(x, g, b):
            mu = jnp.mean(x, axis=-1, keepdims=True)
            var = jnp.mean(jnp.square(x - mu), axis=-1, keepdims=True)
            return (x - mu) * jax.lax.rsqrt(var + EPS) * g + b

        def apply_rope(x, cos, sin):
            d2 = x.shape[-1] // 2
            x1, x2 = (x[..., :d2], x[..., d2:])
            return jnp.concatenate([x1 * cos - x2 * sin, x2 * cos + x1 * sin], axis=-1)
        b, n, _ = latents.shape
        s = context.shape[1]
        lat = layer_norm(latents, ln_lat_g, ln_lat_b)
        ctx = layer_norm(context, ln_ctx_g, ln_ctx_b)
        q = (lat @ Wq).reshape(b, n, HEADS, DHEAD).transpose(0, 2, 1, 3)
        kv = ctx @ Wkv
        k, v = jnp.split(kv, 2, axis=-1)
        k = k.reshape(b, s, HEADS, DHEAD).transpose(0, 2, 1, 3)
        v = v.reshape(b, s, HEADS, DHEAD).transpose(0, 2, 1, 3)
        k = apply_rope(k, cos[None, None], sin[None, None])
        scale = DHEAD ** (-0.5)
        attn = jnp.einsum('bhnd,bhsd->bhns', q, k) * scale
        attn = jnp.clip(attn, -11.0, 11.0)
        attn = jax.nn.softmax(attn, axis=-1)
        out = jnp.einsum('bhns,bhsd->bhnd', attn, v)
        out = out.transpose(0, 2, 1, 3).reshape(b, n, INNER)
        return out @ Wo + bo

    def _L0_ffn_ref(x, Wq, bq, gamma, beta, sk1, sk2, latents, W1, W2):
        import jax, jax.numpy as jnp
        import numpy as np
        D_MODEL = 256
        D_QUERY = 64
        NUM_HEADS = 4
        NUM_EXPERTS = 4096
        NUM_SUB = 128
        TOP_K = 8
        D_LATENT = 64
        D_HIDDEN = 128
        BATCH, SEQ = (4, 512)
        BN_EPS = 1e-05

        def _gelu(v):
            return jax.nn.gelu(v, approximate=False)
        B, S, D = x.shape
        xf = x.reshape(-1, D)
        N = xf.shape[0]
        q = jnp.einsum('nd,hqd->nhq', xf, Wq) + bq
        mean = q.mean(axis=0)
        var = q.var(axis=0)
        qn = (q - mean) / jnp.sqrt(var + BN_EPS) * gamma + beta
        q1, q2 = jnp.split(qn, 2, axis=-1)
        s1 = jnp.einsum('nhq,kq->nhk', q1, sk1)
        s2 = jnp.einsum('nhq,kq->nhk', q2, sk2)
        kc = TOP_K * 2
        ts1, ti1 = jax.lax.top_k(s1, kc)
        ts2, ti2 = jax.lax.top_k(s2, kc)
        comb = (ts1[..., :, None] + ts2[..., None, :]).reshape(N, NUM_HEADS, kc * kc)
        fs, tci = jax.lax.top_k(comb, TOP_K)
        probs = jax.nn.softmax(fs.astype(jnp.float32), axis=-1).astype(xf.dtype)
        i1 = jnp.take_along_axis(ti1, tci // kc, axis=-1)
        i2 = jnp.take_along_axis(ti2, tci % kc, axis=-1)
        eidx = i1 * NUM_SUB + i2
        H_all = _gelu(latents @ W1)
        x_proj = jnp.einsum('nd,fd->nf', xf, W2[:, :D])
        Wv = W2[:, D:]
        hg = H_all[eidx]
        act = _gelu(jnp.einsum('nhkf,nf->nhk', hg, x_proj)) * probs
        acc = jnp.einsum('nhk,nhkf->nf', act, hg)
        out = acc @ Wv / NUM_HEADS
        return out.reshape(B, S, D)

    def _L1_xattn_ref(q, k, v, mask, kernel_q, kernel_k, kernel_v, bias_q, bias_k, bias_v):
        import jax, jax.numpy as jnp
        import numpy as np
        B, S, D_IN, D_MODEL = (4, 512, 256, 256)
        Wq, Wk, Wv = (kernel_q[0, 0], kernel_k[0, 0], kernel_v[0, 0])
        qp = jax.nn.relu(jnp.einsum('bsd,de->bse', q, Wq) + bias_q)
        kp = jax.nn.relu(jnp.einsum('bsd,de->bse', k, Wk) + bias_k)
        vp = jax.nn.relu(jnp.einsum('bsd,de->bse', v, Wv) + bias_v)
        scores = jax.nn.relu(jnp.einsum('bqe,bke->bqk', qp, kp))
        dk = jnp.asarray(kp.shape[-1], dtype=scores.dtype)
        logits = scores / jnp.sqrt(dk) + mask
        out = jax.nn.relu(jnp.einsum('bqk,bke->bqe', logits, vp))
        return out

    def _L1_ffn_ref(x_bsD, router_DE, w_in_shared_FD, w_out_shared_DF, w_swiglu_FD, w_in_eDF, w_swiglu_eDF, w_out_eFD):
        import jax, jax.numpy as jnp
        import numpy as np
        TOP_K = 2
        E = 8
        D = 256
        F = 512
        B, S = (2, 256)
        b, s, d = x_bsD.shape
        x_aD = x_bsD.reshape(-1, d)
        a = x_aD.shape[0]
        scores_aE = x_aD @ router_DE
        topv_aK, topi_aK = jax.lax.top_k(scores_aE, TOP_K)
        masked_aE = jnp.full_like(scores_aE, -jnp.inf)
        masked_aE = masked_aE.at[jnp.arange(a)[:, None], topi_aK].set(topv_aK)
        gates_Ea = jax.nn.sigmoid(masked_aE.astype(jnp.float32)).astype(x_aD.dtype).T
        routed_in_EaD = x_aD[None, :, :] * gates_Ea[:, :, None]
        routed_in_EaD = jax.lax.stop_gradient(routed_in_EaD)
        mid_EaF = jnp.einsum('ead,edf->eaf', routed_in_EaD, w_in_eDF)
        sw_EaF = jnp.einsum('ead,edf->eaf', routed_in_EaD, w_swiglu_eDF)
        h_EaF = jax.nn.silu(mid_EaF) * sw_EaF
        out_EaD = jnp.einsum('eaf,efd->ead', h_EaF, w_out_eFD)
        shared_aF = jax.nn.silu(x_aD @ w_in_shared_FD.T) * (x_aD @ w_swiglu_FD.T)
        shared_out_aD = jax.lax.stop_gradient(shared_aF @ w_out_shared_DF.T)
        out_aD = shared_out_aD + jnp.sum(out_EaD, axis=0)
        return out_aD.reshape(b, s, d)
    x = x + jnp.tanh(g_xattn[0]) * _L0_xattn_ref(_layernorm(x, axis=-1), ctx_1024, L0_xattn_cos, L0_xattn_sin, L0_xattn_ln_lat_g, L0_xattn_ln_lat_b, L0_xattn_ln_ctx_g, L0_xattn_ln_ctx_b, L0_xattn_Wq, L0_xattn_Wkv, L0_xattn_Wo, L0_xattn_bo)
    x = x + jnp.tanh(g_ffn[0]) * _L0_ffn_ref(_layernorm(x, axis=-1), L0_ffn_Wq, L0_ffn_bq, L0_ffn_gamma, L0_ffn_beta, L0_ffn_sk1, L0_ffn_sk2, L0_ffn_latents, L0_ffn_W1, L0_ffn_W2)
    x = x + jnp.tanh(g_xattn[1]) * _L1_xattn_ref(_layernorm(x, axis=-1), ctx_1024, ctx_1024, mask_1xSxS2_ff0, L1_xattn_kernel_q, L1_xattn_kernel_k, L1_xattn_kernel_v, L1_xattn_bias_q, L1_xattn_bias_k, L1_xattn_bias_v)
    x = x + jnp.tanh(g_ffn[1]) * _L1_ffn_ref(_layernorm(x, axis=-1), L1_ffn_router_DE, L1_ffn_w_in_shared_FD, L1_ffn_w_out_shared_DF, L1_ffn_w_swiglu_FD, L1_ffn_w_in_eDF, L1_ffn_w_swiglu_eDF, L1_ffn_w_out_eFD)
    return x

_drawn_inputs = setup_inputs


def setup_inputs(seed=0):
    import zlib

    import numpy as np

    out = dict(_drawn_inputs(seed))
    spreads = {'g_ffn': (-1.0, 0.6),
     'L0_xattn_ln_lat_g': (1.0, 0.6),
     'L0_xattn_ln_lat_b': (0.0, 2.0),
     'L0_xattn_ln_ctx_g': (1.0, 0.6),
     'L0_xattn_ln_ctx_b': (0.0, 0.619),
     'L0_xattn_bo': (0.0, 0.8)}
    factors = {'L0_xattn_cos': 64.0,
     'L0_xattn_sin': 64.0,
     'L0_xattn_Wq': 3.249,
     'L0_ffn_bq': 64.0,
     'L0_ffn_gamma': 30.106,
     'L0_ffn_beta': 25.554,
     'L1_xattn_bias_q': 8.0,
     'L1_xattn_bias_k': 7.845,
     'L1_ffn_router_DE': 37.476,
     'L1_ffn_w_in_shared_FD': 47.97,
     'L1_ffn_w_out_shared_DF': 43.604,
     'L1_ffn_w_swiglu_FD': 42.603,
     'L1_ffn_w_in_eDF': 40.484,
     'L1_ffn_w_swiglu_eDF': 34.476,
     'L1_ffn_w_out_eFD': 35.264}
    for name, (base, spread) in spreads.items():
        noise = np.random.default_rng([zlib.crc32(name.encode()), seed]).standard_normal(out[name].shape)
        drawn = base * np.exp(spread * noise) if base else spread * noise
        out[name] = jnp.asarray(drawn.astype(out[name].dtype))
    for name, factor in factors.items():
        out[name] = (out[name] * factor).astype(out[name].dtype)
    return out
```

```python
from contextlib import ExitStack

import numpy as np

import concourse.bass as bass
import concourse.mybir as mybir
from concourse.alu_op_type import AluOpType as ALU

F32 = mybir.dt.float32
U32 = mybir.dt.uint32
ACT = mybir.ActivationFunctionType
AX = mybir.AxisListType

P = 128
BATCH, SEQ, DIM, CTX = 8, 512, 256, 1024
HEADS, DHEAD = 16, 64
INNER = HEADS * DHEAD
DC = DIM // P
XT = SEQ // P
KT = CTX // P
PAIRS = HEADS // 2
HALF = 512
EPS = 1e-5
CLIP, SCALE = 11.0, DHEAD ** -0.5


class Shared:

    def __init__(self, nc, ctx):
        self.x = ctx.enter_context(nc.sbuf_tensor("x_res", [P, BATCH, XT, DIM], F32))
        self.gate = ctx.enter_context(nc.sbuf_tensor("gate", [P, 4], F32))
        self.ident = ctx.enter_context(nc.sbuf_tensor("ident", [P, P], F32))
        self.eps = ctx.enter_context(nc.sbuf_tensor("epsilon", [P, 16], F32))
        self.mhalf = ctx.enter_context(nc.sbuf_tensor("minus_half", [P, 16], F32))



UNITS = PAIRS * KT
SCORE_SLOTS, PROB_SLOTS = 2, 4
ADD_LAG = 2
AV_LAG = 2


def rope_attention_misc():
    order = [("ctxT", c, h) for c in range(DC) for h in range(2)] + [("latT", c) for c in range(DC)]
    order += [("v", kt, 0) for kt in range(KT)]
    order += [("k", 0, 0), ("k", 0, 1), ("q", 0)]
    for i in range(UNITS):
        order += rope_attention_extras(i)
    order += [("den", PAIRS - 1)] + [("o", m) for m in range(XT // 2)]
    assert len(order) % 2 == 0
    return {name: n for n, name in enumerate(order)}


def rope_attention_extras(i):
    t, kt = divmod(i, KT)
    out = []
    if t + 1 < PAIRS and kt < 2:
        out.append(("k", t + 1, kt))
    if t + 1 < PAIRS and kt == 2:
        out.append(("q", t + 1))
    if kt == 3 and t >= 1:
        out.append(("den", t - 1))
    if t < 4 and kt in (4, 6):
        out.append(("v", 2 * t + (kt == 6), 1))
    return out


def rope_attention(nc, sh, d):
    MISC = rope_attention_misc()
    NM = len(MISC)
    with ExitStack() as ctx:
        def sb(name, shape):
            return ctx.enter_context(nc.sbuf_tensor("s1_" + name, shape, F32))

        def sem(name):
            return ctx.enter_context(nc.semaphore(name))

        x_res, gate, ident, mhalf, eps = sh.x, sh.gate, sh.ident, sh.mhalf, sh.eps
        wq, wkv, wo = sb("wq", [P, DC, INNER]), sb("wkv", [P, DC, 2 * INNER]), sb("wo", [P, PAIRS, DIM])
        cosT, sinT = sb("cosT", [P, CTX]), sb("sinT", [P, CTX])
        affine = sb("affine", [P, 4, DC])
        bo = sb("bo", [P, DIM])
        ctx_in, ctx_norm = sb("ctx_in", [P, KT, DIM]), sb("ctx_norm", [P, KT, DIM])
        ctxT = sb("ctxT", [P, DC, CTX])
        lat, latT = sb("lat", [P, XT, DIM]), sb("latT", [P, DC, SEQ])
        v = sb("v", [P, KT, INNER])
        kraw, kswap = sb("kraw", [P, CTX]), sb("kswap", [P, CTX])
        krope = sb("krope", [P, 2, CTX])
        qpad = sb("qpad", [P, 2, 2, SEQ])
        probs = sb("probs", [P, PROB_SLOTS, 2 * SEQ])
        psums = sb("prob_sums", [P, 2, 2 * SEQ])
        ones = sb("ones", [P, DHEAD])
        recip = sb("recip", [P, SEQ])
        oT = sb("oT", [P, PAIRS, SEQ])
        cst = sb("ctx_stats_sb", [P, KT, 6])
        cmv = sb("ctx_meanvar", [P, KT, 2])
        crs = sb("ctx_rstd_sb", [P, KT])
        xst = sb("x_stats_sb", [P, XT, 6])
        xmv = sb("x_meanvar", [P, XT, 2])
        xrs = sb("x_rstd_sb", [P, XT])

        ps_s = [ctx.enter_context(nc.psum_tensor(f"ps_scores{i}", [P, 2 * SEQ], F32)) for i in range(SCORE_SLOTS)]
        ps_av = [ctx.enter_context(nc.psum_tensor(f"ps_av{i}", [P, SEQ], F32)) for i in range(2)]
        ps_m = [ctx.enter_context(nc.psum_tensor(f"ps_misc{i}", [P, HALF], F32)) for i in range(2)]

        loaded = sem("weights_loaded")
        gates_in = sem("gates_in")
        zeroed = sem("pool_constants")
        ident_ready = sem("ident_ready")
        gates_ready = sem("gates_ready")
        tables_ready = sem("tables_ready")
        ctx_loaded, x_loaded = sem("ctx_loaded"), sem("x_loaded")
        ctx_stats, ctx_eps, ctx_rstd = sem("ctx_stats"), sem("ctx_eps"), sem("ctx_rstd")
        ctx_normed = sem("ctx_normed")
        x_sums, x_eps, x_rstd = sem("x_stats"), sem("x_eps"), sem("x_rstd")
        x_normed = sem("x_normed")
        x_biased = sem("x_biased")
        prep_seq = sem("prep_seq")
        misc_ready = sem("misc_ready")
        misc_evicted = [sem("misc_evicted0"), sem("misc_evicted1")]
        kswap_ready = sem("kswap_ready")
        rope_seq = sem("rope_seq")
        krope_ready = sem("krope_ready")
        scores_ready = sem("scores_ready")
        clipped = sem("scores_clipped")
        exp_done = sem("exp_done")
        added = sem("probs_added")
        probs_used = sem("probs_used")
        recip_ready = sem("recip_ready")
        passed = sem("waits_passed")

        block = ctx.enter_context(nc.Block())
        N_LOADS = 10
        MB = NM // 2

        def stop_until(eng, s, value):
            eng.wait_ge(s, value)
            eng.sem_inc(passed, 1)

        def wait_evicted(eng, b, name):
            n = MISC[name]
            eng.wait_ge(misc_evicted[n % 2], b * MB + n // 2 + 2)

        @block.sync
        def _(sp):
            sp.dma_start(wkv[:], d["wkv"].rearrange("(c p) n -> p c n", p=P)).then_inc(loaded, 16)
            sp.dma_start(wq[:], d["wq"].rearrange("(c p) n -> p c n", p=P)).then_inc(loaded, 16)
            sp.dma_start(cosT[:], d["cosT"]).then_inc(loaded, 16)
            sp.dma_start(sinT[:], d["sinT"]).then_inc(loaded, 16)
            for n, name in enumerate(("lat_g", "lat_b", "ctx_g", "ctx_b")):
                sp.dma_start(affine[:, n, :], d[name]).then_inc(loaded, 16)
            sp.dma_start(wo[:], d["wo"].rearrange("(t p) n -> p t n", p=P)).then_inc(loaded, 16)
            sp.dma_start(bo[:], d["bo"].to_broadcast([P, DIM])).then_inc(loaded, 16)
            with sp.Fori(0, BATCH) as b:
                for t in range(PAIRS):
                    for h in range(2):
                        wait_evicted(sp, b, ("k", t, h))
                        sp.sem_inc(passed, 1)
                    for q in range(4):
                        sp.dma_start(kswap[32 * q:32 * q + 32, :],
                                     kraw[32 * (q ^ 1):32 * (q ^ 1) + 32, :]).then_inc(kswap_ready, 16)

        @block.gpsimd
        def _(pool):
            nc.gpsimd.memset(ident[:], 0.0).then_inc(zeroed, 1)
            nc.gpsimd.memset(eps[:], EPS).then_inc(zeroed, 1)
            nc.gpsimd.memset(mhalf[:], -0.5).then_inc(zeroed, 1)
            pool.wait_ge(zeroed, 3)
            nc.gpsimd.affine_select(out=ident[:], in_=ident[:], compare_op=ALU.not_equal, fill=1.0, base=0,
                                    pattern=[[-1, P]], channel_multiplier=1).then_inc(ident_ready, 1)

            def load(b):
                nc.gpsimd.dma_start(ctx_in[:], d["ctx"][b]).then_inc(ctx_loaded, 16)
                nc.gpsimd.dma_start(x_res[:, b], d["x"][b]).then_inc(x_loaded, 16)

            def prepare(b):
                pool.wait_ge(ctx_stats, b + 1)
                nc.gpsimd.tensor_tensor(crs[:], cmv[:, :, 1], eps[:, 0:KT], ALU.add).then_inc(ctx_eps, 1)
                pool.wait_ge(ctx_eps, b + 1)
                nc.gpsimd.tensor_tensor(crs[:], crs[:], mhalf[:, 0:KT], ALU.pow).then_inc(ctx_rstd, 1)
                for n in range(2):
                    pool.wait_ge(x_sums, 2 * b + n + 1)
                    nc.gpsimd.tensor_tensor(xrs[:], xmv[:, :, 1], eps[:, 0:XT], ALU.add).then_inc(x_eps, 1)
                    pool.wait_ge(x_eps, 2 * b + n + 1)
                    nc.gpsimd.tensor_tensor(xrs[:], xrs[:], mhalf[:, 0:XT], ALU.pow).then_inc(x_rstd, 1)
                pool.wait_ge(x_normed, 2 * b + 1)
                for j in range(XT):
                    ins = nc.gpsimd.tensor_tensor(x_res[:, b, j, :], x_res[:, b, j, :], bo[:], ALU.add)
                ins.then_inc(x_biased, 1)

            load(0)
            pool.wait_ge(tables_ready, 1)
            with pool.Fori(0, BATCH - 1) as b:
                prepare(b)
                pool.wait_ge(ctx_normed, b + 1)
                load(b + 1)
            prepare(BATCH - 1)

        @block.scalar
        def _(act):
            nc.scalar.dma_start(gate[:], d["gates"].to_broadcast([P, 4])).then_inc(gates_in, 16)
            act.wait_ge(gates_in, 16)
            nc.scalar.activation(gate[:], gate[:], ACT.Tanh).then_inc(gates_ready, 1)
            act.wait_ge(loaded, 16 * N_LOADS)
            act.wait_ge(tables_ready, 1)

            def evict(b, name):
                n = MISC[name]
                act.wait_ge(misc_ready, b * NM + n + 1)
                src, kind = ps_m[n % 2], name[0]
                if kind == "ctxT":
                    _, c, h = name
                    ins = nc.scalar.activation(ctxT[:, c, h * HALF:(h + 1) * HALF], src[:], ACT.Identity,
                                               scale=affine[:, 2, c:c + 1], bias=affine[:, 3, c:c + 1])
                elif kind == "latT":
                    c = name[1]
                    ins = nc.scalar.activation(latT[:, c, :], src[:], ACT.Identity,
                                               scale=affine[:, 0, c:c + 1], bias=affine[:, 1, c:c + 1])
                elif kind == "v":
                    _, kt, h = name
                    ins = nc.scalar.copy(v[:, kt, h * HALF:(h + 1) * HALF], src[:])
                elif kind == "k":
                    ins = nc.scalar.copy(kraw[:, name[2] * HALF:(name[2] + 1) * HALF], src[:])
                else:
                    t = name[1]
                    nc.scalar.copy(qpad[0:DHEAD, t % 2, 0, :], src[0:DHEAD, :])
                    ins = nc.scalar.copy(qpad[DHEAD:P, t % 2, 1, :], src[DHEAD:P, :])
                ins.then_inc(misc_evicted[n % 2], 1)

            def batch(b):
                for name in MISC:
                    if name == ("k", 1, 0):
                        break
                    evict(b, name)
                for i in range(UNITS):
                    act.wait_ge(clipped, b * UNITS + i + 1)
                    p = probs[:, i % PROB_SLOTS, :]
                    nc.scalar.activation(p, p, ACT.Exp, scale=SCALE).then_inc(exp_done, 1)
                    for name in rope_attention_extras(i):
                        if name[0] != "den":
                            evict(b, name)

            with act.Fori(0, BATCH) as b:
                batch(b)

        @block.vector
        def _(dve):
            nc.vector.memset(qpad[:], 0.0)
            nc.vector.memset(ones[:], 1.0)
            dve.wait_ge(loaded, 16 * N_LOADS)
            for q in (0, 2):
                nc.vector.tensor_scalar(sinT[32 * q:32 * q + 32, :], sinT[32 * q:32 * q + 32, :], -1.0, None,
                                        ALU.mult)
            dve.wait_ge(gates_ready, 1)
            nc.vector.tensor_scalar(bo[:], bo[:], gate[:, 0:1], None, ALU.mult).then_inc(tables_ready, 1)
            for s in misc_evicted:
                dve.sem_inc(s, 1)

            def ctx_tile_stats(b, kt):
                if kt == 0:
                    dve.wait_ge(ctx_loaded, 16 * b + 16)
                nc.vector.bn_stats(cst[:, kt, :], ctx_in[:, kt, :]).then_inc(prep_seq, 1)
                if kt == KT - 1:
                    stop_until(dve, prep_seq, b * PREP + KT)
                    for k in range(KT):
                        ins = nc.vector.bn_aggr(cmv[:, k, :], cst[:, k, :])
                    ins.then_inc(ctx_stats, 1)

            def ctx_tile_norm(b, kt):
                if kt == 0:
                    dve.wait_ge(ctx_rstd, b + 1)
                ins = nc.vector.tensor_scalar(ctx_norm[:, kt, :], ctx_in[:, kt, :], cmv[:, kt, 0:1],
                                              crs[:, kt:kt + 1], ALU.subtract, ALU.mult)
                if kt == KT - 1:
                    ins.then_inc(ctx_normed, 1)

            def x_stats(b, n):
                if n == 0:
                    dve.wait_ge(x_loaded, 16 * b + 16)
                for j in range(XT):
                    src = lat[:, j, :] if n else x_res[:, b, j, :]
                    nc.vector.bn_stats(xst[:, j, :], src).then_inc(prep_seq, 1)
                stop_until(dve, prep_seq, b * PREP + KT + (n + 1) * XT)
                for j in range(XT):
                    ins = nc.vector.bn_aggr(xmv[:, j, :], xst[:, j, :])
                ins.then_inc(x_sums, 1)

            def x_norm(b, n):
                dve.wait_ge(x_rstd, 2 * b + n + 1)
                for j in range(XT):
                    src = lat[:, j, :] if n else x_res[:, b, j, :]
                    ins = nc.vector.tensor_scalar(lat[:, j, :], src, xmv[:, j, 0:1], xrs[:, j:j + 1],
                                                  ALU.subtract, ALU.mult)
                ins.then_inc(x_normed, 1)

            PREP = KT + 2 * XT

            def prepare_slot(b, i):
                t, kt = divmod(i, KT)
                if t == 1:
                    ctx_tile_stats(b, kt)
                elif t == 2:
                    ctx_tile_norm(b, kt)
                elif (t, kt) == (3, 0):
                    x_stats(b, 0)
                elif (t, kt) == (3, 6):
                    x_norm(b, 0)
                elif (t, kt) == (4, 0):
                    dve.wait_ge(x_normed, 2 * b + 1)
                    x_stats(b, 1)
                elif (t, kt) == (4, 6):
                    x_norm(b, 1)

            def rope(b, t):
                for h in range(2):
                    wait_evicted(dve, b, ("k", t, h))
                dve.wait_ge(kswap_ready, 64 * (b * PAIRS + t + 1))
                if t >= 2:
                    dve.wait_ge(scores_ready, b * UNITS + (t - 1) * KT)
                nc.vector.tensor_tensor(krope[:, t % 2, :], kraw[:], cosT[:], ALU.mult).then_inc(rope_seq, 1)
                nc.vector.tensor_tensor(kswap[:], kswap[:], sinT[:], ALU.mult).then_inc(rope_seq, 1)
                dve.wait_ge(rope_seq, 2 * (b * PAIRS + t + 1))
                nc.vector.tensor_tensor(krope[:, t % 2, :], krope[:, t % 2, :], kswap[:],
                                        ALU.add).then_inc(krope_ready, 1)

            def add(b, i):
                t, kt = divmod(i, KT)
                if kt == 0:
                    return
                s = psums[:, t % 2, :]
                if kt == 1:
                    dve.wait_ge(exp_done, b * UNITS + i + 1)
                    nc.vector.tensor_tensor(s, probs[:, (i - 1) % PROB_SLOTS, :], probs[:, i % PROB_SLOTS, :],
                                            ALU.add).then_inc(added, 2)
                else:
                    dve.wait_ge(exp_done, b * UNITS + i + 1)
                    dve.wait_ge(added, b * UNITS + i)
                    nc.vector.tensor_tensor(s, s, probs[:, i % PROB_SLOTS, :], ALU.add).then_inc(added, 1)

            def normalise(b, t):
                n = MISC[("den", t)]
                dve.wait_ge(misc_ready, b * NM + n + 1)
                nc.vector.reciprocal(recip[:], ps_m[n % 2][:]).then_inc(misc_evicted[n % 2], 1)
                wait_evicted(dve, b, ("den", t))
                dve.wait_ge(probs_used, b * UNITS + (t + 1) * KT)
                nc.vector.tensor_tensor(oT[:, t, :], ps_av[t % 2][:], recip[:], ALU.mult).then_inc(recip_ready, 1)

            def batch(b, last):
                rope(b, 0)
                for i in range(UNITS + ADD_LAG):
                    t, kt = divmod(i, KT)
                    if i < UNITS:
                        dve.wait_ge(scores_ready, b * UNITS + i + 1)
                        if i >= PROB_SLOTS:
                            dve.wait_ge(probs_used, b * UNITS + i - PROB_SLOTS + 1)
                            dve.wait_ge(added, b * UNITS + i - PROB_SLOTS + 1)
                        nc.vector.tensor_scalar(probs[:, i % PROB_SLOTS, :], ps_s[i % SCORE_SLOTS][:],
                                                CLIP / SCALE, -CLIP / SCALE, ALU.min, ALU.max).then_inc(clipped, 1)
                    if i >= ADD_LAG:
                        add(b, i - ADD_LAG)
                    if i < UNITS and kt == 4 and t + 1 < PAIRS:
                        rope(b, t + 1)
                    if i < UNITS and kt == 5 and t >= 1:
                        normalise(b, t - 1)
                    if i < UNITS and not last:
                        prepare_slot(b + 1, i)
                normalise(b, PAIRS - 1)
                dve.wait_ge(x_biased, b + 1)
                for m in range(XT // 2):
                    n = MISC[("o", m)]
                    dve.wait_ge(misc_ready, b * NM + n + 1)
                    x = x_res[:, b, 2 * m:2 * m + 2, :].rearrange("p j n -> p (j n)")
                    nc.vector.scalar_tensor_tensor(x, ps_m[n % 2][:], gate[:, 0:1], x, ALU.mult,
                                                   ALU.add).then_inc(misc_evicted[n % 2], 1)

            for kt in range(KT):
                ctx_tile_stats(0, kt)
            x_stats(0, 0)
            for kt in range(KT):
                ctx_tile_norm(0, kt)
            x_norm(0, 0)
            dve.wait_ge(x_normed, 1)
            x_stats(0, 1)
            x_norm(0, 1)
            with dve.Fori(0, BATCH - 1) as b:
                batch(b, False)
            batch(BATCH - 1, True)

        @block.tensor
        def _(pe):
            pe.wait_ge(loaded, 16 * N_LOADS)
            pe.wait_ge(ident_ready, 1)
            pe.wait_ge(tables_ready, 1)

            def misc(b, name):
                n = MISC[name]
                pe.wait_ge(misc_evicted[n % 2], b * MB + n // 2 + 1)
                return ps_m[n % 2]

            def extra(b, name):
                kind = name[0]
                out = misc(b, name)
                if kind == "ctxT":
                    _, c, h = name
                    for j in range(4):
                        ins = nc.tensor.transpose(out[:, j * P:(j + 1) * P],
                                                  ctx_norm[:, 4 * h + j, c * P:(c + 1) * P], ident[:])
                elif kind == "latT":
                    c = name[1]
                    for j in range(XT):
                        ins = nc.tensor.transpose(out[:, j * P:(j + 1) * P], lat[:, j, c * P:(c + 1) * P], ident[:])
                elif kind == "v":
                    _, kt, h = name
                    for c in range(DC):
                        ins = nc.tensor.matmul(out[:], ctxT[:, c, kt * P:(kt + 1) * P],
                                               wkv[:, c, INNER + h * HALF:INNER + (h + 1) * HALF],
                                               start=c == 0, stop=c == DC - 1)
                elif kind == "k":
                    _, t, h = name
                    for c in range(DC):
                        ins = nc.tensor.matmul(out[:], wkv[:, c, t * P:(t + 1) * P],
                                               ctxT[:, c, h * HALF:(h + 1) * HALF], start=c == 0, stop=c == DC - 1)
                elif kind == "q":
                    t = name[1]
                    for c in range(DC):
                        ins = nc.tensor.matmul(out[:], wq[:, c, t * P:(t + 1) * P], latT[:, c, :],
                                               start=c == 0, stop=c == DC - 1)
                elif kind == "den":
                    t = name[1]
                    pe.wait_ge(added, b * UNITS + (t + 1) * KT)
                    for a in range(2):
                        ins = nc.tensor.matmul(out[DHEAD * a:DHEAD * (a + 1), :], ones[:],
                                               psums[:, t % 2, a * SEQ:(a + 1) * SEQ], start=True, stop=True)
                else:
                    m = name[1]
                    for j in range(2):
                        for t in range(PAIRS):
                            ins = nc.tensor.matmul(out[:, j * DIM:(j + 1) * DIM],
                                                   oT[:, t, (2 * m + j) * P:(2 * m + j + 1) * P], wo[:, t, :],
                                                   start=t == 0, stop=t == PAIRS - 1)
                ins.then_inc(misc_ready, 1)

            def scores(b, i):
                t, kt = divmod(i, KT)
                if kt == 0:
                    pe.wait_ge(krope_ready, b * PAIRS + t + 1)
                    wait_evicted(pe, b, ("q", t))
                if i >= SCORE_SLOTS:
                    pe.wait_ge(clipped, b * UNITS + i - SCORE_SLOTS + 1)
                for a in range(2):
                    ins = nc.tensor.matmul(ps_s[i % SCORE_SLOTS][:, a * SEQ:(a + 1) * SEQ],
                                           krope[:, t % 2, kt * P:(kt + 1) * P], qpad[:, t % 2, a, :],
                                           start=True, stop=True)
                ins.then_inc(scores_ready, 1)

            def values(b, i):
                t, kt = divmod(i, KT)
                pe.wait_ge(exp_done, b * UNITS + i + 1)
                if t % 4 == 0:
                    wait_evicted(pe, b, ("v", kt, t // 4))
                if kt == 0 and t >= 2:
                    pe.wait_ge(recip_ready, b * PAIRS + t - 1)
                for a in range(2):
                    col = (2 * t + a) * DHEAD
                    ins = nc.tensor.matmul(ps_av[t % 2][DHEAD * a:DHEAD * (a + 1), :], v[:, kt, col:col + DHEAD],
                                           probs[:, i % PROB_SLOTS, a * SEQ:(a + 1) * SEQ],
                                           start=kt == 0, stop=kt == KT - 1)
                ins.then_inc(probs_used, 1)

            with pe.Fori(0, BATCH) as b:
                pe.wait_ge(ctx_normed, b + 1)
                for name in MISC:
                    if name == ("k", 1, 0):
                        break
                    if name == ("latT", 0):
                        pe.wait_ge(x_normed, 2 * b + 2)
                    if name == ("v", 0, 0):
                        for c in range(DC):
                            wait_evicted(pe, b, ("latT", c))
                    extra(b, name)
                for i in range(UNITS + AV_LAG):
                    if i < UNITS:
                        scores(b, i)
                        for name in rope_attention_extras(i):
                            extra(b, name)
                    if i >= AV_LAG:
                        values(b, i - AV_LAG)
                extra(b, ("den", PAIRS - 1))
                pe.wait_ge(recip_ready, (b + 1) * PAIRS)
                for m in range(XT // 2):
                    extra(b, ("o", m))



class RowNorm:

    def __init__(self, nc, ctx, sh, name, sem):
        def sb(part, shape):
            return ctx.enter_context(nc.sbuf_tensor(f"{name}_{part}", shape, F32))

        self.nc, self.sh = nc, sh
        self.out = sb("normed", [P, XT, DIM])
        self.sums, self.meanvar, self.rstd = sb("sums", [P, XT, 6]), sb("meanvar", [P, XT, 2]), sb("rstd", [P, XT])
        self.summed = sem(name + "_summed")
        self.stats = sem(name + "_stats")
        self.eps_added, self.rstd_ready = sem(name + "_eps_added"), sem(name + "_rstd_ready")
        self.ready = sem(name + "_ready")
        self.passed = sem(name + "_passed")

    def statistics(self, dve, turn, b):
        for j in range(XT):
            self.nc.vector.bn_stats(self.sums[:, j, :], self.sh.x[:, b, j, :]).then_inc(self.summed, 1)
        dve.wait_ge(self.summed, XT * turn + XT)
        dve.sem_inc(self.passed, 1)
        for j in range(XT):
            ins = self.nc.vector.bn_aggr(self.meanvar[:, j, :], self.sums[:, j, :])
        ins.then_inc(self.stats, 1)

    def power(self, pool, turn):
        pool.wait_ge(self.stats, turn + 1)
        self.nc.gpsimd.tensor_tensor(self.rstd[:], self.meanvar[:, :, 1], self.sh.eps[:, 0:XT],
                                     ALU.add).then_inc(self.eps_added, 1)
        pool.wait_ge(self.eps_added, turn + 1)
        self.nc.gpsimd.tensor_tensor(self.rstd[:], self.rstd[:], self.sh.mhalf[:, 0:XT],
                                     ALU.pow).then_inc(self.rstd_ready, 1)

    def apply(self, dve, turn, b):
        dve.wait_ge(self.rstd_ready, turn + 1)
        for j in range(XT):
            ins = self.nc.vector.tensor_scalar(self.out[:, j, :], self.sh.x[:, b, j, :], self.meanvar[:, j, 0:1],
                                               self.rstd[:, j:j + 1], ALU.subtract, ALU.mult)
        ins.then_inc(self.ready, 1)



KEY_HEADS, D_QUERY, SUBKEYS, D_LATENT, D_HIDDEN = 4, 64, 128, 64, 128
EXPERTS = 4096
TOP = 8
PICKS = KEY_HEADS * TOP
QC = KEY_HEADS * D_QUERY // P
ET = EXPERTS // P


class KeyState:

    def __init__(self, nc, ctx):
        def sb(name, shape):
            return ctx.enter_context(nc.sbuf_tensor(name, shape, F32))

        self.qT = sb("keys_qT", [P, QC, BATCH, SEQ])
        self.proj = sb("keys_proj", [P, BATCH, XT, D_HIDDEN])
        self.scale, self.shift = sb("keys_scale", [P, QC]), sb("keys_shift", [P, QC])


def key_queries(nc, sh, ks, d, sem):
    with ExitStack() as ctx:
        def sb(name, shape):
            return ctx.enter_context(nc.sbuf_tensor("s2_" + name, shape, F32))

        ident = sh.ident
        norm = RowNorm(nc, ctx, sh, "s2_norm", sem)
        wq, wx = sb("wq", [P, DC, QC * P]), sb("wx", [P, DC, D_HIDDEN])
        cols = sb("cols", [P, 3, QC])
        latT, w1 = sb("latentsT", [D_LATENT, EXPERTS]), sb("w1", [D_LATENT, D_HIDDEN])
        hidden = sb("hidden", [P, 2, 4, D_HIDDEN])
        xT = sb("xT", [P, DC, SEQ])
        qsums, qmv = sb("q_sums", [P, QC, BATCH, 6]), sb("q_meanvar", [P, QC, 2])
        qrs = sb("q_rstd", [P, QC])
        ps_t = [ctx.enter_context(nc.psum_tensor(f"s2_ps_t{c}", [P, HALF], F32)) for c in range(DC)]
        ps_q = [ctx.enter_context(nc.psum_tensor(f"s2_ps_q{c}", [P, HALF], F32)) for c in range(QC)]
        ps_x = ctx.enter_context(nc.psum_tensor("s2_ps_x", [P, XT, D_HIDDEN], F32))
        ps_h = [ctx.enter_context(nc.psum_tensor(f"s2_ps_h{c}", [P, 4, D_HIDDEN], F32)) for c in range(2)]

        loaded, hid_ready, hid_done, hid_out = sem("s2_loaded"), sem("hidden_ready"), sem("hidden_done"), \
            [sem("hidden_out0"), sem("hidden_out1")]
        t_ready, t_out = sem("s2_transposed"), sem("s2_xT_out")
        q_ready, q_out = sem("s2_q_ready"), sem("s2_q_out")
        p_ready, p_out = sem("s2_proj_ready"), sem("s2_proj_out")
        q_summed, q_eps, q_rstd, steps = sem("s2_q_summed"), sem("s2_q_eps"), sem("s2_q_rstd"), sem("s2_steps")
        q_stats, passed = sem("s2_q_stats"), sem("s2_passed")
        N_LOADS = 7
        block = ctx.enter_context(nc.Block())

        @block.sync
        def _(sp):
            sp.dma_start(latT[:], d["latentsT"]).then_inc(loaded, 16)
            sp.dma_start(w1[:], d["w1"]).then_inc(loaded, 16)
            sp.dma_start(wq[:], d["keys_wqT"].rearrange("(c p) n -> p c n", p=P)).then_inc(loaded, 16)
            sp.dma_start(wx[:], d["w2xT"].rearrange("(c p) n -> p c n", p=P)).then_inc(loaded, 16)
            for n, name in enumerate(("keys_bq", "keys_gamma", "keys_beta")):
                sp.dma_start(cols[:, n, :], d[name]).then_inc(loaded, 16)
            for n in range(ET // 4):
                sp.wait_ge(hid_done, n + 1)
                sp.dma_start(d["table"][4 * n * P:4 * (n + 1) * P, :].rearrange("(j p) f -> p j f", p=P),
                             hidden[:, n % 2]).then_inc(hid_out[n % 2], 16)
            for s in hid_out:
                sp.wait_ge(s, 16 * ET // 8)

        @block.gpsimd
        def _(pool):
            with pool.Fori(0, BATCH) as b:
                norm.power(pool, b)
            pool.wait_ge(q_stats, 1)
            nc.gpsimd.tensor_tensor(qrs[:], qmv[:, :, 1], sh.eps[:, 0:QC], ALU.add).then_inc(q_eps, 1)
            pool.wait_ge(q_eps, 1)
            nc.gpsimd.tensor_tensor(qrs[:], qrs[:], sh.mhalf[:, 0:QC], ALU.pow).then_inc(q_rstd, 1)

        @block.scalar
        def _(act):
            act.wait_ge(loaded, 16 * N_LOADS)
            for n in range(ET // 4):
                act.wait_ge(hid_ready, n + 1)
                if n >= 2:
                    act.wait_ge(hid_out[n % 2], 16 * (n // 2))
                nc.scalar.activation(hidden[:, n % 2].rearrange("p j f -> p (j f)"),
                                     ps_h[n % 2][:].rearrange("p j f -> p (j f)"), ACT.Gelu).then_inc(hid_done, 1)
            with act.Fori(0, BATCH) as b:
                for c in range(DC):
                    act.wait_ge(t_ready, DC * b + c + 1)
                    nc.scalar.copy(xT[:, c, :], ps_t[c][:]).then_inc(t_out, 1)
                for c in range(QC):
                    act.wait_ge(q_ready, QC * b + c + 1)
                    nc.scalar.activation(ks.qT[:, c, b, :], ps_q[c][:], ACT.Identity,
                                         bias=cols[:, 0, c:c + 1]).then_inc(q_out, 1)
                act.wait_ge(p_ready, b + 1)
                nc.scalar.copy(ks.proj[:, b].rearrange("p j f -> p (j f)"),
                               ps_x[:].rearrange("p j f -> p (j f)")).then_inc(p_out, 1)

        @block.vector
        def _(dve):
            def query_sums(b):
                for c in range(QC):
                    dve.wait_ge(q_out, QC * b + c + 1)
                    nc.vector.bn_stats(qsums[:, c, b, :], ks.qT[:, c, b, :]).then_inc(q_summed, 1)

            norm.statistics(dve, 0, 0)
            norm.apply(dve, 0, 0)
            with dve.Fori(0, BATCH - 1) as b:
                norm.statistics(dve, b + 1, b + 1)
                dve.wait_ge(t_ready, DC * b + DC)
                dve.sem_inc(passed, 1)
                norm.apply(dve, b + 1, b + 1)
                query_sums(b)
            query_sums(BATCH - 1)
            dve.wait_ge(q_summed, QC * BATCH)
            for c in range(QC):
                ins = nc.vector.bn_aggr(qmv[:, c, :], qsums[:, c].rearrange("p b s -> p (b s)"))
            ins.then_inc(q_stats, 1)
            dve.wait_ge(q_rstd, 1)
            dve.wait_ge(loaded, 16 * N_LOADS)
            nc.vector.tensor_tensor(ks.scale[:], qrs[:], cols[:, 1, :], ALU.mult).then_inc(steps, 1)
            dve.wait_ge(steps, 1)
            nc.vector.tensor_tensor(ks.shift[:], qmv[:, :, 0], ks.scale[:], ALU.mult).then_inc(steps, 1)
            dve.wait_ge(steps, 2)
            nc.vector.tensor_tensor(ks.shift[:], cols[:, 2, :], ks.shift[:], ALU.subtract).then_inc(steps, 1)

        @block.tensor
        def _(pe):
            pe.wait_ge(loaded, 16 * N_LOADS)
            for n in range(ET // 4):
                if n >= 2:
                    pe.wait_ge(hid_done, n - 1)
                for j in range(4):
                    ins = nc.tensor.matmul(ps_h[n % 2][:, j, :], latT[:, (4 * n + j) * P:(4 * n + j + 1) * P], w1[:],
                                           start=True, stop=True)
                ins.then_inc(hid_ready, 1)

            def body(b, first):
                pe.wait_ge(norm.ready, b + 1)
                for c in range(DC):
                    if not first and c == 0:
                        pe.wait_ge(t_out, DC * b)
                    for j in range(XT):
                        ins = nc.tensor.transpose(ps_t[c][:, j * P:(j + 1) * P], norm.out[:, j, c * P:(c + 1) * P],
                                                  ident[:])
                    ins.then_inc(t_ready, 1)
                pe.wait_ge(t_out, DC * (b + 1))
                for m in range(QC):
                    if not first and m == 0:
                        pe.wait_ge(q_out, QC * b)
                    for c in range(DC):
                        ins = nc.tensor.matmul(ps_q[m][:], wq[:, c, m * P:(m + 1) * P], xT[:, c, :],
                                               start=c == 0, stop=c == DC - 1)
                    ins.then_inc(q_ready, 1)
                if not first:
                    pe.wait_ge(p_out, b)
                for j in range(XT):
                    for c in range(DC):
                        ins = nc.tensor.matmul(ps_x[:, j, :], xT[:, c, j * P:(j + 1) * P], wx[:, c, :],
                                               start=c == 0, stop=c == DC - 1)
                ins.then_inc(p_ready, 1)

            body(0, True)
            with pe.Fori(1, BATCH) as b:
                body(b, False)



LISTS = 2 * KEY_HEADS


def product_keys(nc, sh, ks, d, sem):
    with ExitStack() as ctx:
        def sb(name, shape, dt=F32):
            return ctx.enter_context(nc.sbuf_tensor("s3_" + name, shape, dt))

        x_res, gate, ident = sh.x, sh.gate, sh.ident
        subkeys = sb("subkeys", [P, 4, SUBKEYS])
        wv = sb("wv", [D_HIDDEN, DIM])
        gate4 = sb("gate4", [P, 1])
        digits = sb("digits", [P, TOP])
        digits_i = sb("digits_i", [P, TOP], mybir.dt.int32)
        qn = sb("qn", [P, QC, SEQ])
        scores = sb("scores", [P, 2, LISTS, SUBKEYS])
        best = sb("best", [P, XT, LISTS, TOP])
        best_at = sb("best_at", [P, XT, LISTS, TOP], U32)
        pair = sb("pair_sums", [P, XT * KEY_HEADS, TOP, TOP])
        top = sb("top", [P, XT * KEY_HEADS, TOP])
        top_at = sb("top_at", [P, XT * KEY_HEADS, TOP], U32)
        digit = sb("digit", [P, XT * KEY_HEADS, 2, TOP], U32)
        pick = sb("pick", [P, XT * LISTS * TOP, TOP])
        part = sb("part", [P, XT * KEY_HEADS, 2, TOP])
        expert = sb("expert", [P, XT * KEY_HEADS, TOP])
        expert_at = sb("expert_at", [P, XT * PICKS], U32)
        prob = sb("prob", [P, XT * KEY_HEADS, TOP])
        psum_ = sb("prob_sum", [P, XT * KEY_HEADS])
        rows = sb("rows", [P, 2, PICKS, D_HIDDEN])
        prod = sb("prod", [P, PICKS, D_HIDDEN])
        dots = sb("dots", [P, 2, PICKS])
        acts = sb("acts", [P, 2, PICKS])
        acc = sb("acc", [P, 2, D_HIDDEN])
        accT = sb("accT", [P, 2, P])

        ps_s = [ctx.enter_context(nc.psum_tensor(f"s3_ps_s{c}", [P, LISTS, SUBKEYS], F32)) for c in range(2)]
        ps_t = [ctx.enter_context(nc.psum_tensor(f"s3_ps_t{c}", [P, P], F32)) for c in range(2)]
        ps_o = [ctx.enter_context(nc.psum_tensor(f"s3_ps_o{c}", [P, DIM], F32)) for c in range(2)]

        loaded, zeroed, ready0 = sem("s3_loaded"), sem("s3_zeroed"), sem("s3_constants")
        qn_ready, s_ready, s_out = sem("s3_qn"), sem("s3_scores"), sem("s3_scores_out")
        listed = sem("s3_listed")
        steps = sem("s3_steps")
        diffs, exps = sem("s3_diffs"), sem("s3_exps")
        experts = sem("s3_experts")
        gathered = [sem("s3_gathered0"), sem("s3_gathered1")]
        dotted, gelued, weighted, used = sem("s3_dotted"), sem("s3_gelued"), sem("s3_weighted"), sem("s3_used")
        passed = sem("s3_waits_passed")

        def stop_until(eng, s, value):
            eng.wait_ge(s, value)
            eng.sem_inc(passed, 1)

        t_ready, t_out, o_ready, o_out = sem("s3_accT"), sem("s3_accT_out"), sem("s3_o_ready"), sem("s3_o_out")
        N_STEPS = 11
        block = ctx.enter_context(nc.Block())

        @block.sync
        def _(sp):
            sp.dma_start(wv[:], d["w2v"]).then_inc(loaded, 16)
            sp.wait_ge(zeroed, 1)
            for h in range(2):
                for half in range(2):
                    n = 2 * h + half
                    sp.dma_start(subkeys[32 * n:32 * n + 32, n, :], d[f"sk{half + 1}T"]).then_inc(loaded, 16)

        @block.gpsimd
        def _(pool):
            nc.gpsimd.iota(digits_i[:], pattern=[[1, TOP]], base=0, channel_multiplier=0).then_inc(ready0, 1)
            pool.wait_ge(ready0, 1)
            nc.gpsimd.tensor_copy(digits[:], digits_i[:]).then_inc(ready0, 1)

            def gather(b, j):
                n = j % 2
                for k in range(PICKS):
                    nc.gpsimd.indirect_dma_start(
                        out=rows[:, n, k, :], out_offset=None, in_=d["table"],
                        in_offset=bass.IndirectOffsetOnAxis(ap=expert_at[:, j * PICKS + k:j * PICKS + k + 1], axis=0),
                    ).then_inc(gathered[n], 16)

            def batch(b, first):
                pool.wait_ge(experts, b + 1)
                for j in range(XT):
                    if j >= 2 or not first:
                        stop_until(pool, used, XT * b + j - 1)
                    gather(b, j)

            batch(0, True)
            with pool.Fori(1, BATCH) as b:
                batch(b, False)

        @block.scalar
        def _(act):
            def queries(b):
                for c in range(QC):
                    nc.scalar.activation(qn[:, c, :], ks.qT[:, c, b, :], ACT.Identity, scale=ks.scale[:, c:c + 1],
                                         bias=ks.shift[:, c:c + 1]).then_inc(qn_ready, 1)

            def score_tiles(b):
                for j in range(XT):
                    act.wait_ge(s_ready, XT * b + j + 1)
                    if j >= 2:
                        act.wait_ge(listed, 2 * (XT * b + j - 1))
                    nc.scalar.copy(scores[:, j % 2].rearrange("p l k -> p (l k)"),
                                   ps_s[j % 2][:].rearrange("p l k -> p (l k)")).then_inc(s_out, 1)

            with act.Fori(0, BATCH) as b:
                queries(b)
                score_tiles(b)
                act.wait_ge(diffs, b + 1)
                nc.scalar.activation(prob[:].rearrange("p h k -> p (h k)"), prob[:].rearrange("p h k -> p (h k)"),
                                     ACT.Exp).then_inc(exps, 1)
                for j in range(XT):
                    act.wait_ge(dotted, XT * b + j + 1)
                    nc.scalar.activation(acts[:, j % 2, :], dots[:, j % 2, :], ACT.Gelu).then_inc(gelued, 1)
                    act.wait_ge(t_ready, XT * b + j + 1)
                    nc.scalar.copy(accT[:, j % 2, :], ps_t[j % 2][:]).then_inc(t_out, 1)

        @block.vector
        def _(dve):
            nc.vector.memset(subkeys[:], 0.0).then_inc(zeroed, 1)
            nc.vector.tensor_scalar(gate4[:], gate[:, 2:3], 1.0 / KEY_HEADS, None, ALU.mult)
            dve.wait_ge(ready0, 2)

            def lists(b):
                for j in range(XT):
                    stop_until(dve, s_out, XT * b + j + 1)
                    for n in range(LISTS):
                        ins = nc.vector.max(best[:, j, n, :], scores[:, j % 2, n, :])
                    ins.then_inc(listed, 1)
                    stop_until(dve, listed, 2 * (XT * b + j) + 1)
                    for n in range(LISTS):
                        ins = nc.vector.max_index(best_at[:, j, n, :], best[:, j, n, :], scores[:, j % 2, n, :])
                    ins.then_inc(listed, 1)

            def choose(b):
                G = XT * KEY_HEADS
                done = [0]

                def step(ins):
                    done[0] += 1
                    ins.then_inc(steps, 1)
                    stop_until(dve, steps, b * N_STEPS + done[0])

                dve.wait_ge(listed, 2 * XT * (b + 1))
                halves = best[:].rearrange("p j (h s) k -> p (j h) s k", s=2)
                step(nc.vector.tensor_tensor(pair[:], halves[:, :, 0, :].unsqueeze(3).to_broadcast([P, G, TOP, TOP]),
                                             halves[:, :, 1, :].unsqueeze(2).to_broadcast([P, G, TOP, TOP]), ALU.add))
                for g in range(G):
                    ins = nc.vector.max(top[:, g, :], pair[:, g].rearrange("p a b -> p (a b)"))
                step(ins)
                for g in range(G):
                    ins = nc.vector.max_index(top_at[:, g, :], top[:, g, :], pair[:, g].rearrange("p a b -> p (a b)"))
                nc.vector.tensor_tensor(prob[:], top[:], top[:, :, 0:1].to_broadcast([P, G, TOP]),
                                        ALU.subtract).then_inc(diffs, 1)
                step(ins)
                nc.vector.tensor_scalar(digit[:, :, 0, :], top_at[:], 3, None, ALU.logical_shift_right)
                step(nc.vector.tensor_scalar(digit[:, :, 1, :], top_at[:], 7, None, ALU.bitwise_and))
                flat = digit[:].rearrange("p g s k -> p (g s k)")
                step(nc.vector.tensor_tensor(pick[:], flat.unsqueeze(2).to_broadcast([P, 2 * G * TOP, TOP]),
                                             digits[:].unsqueeze(1).to_broadcast([P, 2 * G * TOP, TOP]), ALU.is_equal))
                pick4 = pick[:].rearrange("p (l k) a -> p l k a", k=TOP)
                at = best_at[:].rearrange("p j l a -> p (j l) a").unsqueeze(2).to_broadcast([P, 2 * G, TOP, TOP])
                step(nc.vector.tensor_tensor(pick4, pick4, at, ALU.mult))
                step(nc.vector.tensor_reduce(part[:].rearrange("p g s k -> p (g s k)"), pick[:], AX.X, ALU.add))
                step(nc.vector.scalar_tensor_tensor(expert[:], part[:, :, 0, :], float(SUBKEYS), part[:, :, 1, :],
                                                    ALU.mult, ALU.add))
                nc.vector.tensor_scalar(expert_at[:], expert[:].rearrange("p g k -> p (g k)"), float(EXPERTS - 1), None,
                                        ALU.min).then_inc(experts, 1)
                dve.wait_ge(exps, b + 1)
                step(nc.vector.tensor_reduce(psum_[:], prob[:], AX.X, ALU.add))
                step(nc.vector.reciprocal(psum_[:], psum_[:]))
                step(nc.vector.tensor_tensor(prob[:], prob[:], psum_[:].unsqueeze(2).to_broadcast([P, G, TOP]),
                                             ALU.mult))
                assert done[0] == 11

            def combine(b, j):
                n = j % 2
                dve.wait_ge(gathered[n], 16 * PICKS * (XT // 2 * b + j // 2 + 1))
                r = rows[:, n]
                base = (XT * b + j) * 3
                nc.vector.tensor_tensor(prod[:], r, ks.proj[:, b, j, :].unsqueeze(1).to_broadcast([P, PICKS, D_HIDDEN]),
                                        ALU.mult).then_inc(weighted, 1)
                dve.wait_ge(weighted, base + 1)
                nc.vector.tensor_reduce(dots[:, n, :], prod[:], AX.X, ALU.add).then_inc(dotted, 1)
                dve.wait_ge(gelued, XT * b + j + 1)
                nc.vector.tensor_tensor(dots[:, n, :], acts[:, n, :],
                                        prob[:, KEY_HEADS * j:KEY_HEADS * (j + 1), :].rearrange("p h k -> p (h k)"),
                                        ALU.mult).then_inc(weighted, 1)
                dve.wait_ge(weighted, base + 2)
                nc.vector.tensor_tensor(r, r, dots[:, n, :].unsqueeze(2).to_broadcast([P, PICKS, D_HIDDEN]),
                                        ALU.mult).then_inc(weighted, 1)
                dve.wait_ge(weighted, base + 3)
                nc.vector.tensor_reduce(acc[:, n, :], r.rearrange("p k f -> p f k"), AX.X, ALU.add).then_inc(used, 1)
                dve.wait_ge(o_ready, XT * b + j + 1)
                x = x_res[:, b, j, :]
                nc.vector.scalar_tensor_tensor(x, ps_o[n][:], gate4[:], x, ALU.mult, ALU.add).then_inc(o_out, 1)

            with dve.Fori(0, BATCH) as b:
                lists(b)
                choose(b)
                for j in range(XT):
                    combine(b, j)

        @block.tensor
        def _(pe):
            pe.wait_ge(loaded, 16 * 5)
            with pe.Fori(0, BATCH) as b:
                pe.wait_ge(qn_ready, QC * (b + 1))
                for j in range(XT):
                    if j >= 2:
                        pe.wait_ge(s_out, XT * b + j - 1)
                    for c in range(QC):
                        ins = nc.tensor.matmul(ps_s[j % 2][:, 4 * c:4 * c + 4, :], qn[:, c, j * P:(j + 1) * P],
                                               subkeys[:], start=True, stop=True)
                    ins.then_inc(s_ready, 1)
                for j in range(XT):
                    pe.wait_ge(used, XT * b + j + 1)
                    nc.tensor.transpose(ps_t[j % 2][:], acc[:, j % 2, :], ident[:]).then_inc(t_ready, 1)
                    pe.wait_ge(t_out, XT * b + j + 1)
                    nc.tensor.matmul(ps_o[j % 2][:], accT[:, j % 2, :], wv[:], start=True,
                                     stop=True).then_inc(o_ready, 1)



MOE, FF = 8, 512
FT = FF // P
BLOCKS = (MOE + 1) * FT
LOGIT_SLOTS = 4


def layer1(nc, sh, d, sem):
    with ExitStack() as ctx:
        def sb(name, shape, dt=F32):
            return ctx.enter_context(nc.sbuf_tensor("s4_" + name, shape, dt))

        x_res, gate, ident = sh.x, sh.gate, sh.ident
        norm = RowNorm(nc, ctx, sh, "s4_norm", sem)
        wq, wk, wv = sb("wq", [P, DC, DIM]), sb("wk", [P, DC, DIM]), sb("wv", [P, DC, DIM])
        bq, bk, bv = sb("bq", [P, DC]), sb("bk", [P, DC]), sb("bv", [P, 2, DIM])
        maskT = sb("maskT", [P, KT, SEQ])
        ctxT = sb("ctxT", [P, DC, CTX])
        kp, vp, qp = sb("kp", [P, DC, CTX]), sb("vp", [P, KT, DIM]), sb("qp", [P, DC, SEQ])
        logits = sb("logits", [P, LOGIT_SLOTS, SEQ])
        xT = sb("xT", [P, DC, SEQ])
        attn = sb("attn", [P, XT, DIM])
        router = sb("router", [P, DC, MOE])
        w_in = sb("w_in", [P, 3, DC, FF])
        w_sw = sb("w_sw", [P, 3, DC, FF])
        w_out = sb("w_out", [P, 3, FT, DIM])
        digits_i, digits = sb("digits_i", [P, MOE], mybir.dt.int32), sb("digits", [P, MOE])
        rs, rs_top = sb("router_scores", [P, XT, MOE]), sb("router_top", [P, XT, TOP])
        rs_at = sb("router_at", [P, XT, TOP], U32)
        second, gates = sb("second", [P, XT, MOE]), sb("gates", [P, XT, MOE])
        sig = sb("sigmoids", [P, XT, MOE])
        gatesT = sb("gatesT", [MOE, SEQ])
        gates_all = sb("gates_all", [P, 2, SEQ])
        xg = sb("xg", [P, 2, DC, SEQ])
        act_in, hid = sb("act_in", [P, 2, SEQ]), sb("hid", [P, 2, SEQ])

        ps_m = [ctx.enter_context(nc.psum_tensor(f"s4_ps_m{c}", [P, HALF], F32)) for c in range(2)]
        ps_o = ctx.enter_context(nc.psum_tensor("s4_ps_o", [P, XT, DIM], F32))
        ps_a = [ctx.enter_context(nc.psum_tensor(f"s4_ps_a{c}", [P, HALF], F32)) for c in range(2)]
        ps_b = [ctx.enter_context(nc.psum_tensor(f"s4_ps_b{c}", [P, HALF], F32)) for c in range(2)]

        loaded, consts, bias_scaled = sem("s4_loaded"), sem("s4_consts"), sem("s4_bias_scaled")
        ctx_loaded = sem("s4_ctx_loaded")
        expert_in = [sem("s4_expert_in0"), sem("s4_expert_in1")]
        m_ready, m_out = sem("s4_misc"), [sem("s4_misc_out0"), sem("s4_misc_out1")]
        relued = sem("s4_v_relued")
        s_ready, s_out = sem("s4_scores"), sem("s4_logits")
        av_ready = sem("s4_av")
        attn_out, x_done = sem("s4_attn_out"), sem("s4_x_attended")
        steps, listed, sig_ready = sem("s4_steps"), sem("s4_listed"), sem("s4_sigmoids")
        gates_ready = sem("s4_gates")
        gates_stored, gates_in = sem("s4_gates_stored"), [sem("s4_gates_in0"), sem("s4_gates_in1")]
        xg_ready = sem("s4_gated")
        a_ready, a_out = sem("s4_first"), sem("s4_silu")
        h_ready = sem("s4_hidden")
        h_used = sem("s4_hidden_used")
        moe_out, stored = sem("s4_moe_out"), sem("s4_stored")
        passed = sem("s4_waits_passed")
        N_LOADS = 11

        ORDER = [("xT", 0, c) for c in range(DC)] + [("k", m, h) for m in range(DC) for h in range(2)]
        ORDER += [("q", c) for c in range(DC)] + [("v", n) for n in range(KT // 2)]
        ORDER += [("xT", 1, c) for c in range(DC)] + [("router",), ("gatesT",)]
        NM, MB = len(ORDER), len(ORDER) // 2
        MISC = {name: n for n, name in enumerate(ORDER)}
        assert NM % 2 == 0
        block = ctx.enter_context(nc.Block())

        def stop_until(eng, s, value):
            eng.wait_ge(s, value)
            eng.sem_inc(passed, 1)

        def wait_out(eng, b, name):
            n = MISC[name]
            eng.wait_ge(m_out[n % 2], b * MB + n // 2 + 2)

        def wait_made(eng, b, name):
            eng.wait_ge(m_ready, b * NM + MISC[name] + 1)

        @block.sync
        def _(sp):
            for t, name in ((wk, "l1_wk"), (wq, "l1_wq"), (wv, "l1_wv"), (router, "router")):
                sp.dma_start(t[:], d[name].rearrange("(c p) n -> p c n", p=P)).then_inc(loaded, 16)
            sp.dma_start(bq[:], d["l1_bq"]).then_inc(loaded, 16)
            sp.dma_start(bk[:], d["l1_bk"]).then_inc(loaded, 16)
            sp.dma_start(bv[:], d["l1_bv"].unsqueeze(1).to_broadcast([P, 2, DIM])).then_inc(loaded, 16)
            sp.dma_start(w_in[:, 2], d["w_in_shared"].rearrange("(c p) n -> p c n", p=P)).then_inc(loaded, 16)
            sp.dma_start(w_sw[:, 2], d["w_sw_shared"].rearrange("(c p) n -> p c n", p=P)).then_inc(loaded, 16)
            sp.dma_start(w_out[:, 2], d["w_out_shared"].rearrange("(f p) n -> p f n", p=P)).then_inc(loaded, 16)
            sp.dma_start(maskT[:], d["maskT"].rearrange("(t p) q -> p t q", p=P)).then_inc(loaded, 16)

            def expert(b, e, first):
                if not first:
                    stop_until(sp, h_used, b * BLOCKS + (e if e >= 2 else e - 1) * FT)
                s = e % 2
                sp.dma_start(w_in[:, s], d["w_in"][e].rearrange("(c p) n -> p c n", p=P)).then_inc(expert_in[s], 16)
                sp.dma_start(w_sw[:, s], d["w_sw"][e].rearrange("(c p) n -> p c n", p=P)).then_inc(expert_in[s], 16)
                sp.dma_start(w_out[:, s], d["w_out"][e].rearrange("(f p) n -> p f n", p=P)).then_inc(expert_in[s], 16)

            def batch(b, first):
                if not first:
                    stop_until(sp, m_ready, (b - 1) * NM + MISC[("v", KT // 2 - 1)] + 1)
                sp.dma_start(ctxT[:], d["ctxT"][b]).then_inc(ctx_loaded, 16)
                for e in range(2):
                    expert(b, e, first)
                if not first:
                    stop_until(sp, moe_out, b)
                    sp.dma_start(d["out"][b - 1], x_res[:, b - 1]).then_inc(stored, 16)
                wait_out(sp, b, ("gatesT",))
                sp.sem_inc(passed, 1)
                sp.dma_start(d["gates_dram"], gatesT[:]).then_inc(gates_stored, 16)
                stop_until(sp, gates_stored, 16 * (b + 1))
                for e in range(MOE):
                    if e >= 2:
                        stop_until(sp, xg_ready, MOE * b + e - 1)
                    sp.dma_start(gates_all[:, e % 2, :],
                                 d["gates_dram"][e:e + 1, :].to_broadcast([P, SEQ])).then_inc(gates_in[e % 2], 16)
                    if e >= 2:
                        expert(b, e, False)

            batch(0, True)
            with sp.Fori(1, BATCH) as b:
                batch(b, False)
            sp.wait_ge(moe_out, BATCH)
            sp.dma_start(d["out"][BATCH - 1], x_res[:, BATCH - 1]).then_inc(stored, 16)
            sp.wait_ge(stored, 16 * BATCH)

        @block.gpsimd
        def _(pool):
            nc.gpsimd.iota(digits_i[:], pattern=[[1, MOE]], base=0, channel_multiplier=0).then_inc(consts, 1)
            pool.wait_ge(consts, 1)
            nc.gpsimd.tensor_copy(digits[:], digits_i[:]).then_inc(consts, 1)
            with pool.Fori(0, BATCH) as b:
                for n in range(2):
                    norm.power(pool, 2 * b + n)

        @block.scalar
        def _(act):
            act.wait_ge(loaded, 16 * N_LOADS)
            nc.scalar.mul(bq[:], bq[:], 1.0 / 16.0).then_inc(bias_scaled, 1)
            act.wait_ge(bias_scaled, 1)
            for s in m_out:
                act.sem_inc(s, 1)

            def take(b, name):
                wait_made(act, b, name)
                n = MISC[name]
                src = ps_m[n % 2]
                if name[0] == "xT":
                    ins = nc.scalar.copy(xT[:, name[2], :], src[:])
                elif name[0] == "k":
                    _, m, h = name
                    ins = nc.scalar.activation(kp[:, m, h * HALF:(h + 1) * HALF], src[:], ACT.Relu, bias=bk[:, m:m + 1])
                elif name[0] == "q":
                    ins = nc.scalar.activation(qp[:, name[1], :], src[:], ACT.Relu, bias=bq[:, name[1]:name[1] + 1],
                                               scale=1.0 / 16.0)
                else:
                    ins = nc.scalar.copy(gatesT[:], src[0:MOE, :])
                ins.then_inc(m_out[n % 2], 1)

            with act.Fori(0, BATCH) as b:
                for name in ORDER:
                    if name[0] in ("k", "q") or name[:2] == ("xT", 0):
                        take(b, name)
                for n in range(KT // 2):
                    wait_out(act, b, ("v", n))
                    v = vp[:, 2 * n:2 * n + 2, :].rearrange("p t n -> p (t n)")
                    nc.scalar.activation(v, v, ACT.Relu).then_inc(relued, 1)
                act.wait_ge(av_ready, KT * (b + 1))
                nc.scalar.activation(attn[:].rearrange("p j n -> p (j n)"), ps_o[:].rearrange("p j n -> p (j n)"),
                                     ACT.Relu).then_inc(attn_out, 1)
                for c in range(DC):
                    take(b, ("xT", 1, c))
                wait_out(act, b, ("router",))
                nc.scalar.activation(sig[:], rs[:], ACT.Sigmoid).then_inc(sig_ready, 1)
                for n in range(BLOCKS):
                    if n == FT:
                        take(b, ("gatesT",))
                    act.wait_ge(a_ready, b * BLOCKS + n + 1)
                    if n >= 2:
                        act.wait_ge(h_ready, b * BLOCKS + n - 1)
                    nc.scalar.activation(act_in[:, n % 2, :], ps_a[n % 2][:], ACT.Silu).then_inc(a_out, 1)

        @block.vector
        def _(dve):
            dve.wait_ge(loaded, 16 * N_LOADS)
            dve.wait_ge(consts, 2)
            N_STEPS = 4

            def route(b):
                done = [0]

                def step(ins):
                    done[0] += 1
                    ins.then_inc(steps, 1)
                    stop_until(dve, steps, b * N_STEPS + done[0])

                name = ("router",)
                wait_made(dve, b, name)
                n = MISC[name]
                nc.vector.tensor_copy(rs[:].rearrange("p j e -> p (j e)"), ps_m[n % 2][:, 0:XT * MOE])\
                    .then_inc(m_out[n % 2], 1)
                stop_until(dve, m_out[n % 2], b * MB + n // 2 + 2)
                for j in range(XT):
                    ins = nc.vector.max(rs_top[:, j, :], rs[:, j, :])
                step(ins)
                for j in range(XT):
                    ins = nc.vector.max_index(rs_at[:, j, :], rs_top[:, j, :], rs[:, j, :])
                step(ins)
                every = digits[:].unsqueeze(1).to_broadcast([P, XT, MOE])
                nc.vector.tensor_tensor(gates[:], every, rs_at[:, :, 0:1].to_broadcast([P, XT, MOE]), ALU.is_equal)
                step(nc.vector.tensor_tensor(second[:], every, rs_at[:, :, 1:2].to_broadcast([P, XT, MOE]),
                                             ALU.is_equal))
                step(nc.vector.tensor_tensor(gates[:], gates[:], second[:], ALU.add))
                dve.wait_ge(sig_ready, b + 1)
                nc.vector.tensor_tensor(gates[:], gates[:], sig[:], ALU.mult).then_inc(gates_ready, 1)

            def gated(b, e):
                dve.wait_ge(gates_in[e % 2], 16 * (MOE // 2 * b + e // 2 + 1))
                nc.vector.tensor_tensor(xg[:, e % 2], xT[:], gates_all[:, e % 2, :].unsqueeze(1)
                                        .to_broadcast([P, DC, SEQ]), ALU.mult).then_inc(xg_ready, 1)

            with dve.Fori(0, BATCH) as b:
                norm.statistics(dve, 2 * b, b)
                norm.apply(dve, 2 * b, b)
                for n in range(KT // 2):
                    name = ("v", n)
                    wait_made(dve, b, name)
                    k = MISC[name]
                    nc.vector.tensor_tensor(vp[:, 2 * n:2 * n + 2, :].rearrange("p t n -> p (t n)"), ps_m[k % 2][:],
                                            bv[:].rearrange("p t n -> p (t n)"), ALU.add).then_inc(m_out[k % 2], 1)
                for kt in range(KT):
                    dve.wait_ge(s_ready, KT * b + kt + 1)
                    if kt >= LOGIT_SLOTS:
                        dve.wait_ge(av_ready, KT * b + kt - LOGIT_SLOTS + 1)
                    nc.vector.scalar_tensor_tensor(logits[:, kt % LOGIT_SLOTS, :], ps_a[kt % 2][:], 0.0,
                                                   maskT[:, kt, :], ALU.max, ALU.add).then_inc(s_out, 1)
                dve.wait_ge(attn_out, b + 1)
                x = x_res[:, b].rearrange("p j n -> p (j n)")
                nc.vector.scalar_tensor_tensor(x, attn[:].rearrange("p j n -> p (j n)"), gate[:, 1:2], x, ALU.mult,
                                               ALU.add).then_inc(x_done, 1)
                stop_until(dve, x_done, b + 1)
                norm.statistics(dve, 2 * b + 1, b)
                norm.apply(dve, 2 * b + 1, b)
                route(b)
                for n in range(BLOCKS):
                    e, f = divmod(n, FT)
                    if f == 2 and e < MOE:
                        gated(b, e)
                    dve.wait_ge(a_out, b * BLOCKS + n + 1)
                    if n >= 2:
                        dve.wait_ge(h_used, b * BLOCKS + n - 1)
                    nc.vector.tensor_tensor(hid[:, n % 2, :], act_in[:, n % 2, :], ps_b[n % 2][:],
                                            ALU.mult).then_inc(h_ready, 1)
                dve.wait_ge(h_used, (b + 1) * BLOCKS)
                nc.vector.scalar_tensor_tensor(x, ps_o[:].rearrange("p j n -> p (j n)"), gate[:, 3:4], x, ALU.mult,
                                               ALU.add).then_inc(moe_out, 1)

        @block.tensor
        def _(pe):
            pe.wait_ge(loaded, 16 * N_LOADS)

            def make(b, name):
                n = MISC[name]
                pe.wait_ge(m_out[n % 2], b * MB + n // 2 + 1)
                o = ps_m[n % 2]
                if name[0] == "xT":
                    for j in range(XT):
                        ins = nc.tensor.transpose(o[:, j * P:(j + 1) * P], norm.out[:, j, name[2] * P:(name[2] + 1) * P],
                                                  ident[:])
                elif name[0] == "k":
                    _, m, h = name
                    for c in range(DC):
                        ins = nc.tensor.matmul(o[:], wk[:, c, m * P:(m + 1) * P], ctxT[:, c, h * HALF:(h + 1) * HALF],
                                               start=c == 0, stop=c == DC - 1)
                elif name[0] == "q":
                    m = name[1]
                    for c in range(DC):
                        ins = nc.tensor.matmul(o[:], wq[:, c, m * P:(m + 1) * P], xT[:, c, :], start=c == 0,
                                               stop=c == DC - 1)
                elif name[0] == "v":
                    for t in range(2):
                        kt = 2 * name[1] + t
                        for c in range(DC):
                            ins = nc.tensor.matmul(o[:, t * DIM:(t + 1) * DIM], ctxT[:, c, kt * P:(kt + 1) * P],
                                                   wv[:, c, :], start=c == 0, stop=c == DC - 1)
                elif name[0] == "router":
                    for j in range(XT):
                        for c in range(DC):
                            ins = nc.tensor.matmul(o[:, j * MOE:(j + 1) * MOE], xT[:, c, j * P:(j + 1) * P],
                                                   router[:, c, :], start=c == 0, stop=c == DC - 1)
                else:
                    pe.wait_ge(gates_ready, b + 1)
                    for j in range(XT):
                        ins = nc.tensor.transpose(o[0:MOE, j * P:(j + 1) * P], gates[:, j, :], ident[:])
                ins.then_inc(m_ready, 1)

            def summed(o, lhsT, rhs, n, last):
                for j in range(XT):
                    ins = nc.tensor.matmul(o[:, j, :], lhsT(j), rhs, start=n == 0 and j % 2 == 0, stop=n == last,
                                           skip_group_check=True)
                return ins

            def expert_products(b, n):
                e, f = divmod(n, FT)
                slot = 2 if e == 0 else (e - 1) % 2
                if f == 0 and e >= 1:
                    pe.wait_ge(expert_in[slot], 48 * (MOE // 2 * b + (e - 1) // 2 + 1))
                    pe.wait_ge(xg_ready, MOE * b + e)
                if n >= 2:
                    pe.wait_ge(h_ready, b * BLOCKS + n - 1)
                src = xT[:] if e == 0 else xg[:, slot]
                for w, o in ((w_in, ps_a[n % 2]), (w_sw, ps_b[n % 2])):
                    for c in range(DC):
                        ins = nc.tensor.matmul(o[:], w[:, slot, c, f * P:(f + 1) * P], src[:, c, :], start=c == 0,
                                               stop=c == DC - 1)
                ins.then_inc(a_ready, 1)

            def expert_sums(b, n):
                e, f = divmod(n, FT)
                slot = 2 if e == 0 else (e - 1) % 2
                pe.wait_ge(h_ready, b * BLOCKS + n + 1)
                summed(ps_o, lambda j: hid[:, n % 2, j * P:(j + 1) * P], w_out[:, slot, f, :], n,
                       BLOCKS - 1).then_inc(h_used, 1)

            with pe.Fori(0, BATCH) as b:
                pe.wait_ge(norm.ready, 2 * b + 1)
                for name in ORDER[:MISC[("xT", 1, 0)]]:
                    if name == ("k", 0, 0):
                        pe.wait_ge(ctx_loaded, 16 * (b + 1))
                    if name == ("q", 0):
                        for h in range(2):
                            wait_out(pe, b, ("k", DC - 1, h))
                    make(b, name)
                for kt in range(KT + 1):
                    if kt < KT:
                        if kt >= 2:
                            pe.wait_ge(s_out, KT * b + kt - 1)
                        for c in range(DC):
                            ins = nc.tensor.matmul(ps_a[kt % 2][:], kp[:, c, kt * P:(kt + 1) * P], qp[:, c, :],
                                                   start=c == 0, stop=c == DC - 1)
                        ins.then_inc(s_ready, 1)
                    if kt >= 1:
                        k = kt - 1
                        pe.wait_ge(relued, KT // 2 * b + k // 2 + 1)
                        pe.wait_ge(s_out, KT * b + k + 1)
                        summed(ps_o, lambda j: logits[:, k % LOGIT_SLOTS, j * P:(j + 1) * P], vp[:, k, :], k,
                               KT - 1).then_inc(av_ready, 1)
                pe.wait_ge(norm.ready, 2 * b + 2)
                for c in range(DC):
                    make(b, ("xT", 1, c))
                for c in range(DC):
                    wait_out(pe, b, ("xT", 1, c))
                make(b, ("router",))
                for n in range(BLOCKS + 1):
                    if n < BLOCKS:
                        if n == FT - 1:
                            make(b, ("gatesT",))
                        expert_products(b, n)
                    if n >= 1:
                        expert_sums(b, n - 1)


def program(nc, d):
    with ExitStack() as ctx:
        def sem(name):
            return ctx.enter_context(nc.semaphore(name))

        d["table"] = nc.dram_tensor("hidden_table", [EXPERTS, D_HIDDEN], F32).ap()
        d["gates_dram"] = nc.dram_tensor("gates_by_expert", [MOE, SEQ], F32).ap()
        sh = Shared(nc, ctx)
        rope_attention(nc, sh, d)
        with ExitStack() as keys:
            ks = KeyState(nc, keys)
            key_queries(nc, sh, ks, d, sem)
            product_keys(nc, sh, ks, d, sem)
        layer1(nc, sh, d, sem)



def tokens(a):
    b, s, f = a.shape
    return np.ascontiguousarray(a.reshape(b, s // P, P, f).transpose(0, 2, 1, 3))


def columns(a):
    return np.ascontiguousarray(a.reshape(-1, P).T)


def layout(a):
    x0, f0, x1, f1 = "L0_xattn_", "L0_ffn_", "L1_xattn_", "L1_ffn_"
    w2 = a[f0 + "W2"]
    ctx = a["ctx_1024"]
    return {
        "x": tokens(a["x"]),
        "ctx": tokens(ctx),
        "ctxT": ctx.transpose(0, 2, 1).reshape(BATCH, DC, P, CTX).transpose(0, 2, 1, 3),
        "gates": np.concatenate([a["g_xattn"], a["g_ffn"]])[None, :],
        "wq": a[x0 + "Wq"], "wkv": a[x0 + "Wkv"], "wo": a[x0 + "Wo"], "bo": a[x0 + "bo"][None, :],
        "cosT": np.tile(a[x0 + "cos"].T, (P // (DHEAD // 2), 1)),
        "sinT": np.tile(a[x0 + "sin"].T, (P // (DHEAD // 2), 1)),
        "lat_g": columns(a[x0 + "ln_lat_g"]), "lat_b": columns(a[x0 + "ln_lat_b"]),
        "ctx_g": columns(a[x0 + "ln_ctx_g"]), "ctx_b": columns(a[x0 + "ln_ctx_b"]),
        "keys_wqT": a[f0 + "Wq"].reshape(QC * P, DIM).T,
        "keys_bq": columns(a[f0 + "bq"]), "keys_gamma": columns(a[f0 + "gamma"]),
        "keys_beta": columns(a[f0 + "beta"]),
        "sk1T": a[f0 + "sk1"].T, "sk2T": a[f0 + "sk2"].T,
        "latentsT": a[f0 + "latents"].T, "w1": a[f0 + "W1"],
        "w2xT": w2[:, :DIM].T, "w2v": w2[:, DIM:],
        "l1_wq": a[x1 + "kernel_q"][0, 0], "l1_wk": a[x1 + "kernel_k"][0, 0], "l1_wv": a[x1 + "kernel_v"][0, 0],
        "l1_bq": columns(a[x1 + "bias_q"]), "l1_bk": columns(a[x1 + "bias_k"]), "l1_bv": a[x1 + "bias_v"][None, :],
        "maskT": a["mask_1xSxS2_ff0"][0].T,
        "router": a[f1 + "router_DE"],
        "w_in_shared": a[f1 + "w_in_shared_FD"].T, "w_sw_shared": a[f1 + "w_swiglu_FD"].T,
        "w_out_shared": a[f1 + "w_out_shared_DF"].T,
        "w_in": a[f1 + "w_in_eDF"], "w_sw": a[f1 + "w_swiglu_eDF"], "w_out": a[f1 + "w_out_eFD"],
    }


def kernel(**inputs):
    import concourse.bacc as bacc
    from concourse.bass_utils import run_bass_kernel_spmd

    nc = bacc.Bacc("TRN2", target_bir_lowering=False, num_devices=1)
    arrays, d = {}, {}
    for name, a in layout({k: np.asarray(v) for k, v in inputs.items()}).items():
        a = np.ascontiguousarray(a)
        arrays["in_" + name] = a
        d[name] = nc.dram_tensor("in_" + name, a.shape, mybir.dt.from_np(a.dtype), kind="ExternalInput").ap()
    d["out"] = nc.dram_tensor("out", (BATCH, P, XT, DIM), F32, kind="ExternalOutput").ap()
    program(nc, d)
    out = run_bass_kernel_spmd(nc, [arrays], core_ids=[0]).results[0]["out"]
    return np.ascontiguousarray(out.transpose(0, 2, 1, 3)).reshape(BATCH, SEQ, DIM)
```

```python
from contextlib import ExitStack

import numpy as np

import concourse.bass as bass
import concourse.mybir as mybir
from concourse.alu_op_type import AluOpType as ALU

F32 = mybir.dt.float32
U32 = mybir.dt.uint32
ACT = mybir.ActivationFunctionType
AX = mybir.AxisListType

P = 128
BATCH, SEQ, DIM, CTX = 8, 512, 256, 1024
HEADS, DHEAD = 16, 64
INNER = HEADS * DHEAD
DC = DIM // P
XT = SEQ // P
KT = CTX // P
PAIRS = HEADS // 2
HALF = 512
EPS = 1e-5
CLIP, SCALE = 11.0, DHEAD ** -0.5


class Shared:

    def __init__(self, nc, ctx):
        self.x = ctx.enter_context(nc.sbuf_tensor("x_res", [P, BATCH, XT, DIM], F32))
        self.gate = ctx.enter_context(nc.sbuf_tensor("gate", [P, 4], F32))
        self.ident = ctx.enter_context(nc.sbuf_tensor("ident", [P, P], F32))
        self.eps = ctx.enter_context(nc.sbuf_tensor("epsilon", [P, 16], F32))
        self.mhalf = ctx.enter_context(nc.sbuf_tensor("minus_half", [P, 16], F32))



UNITS = PAIRS * KT
SCORE_SLOTS, PROB_SLOTS = 2, 4
ADD_LAG = 2
AV_LAG = 2


def rope_attention_misc():
    order = [("ctxT", c, h) for c in range(DC) for h in range(2)] + [("latT", c) for c in range(DC)]
    order += [("v", kt, 0) for kt in range(KT)]
    order += [("k", 0, 0), ("k", 0, 1), ("q", 0)]
    for i in range(UNITS):
        order += rope_attention_extras(i)
    order += [("den", PAIRS - 1)] + [("o", m) for m in range(XT // 2)]
    assert len(order) % 2 == 0
    return {name: n for n, name in enumerate(order)}


def rope_attention_extras(i):
    t, kt = divmod(i, KT)
    out = []
    if t + 1 < PAIRS and kt < 2:
        out.append(("k", t + 1, kt))
    if t + 1 < PAIRS and kt == 2:
        out.append(("q", t + 1))
    if kt == 3 and t >= 1:
        out.append(("den", t - 1))
    if t < 4 and kt in (4, 6):
        out.append(("v", 2 * t + (kt == 6), 1))
    return out


def rope_attention(nc, sh, d):
    MISC = rope_attention_misc()
    NM = len(MISC)
    with ExitStack() as ctx:
        def sb(name, shape):
            return ctx.enter_context(nc.sbuf_tensor("s1_" + name, shape, F32))

        def sem(name):
            return ctx.enter_context(nc.semaphore(name))

        x_res, gate, ident, mhalf, eps = sh.x, sh.gate, sh.ident, sh.mhalf, sh.eps
        wq, wkv, wo = sb("wq", [P, DC, INNER]), sb("wkv", [P, DC, 2 * INNER]), sb("wo", [P, PAIRS, DIM])
        cosT, sinT = sb("cosT", [P, CTX]), sb("sinT", [P, CTX])
        affine = sb("affine", [P, 4, DC])
        bo = sb("bo", [P, DIM])
        ctx_in, ctx_norm = sb("ctx_in", [P, KT, DIM]), sb("ctx_norm", [P, KT, DIM])
        ctxT = sb("ctxT", [P, DC, CTX])
        lat, latT = sb("lat", [P, XT, DIM]), sb("latT", [P, DC, SEQ])
        v = sb("v", [P, KT, INNER])
        kraw, kswap = sb("kraw", [P, CTX]), sb("kswap", [P, CTX])
        krope = sb("krope", [P, 2, CTX])
        qpad = sb("qpad", [P, 2, 2, SEQ])
        probs = sb("probs", [P, PROB_SLOTS, 2 * SEQ])
        psums = sb("prob_sums", [P, 2, 2 * SEQ])
        ones = sb("ones", [P, DHEAD])
        recip = sb("recip", [P, SEQ])
        oT = sb("oT", [P, PAIRS, SEQ])
        cst = sb("ctx_stats_sb", [P, KT, 6])
        cmv = sb("ctx_meanvar", [P, KT, 2])
        crs = sb("ctx_rstd_sb", [P, KT])
        xst = sb("x_stats_sb", [P, XT, 6])
        xmv = sb("x_meanvar", [P, XT, 2])
        xrs = sb("x_rstd_sb", [P, XT])

        ps_s = [ctx.enter_context(nc.psum_tensor(f"ps_scores{i}", [P, 2 * SEQ], F32)) for i in range(SCORE_SLOTS)]
        ps_av = [ctx.enter_context(nc.psum_tensor(f"ps_av{i}", [P, SEQ], F32)) for i in range(2)]
        ps_m = [ctx.enter_context(nc.psum_tensor(f"ps_misc{i}", [P, HALF], F32)) for i in range(2)]

        loaded = sem("weights_loaded")
        gates_in = sem("gates_in")
        zeroed = sem("pool_constants")
        ident_ready = sem("ident_ready")
        gates_ready = sem("gates_ready")
        tables_ready = sem("tables_ready")
        ctx_loaded, x_loaded = sem("ctx_loaded"), sem("x_loaded")
        ctx_stats, ctx_eps, ctx_rstd = sem("ctx_stats"), sem("ctx_eps"), sem("ctx_rstd")
        ctx_normed = sem("ctx_normed")
        x_sums, x_eps, x_rstd = sem("x_stats"), sem("x_eps"), sem("x_rstd")
        x_normed = sem("x_normed")
        x_biased = sem("x_biased")
        prep_seq = sem("prep_seq")
        misc_ready = sem("misc_ready")
        misc_evicted = [sem("misc_evicted0"), sem("misc_evicted1")]
        kswap_ready = sem("kswap_ready")
        rope_seq = sem("rope_seq")
        krope_ready = sem("krope_ready")
        scores_ready = sem("scores_ready")
        clipped = sem("scores_clipped")
        exp_done = sem("exp_done")
        added = sem("probs_added")
        probs_used = sem("probs_used")
        recip_ready = sem("recip_ready")
        passed = sem("waits_passed")

        block = ctx.enter_context(nc.Block())
        N_LOADS = 10
        MB = NM // 2

        def stop_until(eng, s, value):
            eng.wait_ge(s, value)
            eng.sem_inc(passed, 1)

        def wait_evicted(eng, b, name):
            n = MISC[name]
            eng.wait_ge(misc_evicted[n % 2], b * MB + n // 2 + 2)

        @block.sync
        def _(sp):
            sp.dma_start(wkv[:], d["wkv"].rearrange("(c p) n -> p c n", p=P)).then_inc(loaded, 16)
            sp.dma_start(wq[:], d["wq"].rearrange("(c p) n -> p c n", p=P)).then_inc(loaded, 16)
            sp.dma_start(cosT[:], d["cosT"]).then_inc(loaded, 16)
            sp.dma_start(sinT[:], d["sinT"]).then_inc(loaded, 16)
            for n, name in enumerate(("lat_g", "lat_b", "ctx_g", "ctx_b")):
                sp.dma_start(affine[:, n, :], d[name]).then_inc(loaded, 16)
            sp.dma_start(wo[:], d["wo"].rearrange("(t p) n -> p t n", p=P)).then_inc(loaded, 16)
            sp.dma_start(bo[:], d["bo"].to_broadcast([P, DIM])).then_inc(loaded, 16)
            with sp.Fori(0, BATCH) as b:
                for t in range(PAIRS):
                    for h in range(2):
                        wait_evicted(sp, b, ("k", t, h))
                        sp.sem_inc(passed, 1)
                    for q in range(4):
                        sp.dma_start(kswap[32 * q:32 * q + 32, :],
                                     kraw[32 * (q ^ 1):32 * (q ^ 1) + 32, :]).then_inc(kswap_ready, 16)

        @block.gpsimd
        def _(pool):
            nc.gpsimd.memset(ident[:], 0.0).then_inc(zeroed, 1)
            nc.gpsimd.memset(eps[:], EPS).then_inc(zeroed, 1)
            nc.gpsimd.memset(mhalf[:], -0.5).then_inc(zeroed, 1)
            pool.wait_ge(zeroed, 3)
            nc.gpsimd.affine_select(out=ident[:], in_=ident[:], compare_op=ALU.not_equal, fill=1.0, base=0,
                                    pattern=[[-1, P]], channel_multiplier=1).then_inc(ident_ready, 1)

            def load(b):
                nc.gpsimd.dma_start(ctx_in[:], d["ctx"][b]).then_inc(ctx_loaded, 16)
                nc.gpsimd.dma_start(x_res[:, b], d["x"][b]).then_inc(x_loaded, 16)

            def prepare(b):
                pool.wait_ge(ctx_stats, b + 1)
                nc.gpsimd.tensor_tensor(crs[:], cmv[:, :, 1], eps[:, 0:KT], ALU.add).then_inc(ctx_eps, 1)
                pool.wait_ge(ctx_eps, b + 1)
                nc.gpsimd.tensor_tensor(crs[:], crs[:], mhalf[:, 0:KT], ALU.pow).then_inc(ctx_rstd, 1)
                for n in range(2):
                    pool.wait_ge(x_sums, 2 * b + n + 1)
                    nc.gpsimd.tensor_tensor(xrs[:], xmv[:, :, 1], eps[:, 0:XT], ALU.add).then_inc(x_eps, 1)
                    pool.wait_ge(x_eps, 2 * b + n + 1)
                    nc.gpsimd.tensor_tensor(xrs[:], xrs[:], mhalf[:, 0:XT], ALU.pow).then_inc(x_rstd, 1)
                pool.wait_ge(x_normed, 2 * b + 1)
                for j in range(XT):
                    ins = nc.gpsimd.tensor_tensor(x_res[:, b, j, :], x_res[:, b, j, :], bo[:], ALU.add)
                ins.then_inc(x_biased, 1)

            load(0)
            pool.wait_ge(tables_ready, 1)
            with pool.Fori(0, BATCH - 1) as b:
                prepare(b)
                pool.wait_ge(ctx_normed, b + 1)
                load(b + 1)
            prepare(BATCH - 1)

        @block.scalar
        def _(act):
            nc.scalar.dma_start(gate[:], d["gates"].to_broadcast([P, 4])).then_inc(gates_in, 16)
            act.wait_ge(gates_in, 16)
            nc.scalar.activation(gate[:], gate[:], ACT.Tanh).then_inc(gates_ready, 1)
            act.wait_ge(loaded, 16 * N_LOADS)
            act.wait_ge(tables_ready, 1)

            def evict(b, name):
                n = MISC[name]
                act.wait_ge(misc_ready, b * NM + n + 1)
                src, kind = ps_m[n % 2], name[0]
                if kind == "ctxT":
                    _, c, h = name
                    ins = nc.scalar.activation(ctxT[:, c, h * HALF:(h + 1) * HALF], src[:], ACT.Identity,
                                               scale=affine[:, 2, c:c + 1], bias=affine[:, 3, c:c + 1])
                elif kind == "latT":
                    c = name[1]
                    ins = nc.scalar.activation(latT[:, c, :], src[:], ACT.Identity,
                                               scale=affine[:, 0, c:c + 1], bias=affine[:, 1, c:c + 1])
                elif kind == "v":
                    _, kt, h = name
                    ins = nc.scalar.copy(v[:, kt, h * HALF:(h + 1) * HALF], src[:])
                elif kind == "k":
                    ins = nc.scalar.copy(kraw[:, name[2] * HALF:(name[2] + 1) * HALF], src[:])
                else:
                    t = name[1]
                    nc.scalar.copy(qpad[0:DHEAD, t % 2, 0, :], src[0:DHEAD, :])
                    ins = nc.scalar.copy(qpad[DHEAD:P, t % 2, 1, :], src[DHEAD:P, :])
                ins.then_inc(misc_evicted[n % 2], 1)

            def batch(b):
                for name in MISC:
                    if name == ("k", 1, 0):
                        break
                    evict(b, name)
                for i in range(UNITS):
                    act.wait_ge(clipped, b * UNITS + i + 1)
                    p = probs[:, i % PROB_SLOTS, :]
                    nc.scalar.activation(p, p, ACT.Exp, scale=SCALE).then_inc(exp_done, 1)
                    for name in rope_attention_extras(i):
                        if name[0] != "den":
                            evict(b, name)

            with act.Fori(0, BATCH) as b:
                batch(b)

        @block.vector
        def _(dve):
            nc.vector.memset(qpad[:], 0.0)
            nc.vector.memset(ones[:], 1.0)
            dve.wait_ge(loaded, 16 * N_LOADS)
            for q in (0, 2):
                nc.vector.tensor_scalar(sinT[32 * q:32 * q + 32, :], sinT[32 * q:32 * q + 32, :], -1.0, None,
                                        ALU.mult)
            dve.wait_ge(gates_ready, 1)
            nc.vector.tensor_scalar(bo[:], bo[:], gate[:, 0:1], None, ALU.mult).then_inc(tables_ready, 1)
            for s in misc_evicted:
                dve.sem_inc(s, 1)

            def ctx_tile_stats(b, kt):
                if kt == 0:
                    dve.wait_ge(ctx_loaded, 16 * b + 16)
                nc.vector.bn_stats(cst[:, kt, :], ctx_in[:, kt, :]).then_inc(prep_seq, 1)
                if kt == KT - 1:
                    stop_until(dve, prep_seq, b * PREP + KT)
                    for k in range(KT):
                        ins = nc.vector.bn_aggr(cmv[:, k, :], cst[:, k, :])
                    ins.then_inc(ctx_stats, 1)

            def ctx_tile_norm(b, kt):
                if kt == 0:
                    dve.wait_ge(ctx_rstd, b + 1)
                ins = nc.vector.tensor_scalar(ctx_norm[:, kt, :], ctx_in[:, kt, :], cmv[:, kt, 0:1],
                                              crs[:, kt:kt + 1], ALU.subtract, ALU.mult)
                if kt == KT - 1:
                    ins.then_inc(ctx_normed, 1)

            def x_stats(b, n):
                if n == 0:
                    dve.wait_ge(x_loaded, 16 * b + 16)
                for j in range(XT):
                    src = lat[:, j, :] if n else x_res[:, b, j, :]
                    nc.vector.bn_stats(xst[:, j, :], src).then_inc(prep_seq, 1)
                stop_until(dve, prep_seq, b * PREP + KT + (n + 1) * XT)
                for j in range(XT):
                    ins = nc.vector.bn_aggr(xmv[:, j, :], xst[:, j, :])
                ins.then_inc(x_sums, 1)

            def x_norm(b, n):
                dve.wait_ge(x_rstd, 2 * b + n + 1)
                for j in range(XT):
                    src = lat[:, j, :] if n else x_res[:, b, j, :]
                    ins = nc.vector.tensor_scalar(lat[:, j, :], src, xmv[:, j, 0:1], xrs[:, j:j + 1],
                                                  ALU.subtract, ALU.mult)
                ins.then_inc(x_normed, 1)

            PREP = KT + 2 * XT

            def prepare_slot(b, i):
                t, kt = divmod(i, KT)
                if t == 1:
                    ctx_tile_stats(b, kt)
                elif t == 2:
                    ctx_tile_norm(b, kt)
                elif (t, kt) == (3, 0):
                    x_stats(b, 0)
                elif (t, kt) == (3, 6):
                    x_norm(b, 0)
                elif (t, kt) == (4, 0):
                    dve.wait_ge(x_normed, 2 * b + 1)
                    x_stats(b, 1)
                elif (t, kt) == (4, 6):
                    x_norm(b, 1)

            def rope(b, t):
                for h in range(2):
                    wait_evicted(dve, b, ("k", t, h))
                dve.wait_ge(kswap_ready, 64 * (b * PAIRS + t + 1))
                if t >= 2:
                    dve.wait_ge(scores_ready, b * UNITS + (t - 1) * KT)
                nc.vector.tensor_tensor(krope[:, t % 2, :], kraw[:], cosT[:], ALU.mult).then_inc(rope_seq, 1)
                nc.vector.tensor_tensor(kswap[:], kswap[:], sinT[:], ALU.mult).then_inc(rope_seq, 1)
                dve.wait_ge(rope_seq, 2 * (b * PAIRS + t + 1))
                nc.vector.tensor_tensor(krope[:, t % 2, :], krope[:, t % 2, :], kswap[:],
                                        ALU.add).then_inc(krope_ready, 1)

            def add(b, i):
                t, kt = divmod(i, KT)
                if kt == 0:
                    return
                s = psums[:, t % 2, :]
                if kt == 1:
                    dve.wait_ge(exp_done, b * UNITS + i + 1)
                    nc.vector.tensor_tensor(s, probs[:, (i - 1) % PROB_SLOTS, :], probs[:, i % PROB_SLOTS, :],
                                            ALU.add).then_inc(added, 2)
                else:
                    dve.wait_ge(exp_done, b * UNITS + i + 1)
                    dve.wait_ge(added, b * UNITS + i)
                    nc.vector.tensor_tensor(s, s, probs[:, i % PROB_SLOTS, :], ALU.add).then_inc(added, 1)

            def normalise(b, t):
                n = MISC[("den", t)]
                dve.wait_ge(misc_ready, b * NM + n + 1)
                nc.vector.reciprocal(recip[:], ps_m[n % 2][:]).then_inc(misc_evicted[n % 2], 1)
                wait_evicted(dve, b, ("den", t))
                dve.wait_ge(probs_used, b * UNITS + (t + 1) * KT)
                nc.vector.tensor_tensor(oT[:, t, :], ps_av[t % 2][:], recip[:], ALU.mult).then_inc(recip_ready, 1)

            def batch(b, last):
                rope(b, 0)
                for i in range(UNITS + ADD_LAG):
                    t, kt = divmod(i, KT)
                    if i < UNITS:
                        dve.wait_ge(scores_ready, b * UNITS + i + 1)
                        if i >= PROB_SLOTS:
                            dve.wait_ge(probs_used, b * UNITS + i - PROB_SLOTS + 1)
                            dve.wait_ge(added, b * UNITS + i - PROB_SLOTS + 1)
                        nc.vector.tensor_scalar(probs[:, i % PROB_SLOTS, :], ps_s[i % SCORE_SLOTS][:],
                                                CLIP / SCALE, -CLIP / SCALE, ALU.min, ALU.max).then_inc(clipped, 1)
                    if i >= ADD_LAG:
                        add(b, i - ADD_LAG)
                    if i < UNITS and kt == 4 and t + 1 < PAIRS:
                        rope(b, t + 1)
                    if i < UNITS and kt == 5 and t >= 1:
                        normalise(b, t - 1)
                    if i < UNITS and not last:
                        prepare_slot(b + 1, i)
                normalise(b, PAIRS - 1)
                dve.wait_ge(x_biased, b + 1)
                for m in range(XT // 2):
                    n = MISC[("o", m)]
                    dve.wait_ge(misc_ready, b * NM + n + 1)
                    x = x_res[:, b, 2 * m:2 * m + 2, :].rearrange("p j n -> p (j n)")
                    nc.vector.scalar_tensor_tensor(x, ps_m[n % 2][:], gate[:, 0:1], x, ALU.mult,
                                                   ALU.add).then_inc(misc_evicted[n % 2], 1)

            for kt in range(KT):
                ctx_tile_stats(0, kt)
            x_stats(0, 0)
            for kt in range(KT):
                ctx_tile_norm(0, kt)
            x_norm(0, 0)
            dve.wait_ge(x_normed, 1)
            x_stats(0, 1)
            x_norm(0, 1)
            with dve.Fori(0, BATCH - 1) as b:
                batch(b, False)
            batch(BATCH - 1, True)

        @block.tensor
        def _(pe):
            pe.wait_ge(loaded, 16 * N_LOADS)
            pe.wait_ge(ident_ready, 1)
            pe.wait_ge(tables_ready, 1)

            def misc(b, name):
                n = MISC[name]
                pe.wait_ge(misc_evicted[n % 2], b * MB + n // 2 + 1)
                return ps_m[n % 2]

            def extra(b, name):
                kind = name[0]
                out = misc(b, name)
                if kind == "ctxT":
                    _, c, h = name
                    for j in range(4):
                        ins = nc.tensor.transpose(out[:, j * P:(j + 1) * P],
                                                  ctx_norm[:, 4 * h + j, c * P:(c + 1) * P], ident[:])
                elif kind == "latT":
                    c = name[1]
                    for j in range(XT):
                        ins = nc.tensor.transpose(out[:, j * P:(j + 1) * P], lat[:, j, c * P:(c + 1) * P], ident[:])
                elif kind == "v":
                    _, kt, h = name
                    for c in range(DC):
                        ins = nc.tensor.matmul(out[:], ctxT[:, c, kt * P:(kt + 1) * P],
                                               wkv[:, c, INNER + h * HALF:INNER + (h + 1) * HALF],
                                               start=c == 0, stop=c == DC - 1)
                elif kind == "k":
                    _, t, h = name
                    for c in range(DC):
                        ins = nc.tensor.matmul(out[:], wkv[:, c, t * P:(t + 1) * P],
                                               ctxT[:, c, h * HALF:(h + 1) * HALF], start=c == 0, stop=c == DC - 1)
                elif kind == "q":
                    t = name[1]
                    for c in range(DC):
                        ins = nc.tensor.matmul(out[:], wq[:, c, t * P:(t + 1) * P], latT[:, c, :],
                                               start=c == 0, stop=c == DC - 1)
                elif kind == "den":
                    t = name[1]
                    pe.wait_ge(added, b * UNITS + (t + 1) * KT)
                    for a in range(2):
                        ins = nc.tensor.matmul(out[DHEAD * a:DHEAD * (a + 1), :], ones[:],
                                               psums[:, t % 2, a * SEQ:(a + 1) * SEQ], start=True, stop=True)
                else:
                    m = name[1]
                    for j in range(2):
                        for t in range(PAIRS):
                            ins = nc.tensor.matmul(out[:, j * DIM:(j + 1) * DIM],
                                                   oT[:, t, (2 * m + j) * P:(2 * m + j + 1) * P], wo[:, t, :],
                                                   start=t == 0, stop=t == PAIRS - 1)
                ins.then_inc(misc_ready, 1)

            def scores(b, i):
                t, kt = divmod(i, KT)
                if kt == 0:
                    pe.wait_ge(krope_ready, b * PAIRS + t + 1)
                    wait_evicted(pe, b, ("q", t))
                if i >= SCORE_SLOTS:
                    pe.wait_ge(clipped, b * UNITS + i - SCORE_SLOTS + 1)
                for a in range(2):
                    ins = nc.tensor.matmul(ps_s[i % SCORE_SLOTS][:, a * SEQ:(a + 1) * SEQ],
                                           krope[:, t % 2, kt * P:(kt + 1) * P], qpad[:, t % 2, a, :],
                                           start=True, stop=True)
                ins.then_inc(scores_ready, 1)

            def values(b, i):
                t, kt = divmod(i, KT)
                pe.wait_ge(exp_done, b * UNITS + i + 1)
                if t % 4 == 0:
                    wait_evicted(pe, b, ("v", kt, t // 4))
                if kt == 0 and t >= 2:
                    pe.wait_ge(recip_ready, b * PAIRS + t - 1)
                for a in range(2):
                    col = (2 * t + a) * DHEAD
                    ins = nc.tensor.matmul(ps_av[t % 2][DHEAD * a:DHEAD * (a + 1), :], v[:, kt, col:col + DHEAD],
                                           probs[:, i % PROB_SLOTS, a * SEQ:(a + 1) * SEQ],
                                           start=kt == 0, stop=kt == KT - 1)
                ins.then_inc(probs_used, 1)

            with pe.Fori(0, BATCH) as b:
                pe.wait_ge(ctx_normed, b + 1)
                for name in MISC:
                    if name == ("k", 1, 0):
                        break
                    if name == ("latT", 0):
                        pe.wait_ge(x_normed, 2 * b + 2)
                    if name == ("v", 0, 0):
                        for c in range(DC):
                            wait_evicted(pe, b, ("latT", c))
                    extra(b, name)
                for i in range(UNITS + AV_LAG):
                    if i < UNITS:
                        scores(b, i)
                        for name in rope_attention_extras(i):
                            extra(b, name)
                    if i >= AV_LAG:
                        values(b, i - AV_LAG)
                extra(b, ("den", PAIRS - 1))
                pe.wait_ge(recip_ready, (b + 1) * PAIRS)
                for m in range(XT // 2):
                    extra(b, ("o", m))



class RowNorm:

    def __init__(self, nc, ctx, sh, name, sem):
        def sb(part, shape):
            return ctx.enter_context(nc.sbuf_tensor(f"{name}_{part}", shape, F32))

        self.nc, self.sh = nc, sh
        self.out = sb("normed", [P, XT, DIM])
        self.sums, self.meanvar, self.rstd = sb("sums", [P, XT, 6]), sb("meanvar", [P, XT, 2]), sb("rstd", [P, XT])
        self.summed = sem(name + "_summed")
        self.stats = sem(name + "_stats")
        self.eps_added, self.rstd_ready = sem(name + "_eps_added"), sem(name + "_rstd_ready")
        self.ready = sem(name + "_ready")
        self.passed = sem(name + "_passed")

    def statistics(self, dve, turn, b):
        for j in range(XT):
            self.nc.vector.bn_stats(self.sums[:, j, :], self.sh.x[:, b, j, :]).then_inc(self.summed, 1)
        dve.wait_ge(self.summed, XT * turn + XT)
        dve.sem_inc(self.passed, 1)
        for j in range(XT):
            ins = self.nc.vector.bn_aggr(self.meanvar[:, j, :], self.sums[:, j, :])
        ins.then_inc(self.stats, 1)

    def power(self, pool, turn):
        pool.wait_ge(self.stats, turn + 1)
        self.nc.gpsimd.tensor_tensor(self.rstd[:], self.meanvar[:, :, 1], self.sh.eps[:, 0:XT],
                                     ALU.add).then_inc(self.eps_added, 1)
        pool.wait_ge(self.eps_added, turn + 1)
        self.nc.gpsimd.tensor_tensor(self.rstd[:], self.rstd[:], self.sh.mhalf[:, 0:XT],
                                     ALU.pow).then_inc(self.rstd_ready, 1)

    def apply(self, dve, turn, b):
        dve.wait_ge(self.rstd_ready, turn + 1)
        for j in range(XT):
            ins = self.nc.vector.tensor_scalar(self.out[:, j, :], self.sh.x[:, b, j, :], self.meanvar[:, j, 0:1],
                                               self.rstd[:, j:j + 1], ALU.subtract, ALU.mult)
        ins.then_inc(self.ready, 1)



KEY_HEADS, D_QUERY, SUBKEYS, D_LATENT, D_HIDDEN = 4, 64, 128, 64, 128
EXPERTS = 4096
TOP = 8
PICKS = KEY_HEADS * TOP
QC = KEY_HEADS * D_QUERY // P
ET = EXPERTS // P


class KeyState:

    def __init__(self, nc, ctx):
        self.scale = ctx.enter_context(nc.sbuf_tensor("keys_scale", [P, QC], F32))
        self.shift = ctx.enter_context(nc.sbuf_tensor("keys_shift", [P, QC], F32))


def key_queries(nc, sh, ks, d, sem):
    with ExitStack() as ctx:
        def sb(name, shape):
            return ctx.enter_context(nc.sbuf_tensor("s2_" + name, shape, F32))

        ident = sh.ident
        norm = RowNorm(nc, ctx, sh, "s2_norm", sem)
        wq, wx = sb("wq", [P, DC, QC * P]), sb("wx", [P, DC, D_HIDDEN])
        cols = sb("cols", [P, 3, QC])
        latT, w1 = sb("latentsT", [D_LATENT, EXPERTS]), sb("w1", [D_LATENT, D_HIDDEN])
        hidden = sb("hidden", [P, 2, 4, D_HIDDEN])
        xT = sb("xT", [P, DC, SEQ])
        qT, proj = sb("qT", [P, BATCH, QC, SEQ]), sb("proj", [P, BATCH, XT, D_HIDDEN])
        qsums, qmv = sb("q_sums", [P, QC, BATCH, 6]), sb("q_meanvar", [P, QC, 2])
        qrs = sb("q_rstd", [P, QC])
        ps_t = [ctx.enter_context(nc.psum_tensor(f"s2_ps_t{c}", [P, HALF], F32)) for c in range(DC)]
        ps_q = [ctx.enter_context(nc.psum_tensor(f"s2_ps_q{c}", [P, HALF], F32)) for c in range(QC)]
        ps_x = ctx.enter_context(nc.psum_tensor("s2_ps_x", [P, XT, D_HIDDEN], F32))
        ps_h = [ctx.enter_context(nc.psum_tensor(f"s2_ps_h{c}", [P, 4, D_HIDDEN], F32)) for c in range(2)]

        loaded, hid_ready, hid_done, hid_out = sem("s2_loaded"), sem("hidden_ready"), sem("hidden_done"), \
            [sem("hidden_out0"), sem("hidden_out1")]
        t_ready, t_out = sem("s2_transposed"), sem("s2_xT_out")
        q_ready, q_out = sem("s2_q_ready"), sem("s2_q_out")
        p_ready, p_out = sem("s2_proj_ready"), sem("s2_proj_out")
        q_summed, q_eps, q_rstd, steps = sem("s2_q_summed"), sem("s2_q_eps"), sem("s2_q_rstd"), sem("s2_steps")
        q_stats, passed = sem("s2_q_stats"), sem("s2_passed")
        q_stored = sem("s2_stored")
        N_LOADS = 7
        block = ctx.enter_context(nc.Block())

        @block.sync
        def _(sp):
            sp.dma_start(latT[:], d["latentsT"]).then_inc(loaded, 16)
            sp.dma_start(w1[:], d["w1"]).then_inc(loaded, 16)
            sp.dma_start(wq[:], d["keys_wqT"].rearrange("(c p) n -> p c n", p=P)).then_inc(loaded, 16)
            sp.dma_start(wx[:], d["w2xT"].rearrange("(c p) n -> p c n", p=P)).then_inc(loaded, 16)
            for n, name in enumerate(("keys_bq", "keys_gamma", "keys_beta")):
                sp.dma_start(cols[:, n, :], d[name]).then_inc(loaded, 16)
            for n in range(ET // 4):
                sp.wait_ge(hid_done, n + 1)
                sp.dma_start(d["table"][4 * n * P:4 * (n + 1) * P, :].rearrange("(j p) f -> p j f", p=P),
                             hidden[:, n % 2]).then_inc(hid_out[n % 2], 16)
            for s in hid_out:
                sp.wait_ge(s, 16 * ET // 8)
            with sp.Fori(0, BATCH) as b:
                sp.wait_ge(q_out, QC * (b + 1))
                sp.sem_inc(passed, 1)
                sp.dma_start(d["q_dram"][b], qT[:, b]).then_inc(q_stored, 16)
                sp.wait_ge(p_out, b + 1)
                sp.sem_inc(passed, 1)
                sp.dma_start(d["proj_dram"][b], proj[:, b]).then_inc(q_stored, 16)
            sp.wait_ge(q_stored, 32 * BATCH)

        @block.gpsimd
        def _(pool):
            with pool.Fori(0, BATCH) as b:
                norm.power(pool, b)
            pool.wait_ge(q_stats, 1)
            nc.gpsimd.tensor_tensor(qrs[:], qmv[:, :, 1], sh.eps[:, 0:QC], ALU.add).then_inc(q_eps, 1)
            pool.wait_ge(q_eps, 1)
            nc.gpsimd.tensor_tensor(qrs[:], qrs[:], sh.mhalf[:, 0:QC], ALU.pow).then_inc(q_rstd, 1)

        @block.scalar
        def _(act):
            act.wait_ge(loaded, 16 * N_LOADS)
            for n in range(ET // 4):
                act.wait_ge(hid_ready, n + 1)
                if n >= 2:
                    act.wait_ge(hid_out[n % 2], 16 * (n // 2))
                nc.scalar.activation(hidden[:, n % 2].rearrange("p j f -> p (j f)"),
                                     ps_h[n % 2][:].rearrange("p j f -> p (j f)"), ACT.Gelu).then_inc(hid_done, 1)
            with act.Fori(0, BATCH) as b:
                for c in range(DC):
                    act.wait_ge(t_ready, DC * b + c + 1)
                    nc.scalar.copy(xT[:, c, :], ps_t[c][:]).then_inc(t_out, 1)
                for c in range(QC):
                    act.wait_ge(q_ready, QC * b + c + 1)
                    nc.scalar.activation(qT[:, b, c, :], ps_q[c][:], ACT.Identity,
                                         bias=cols[:, 0, c:c + 1]).then_inc(q_out, 1)
                act.wait_ge(p_ready, b + 1)
                nc.scalar.copy(proj[:, b].rearrange("p j f -> p (j f)"),
                               ps_x[:].rearrange("p j f -> p (j f)")).then_inc(p_out, 1)

        @block.vector
        def _(dve):
            def query_sums(b):
                for c in range(QC):
                    dve.wait_ge(q_out, QC * b + c + 1)
                    nc.vector.bn_stats(qsums[:, c, b, :], qT[:, b, c, :]).then_inc(q_summed, 1)

            norm.statistics(dve, 0, 0)
            norm.apply(dve, 0, 0)
            with dve.Fori(0, BATCH - 1) as b:
                norm.statistics(dve, b + 1, b + 1)
                dve.wait_ge(t_ready, DC * b + DC)
                dve.sem_inc(passed, 1)
                norm.apply(dve, b + 1, b + 1)
                query_sums(b)
            query_sums(BATCH - 1)
            dve.wait_ge(q_summed, QC * BATCH)
            for c in range(QC):
                ins = nc.vector.bn_aggr(qmv[:, c, :], qsums[:, c].rearrange("p b s -> p (b s)"))
            ins.then_inc(q_stats, 1)
            dve.wait_ge(q_rstd, 1)
            dve.wait_ge(loaded, 16 * N_LOADS)
            nc.vector.tensor_tensor(ks.scale[:], qrs[:], cols[:, 1, :], ALU.mult).then_inc(steps, 1)
            dve.wait_ge(steps, 1)
            nc.vector.tensor_tensor(ks.shift[:], qmv[:, :, 0], ks.scale[:], ALU.mult).then_inc(steps, 1)
            dve.wait_ge(steps, 2)
            nc.vector.tensor_tensor(ks.shift[:], cols[:, 2, :], ks.shift[:], ALU.subtract).then_inc(steps, 1)

        @block.tensor
        def _(pe):
            pe.wait_ge(loaded, 16 * N_LOADS)
            for n in range(ET // 4):
                if n >= 2:
                    pe.wait_ge(hid_done, n - 1)
                for j in range(4):
                    ins = nc.tensor.matmul(ps_h[n % 2][:, j, :], latT[:, (4 * n + j) * P:(4 * n + j + 1) * P], w1[:],
                                           start=True, stop=True)
                ins.then_inc(hid_ready, 1)

            def body(b, first):
                pe.wait_ge(norm.ready, b + 1)
                for c in range(DC):
                    if not first and c == 0:
                        pe.wait_ge(t_out, DC * b)
                    for j in range(XT):
                        ins = nc.tensor.transpose(ps_t[c][:, j * P:(j + 1) * P], norm.out[:, j, c * P:(c + 1) * P],
                                                  ident[:])
                    ins.then_inc(t_ready, 1)
                pe.wait_ge(t_out, DC * (b + 1))
                for m in range(QC):
                    if not first and m == 0:
                        pe.wait_ge(q_out, QC * b)
                    for c in range(DC):
                        ins = nc.tensor.matmul(ps_q[m][:], wq[:, c, m * P:(m + 1) * P], xT[:, c, :],
                                               start=c == 0, stop=c == DC - 1)
                    ins.then_inc(q_ready, 1)
                if not first:
                    pe.wait_ge(p_out, b)
                for j in range(XT):
                    for c in range(DC):
                        ins = nc.tensor.matmul(ps_x[:, j, :], xT[:, c, j * P:(j + 1) * P], wx[:, c, :],
                                               start=c == 0, stop=c == DC - 1)
                ins.then_inc(p_ready, 1)

            body(0, True)
            with pe.Fori(1, BATCH) as b:
                body(b, False)



LISTS = 2 * KEY_HEADS
GROUPS = XT * KEY_HEADS
HALVES = 2 * XT
HP = PICKS // 2
MOE, FF = 8, 512
FT = FF // P
BLOCKS = (MOE + 1) * FT
LOGIT_SLOTS = 4
FIRST_HALF = 3


def half_step(n):
    u, step = divmod(n - FIRST_HALF, 4)
    return (u, step) if 0 <= u < HALVES else None


def tile_at(n, lag):
    j, r = divmod(n - lag - FIRST_HALF - 7, 8)
    return j if r == 0 and 0 <= j < XT else None


TAIL = 4


class Order:

    def __init__(self, names, before):
        assert len(names) % 2 == 0 and before % 2 == 0
        self.names, self.before, self.no = names, before, {name: n for n, name in enumerate(names)}

    def made(self, b, name):
        return self.before + self.turn * b + self.no[name] + 1

    def bank(self, name):
        return self.no[name] % 2

    def free(self, b, name):
        return (self.before + self.turn * b) // 2 + self.no[name] // 2 + 1 if isinstance(b, int) else \
            b * (self.turn // 2) + self.before // 2 + self.no[name] // 2 + 1

    def out(self, b, name):
        return self.free(b, name) + 1


def orders():
    s = [[("s", j, c) for c in range(QC)] for j in range(XT)]
    first = sum(s, []) + [x for j in range(XT) for x in (("accT", j), ("keys", j))]

    def turn(with_keys):
        none = [[]] * XT
        s_ = s if with_keys else none
        names = s_[0] + s_[1] + [("xT", 0, c) for c in range(DC)]
        names += [("k", 0, 0), ("k", 0, 1)] + s_[2] + [("k", 1, 0), ("k", 1, 1)] + [("q", c) for c in range(DC)]
        names += s_[3] + [("v", n) for n in range(KT // 2)]
        names += [("xT", 1, c) for c in range(DC)] + [("router",), ("gatesT",)]
        if with_keys:
            names += [x for j in range(XT) for x in (("accT", j), ("keys", j))]
        return names

    Order.turn = len(turn(True))
    return Order(first, 0), Order(turn(True), len(first)), Order(turn(False), len(first))


def keys_and_layer1(nc, sh, ks, d, sem):
    with ExitStack() as ctx:
        def sb(name, shape, dt=F32):
            return ctx.enter_context(nc.sbuf_tensor("s3_" + name, shape, dt))

        x_res, gate, ident = sh.x, sh.gate, sh.ident
        subkeys = sb("subkeys", [P, 4, SUBKEYS])
        wkeys = sb("wkeys", [D_HIDDEN, DIM])
        gate4 = sb("gate4", [P, 1])
        digits_i, digits = sb("digits_i", [P, TOP], mybir.dt.int32), sb("digits", [P, TOP])
        qn, proj = sb("qn", [P, QC, SEQ]), sb("proj", [P, XT, D_HIDDEN])
        scores = sb("scores", [P, 2, LISTS, SUBKEYS])
        best, best_at = sb("best", [P, XT, LISTS, TOP]), sb("best_at", [P, XT, LISTS, TOP], U32)
        pair = sb("pair_sums", [P, GROUPS, TOP, TOP])
        top, top_at = sb("top", [P, GROUPS, TOP]), sb("top_at", [P, GROUPS, TOP], U32)
        digit = sb("digit", [P, GROUPS, 2, TOP], U32)
        prod = sb("prod", [P, HP * D_HIDDEN])
        pick = prod[:].rearrange("p (n a) -> p n a", a=TOP)
        part = sb("part", [P, GROUPS, 2, TOP])
        expert, expert_at = sb("expert", [P, GROUPS, TOP]), sb("expert_at", [P, XT * PICKS], U32)
        prob, prob_sum = sb("prob", [P, GROUPS, TOP]), sb("prob_sum", [P, GROUPS])
        rows = sb("rows", [P, 2, HP, D_HIDDEN])
        dots, acts = sb("dots", [P, 2, HP]), sb("acts", [P, 2, HP])
        acc, accT = sb("acc", [P, 4, D_HIDDEN]), sb("accT", [P, 2, P])
        norm = RowNorm(nc, ctx, sh, "s3_norm", sem)
        wq, wk, wv = sb("wq", [P, DC, DIM]), sb("wk", [P, DC, DIM]), sb("wv", [P, DC, DIM])
        bq, bk, bv = sb("bq", [P, DC]), sb("bk", [P, DC]), sb("bv", [P, 2, DIM])
        maskT = sb("maskT", [P, KT, SEQ])
        ctxT = sb("ctxT", [P, DC, CTX])
        kp, vp, qp = sb("kp", [P, DC, CTX]), sb("vp", [P, KT, DIM]), sb("qp", [P, DC, SEQ])
        logits = sb("logits", [P, LOGIT_SLOTS, SEQ])
        act_in, hid = logits[:, 0:2, :], logits[:, 2:4, :]
        xT = sb("xT", [P, DC, SEQ])
        router = sb("router", [P, DC, MOE])
        w_in, w_sw = sb("w_in", [P, 3, DC, FF]), sb("w_sw", [P, 3, DC, FF])
        w_out = sb("w_out", [P, 3, FT, DIM])
        rs, rs_top = sb("router_scores", [P, XT, MOE]), sb("router_top", [P, XT, TOP])
        rs_at = sb("router_at", [P, XT, TOP], U32)
        second, gates, sig = sb("second", [P, XT, MOE]), sb("gates", [P, XT, MOE]), sb("sigmoids", [P, XT, MOE])
        gatesT = sb("gatesT", [MOE, SEQ])
        gates_all = sb("gates_all", [P, 2, SEQ])
        xg = sb("xg", [P, 2, DC, SEQ])
        attn = xg[:, 0].rearrange("p c q -> p (c q)")

        ps_m = [ctx.enter_context(nc.psum_tensor(f"s3_ps_m{c}", [P, HALF], F32)) for c in range(2)]
        ps_o = ctx.enter_context(nc.psum_tensor("s3_ps_o", [P, XT, DIM], F32))
        ps_a = [ctx.enter_context(nc.psum_tensor(f"s3_ps_a{c}", [P, HALF], F32)) for c in range(2)]
        ps_b = [ctx.enter_context(nc.psum_tensor(f"s3_ps_b{c}", [P, HALF], F32)) for c in range(2)]

        loaded, consts, bias_scaled = sem("s3_loaded"), sem("s3_consts"), sem("s3_bias_scaled")
        zeroed = sem("s3_zeroed")
        misc_made, misc_out = sem("misc_made"), [sem("misc_out0"), sem("misc_out1")]
        q_loaded, qn_ready = sem("q_loaded"), sem("qn_ready")
        listed = sem("listed")
        steps = sem("choice_steps")
        diffs, exps = sem("prob_diffs"), sem("prob_exps")
        experts = sem("experts_known")
        gathered = [sem("rows_gathered0"), sem("rows_gathered1")]
        weighed = sem("rows_weighed")
        dotted, gelued = sem("rows_dotted"), sem("dots_gelued")
        used = sem("rows_used")
        keys_done = sem("keys_added")
        ctx_loaded, expert_in = sem("l1_ctx_loaded"), [sem("expert_in0"), sem("expert_in1")]
        relued = sem("v_relued")
        s_ready, s_out = sem("l1_scores"), sem("l1_logits")
        av_ready, attn_out, x_done = sem("l1_av"), sem("l1_attn_out"), sem("l1_x_attended")
        route_steps, sig_ready, gates_ready = sem("route_steps"), sem("sigmoids_ready"), sem("gates_chosen")
        gates_stored, gates_in = sem("gates_stored"), [sem("gates_in0"), sem("gates_in1")]
        xg_ready = sem("rows_gated")
        a_ready, a_out, h_ready, h_used = sem("first_ready"), sem("silu_out"), sem("hidden_ready_l1"), sem("hidden_used")
        moe_out, stored = sem("moe_added"), sem("out_stored")
        passed = sem("s3_waits_passed")
        N_LOADS = 11 + 5
        FIRST, LOOP, LAST = orders()
        block = ctx.enter_context(nc.Block())

        def stop_until(eng, s, value):
            eng.wait_ge(s, value)
            eng.sem_inc(passed, 1)

        def wait_made(eng, o, b, name):
            eng.wait_ge(misc_made, o.made(b, name))

        def wait_out(eng, o, b, name):
            eng.wait_ge(misc_out[o.bank(name)], o.out(b, name))

        @block.sync
        def _(sp):
            sp.dma_start(qn[:], d["q_dram"][0]).then_inc(q_loaded, 16)
            sp.dma_start(proj[:], d["proj_dram"][0]).then_inc(q_loaded, 16)
            sp.dma_start(wkeys[:], d["w2v"]).then_inc(loaded, 16)
            sp.wait_ge(zeroed, 1)
            for n in range(4):
                sp.dma_start(subkeys[32 * n:32 * n + 32, n, :], d[f"sk{n % 2 + 1}T"]).then_inc(loaded, 16)
            for t, name in ((wk, "l1_wk"), (wq, "l1_wq"), (wv, "l1_wv"), (router, "router")):
                sp.dma_start(t[:], d[name].rearrange("(c p) n -> p c n", p=P)).then_inc(loaded, 16)
            sp.dma_start(bq[:], d["l1_bq"]).then_inc(loaded, 16)
            sp.dma_start(bk[:], d["l1_bk"]).then_inc(loaded, 16)
            sp.dma_start(bv[:], d["l1_bv"].unsqueeze(1).to_broadcast([P, 2, DIM])).then_inc(loaded, 16)
            sp.dma_start(w_in[:, 2], d["w_in_shared"].rearrange("(c p) n -> p c n", p=P)).then_inc(loaded, 16)
            sp.dma_start(w_sw[:, 2], d["w_sw_shared"].rearrange("(c p) n -> p c n", p=P)).then_inc(loaded, 16)
            sp.dma_start(w_out[:, 2], d["w_out_shared"].rearrange("(f p) n -> p f n", p=P)).then_inc(loaded, 16)
            sp.dma_start(maskT[:], d["maskT"].rearrange("(t p) q -> p t q", p=P)).then_inc(loaded, 16)

            def expert_weights(b, e, first):
                if not first:
                    stop_until(sp, h_used, b * BLOCKS + (e if e >= 2 else e - 1) * FT)
                s = e % 2
                sp.dma_start(w_in[:, s], d["w_in"][e].rearrange("(c p) n -> p c n", p=P)).then_inc(expert_in[s], 16)
                sp.dma_start(w_sw[:, s], d["w_sw"][e].rearrange("(c p) n -> p c n", p=P)).then_inc(expert_in[s], 16)
                sp.dma_start(w_out[:, s], d["w_out"][e].rearrange("(f p) n -> p f n", p=P)).then_inc(expert_in[s], 16)

            def batch(b, o, first):
                if not first:
                    stop_until(sp, misc_made, LOOP.made(b - 1, ("v", KT // 2 - 1)))
                sp.dma_start(ctxT[:], d["ctxT"][b]).then_inc(ctx_loaded, 16)
                for e in range(2):
                    expert_weights(b, e, first)
                if o is LOOP:
                    stop_until(sp, used, HALVES * (b + 1))
                    sp.dma_start(qn[:], d["q_dram"][b + 1]).then_inc(q_loaded, 16)
                    sp.dma_start(proj[:], d["proj_dram"][b + 1]).then_inc(q_loaded, 16)
                if not first:
                    stop_until(sp, moe_out, b)
                    sp.dma_start(d["out"][b - 1], x_res[:, b - 1]).then_inc(stored, 16)
                wait_out(sp, o, b, ("gatesT",))
                sp.sem_inc(passed, 1)
                sp.dma_start(d["gates_dram"], gatesT[:]).then_inc(gates_stored, 16)
                stop_until(sp, gates_stored, 16 * (b + 1))
                for e in range(MOE):
                    if e >= 2:
                        stop_until(sp, xg_ready, MOE * b + e - 1)
                    sp.dma_start(gates_all[:, e % 2, :],
                                 d["gates_dram"][e:e + 1, :].to_broadcast([P, SEQ])).then_inc(gates_in[e % 2], 16)
                    if e >= 2:
                        expert_weights(b, e, False)

            batch(0, LOOP, True)
            with sp.Fori(1, BATCH - 1) as b:
                batch(b, LOOP, False)
            batch(BATCH - 1, LAST, False)
            sp.wait_ge(moe_out, BATCH)
            sp.dma_start(d["out"][BATCH - 1], x_res[:, BATCH - 1]).then_inc(stored, 16)
            sp.wait_ge(stored, 16 * BATCH)

        @block.gpsimd
        def _(pool):
            nc.gpsimd.iota(digits_i[:], pattern=[[1, TOP]], base=0, channel_multiplier=0).then_inc(consts, 1)
            pool.wait_ge(consts, 1)
            nc.gpsimd.tensor_copy(digits[:], digits_i[:]).then_inc(consts, 1)

            def gather(b, us, first=False):
                for u in us:
                    if not (first and u < 2):
                        stop_until(pool, used, HALVES * b + u - 1)
                    for k in range(HP):
                        at = u * HP + k
                        nc.gpsimd.indirect_dma_start(
                            out=rows[:, u % 2, k, :], out_offset=None, in_=d["table"],
                            in_offset=bass.IndirectOffsetOnAxis(ap=expert_at[:, at:at + 1], axis=0),
                        ).then_inc(gathered[u % 2], 16)

            pool.wait_ge(experts, 1)
            gather(0, range(HALVES), True)
            with pool.Fori(0, BATCH - 1) as b:
                norm.power(pool, 2 * b)
                pool.wait_ge(experts, b + 2)
                gather(b + 1, range(1))
                norm.power(pool, 2 * b + 1)
                gather(b + 1, range(1, HALVES))
            for n in range(2):
                norm.power(pool, 2 * (BATCH - 1) + n)

        @block.scalar
        def _(act):
            act.wait_ge(loaded, 16 * N_LOADS)
            nc.scalar.mul(bq[:], bq[:], 1.0 / 16.0).then_inc(bias_scaled, 1)
            act.wait_ge(bias_scaled, 1)
            for s in misc_out:
                act.sem_inc(s, 1)

            def queries(kb):
                act.wait_ge(q_loaded, 32 * (kb + 1))
                for c in range(QC):
                    nc.scalar.activation(qn[:, c, :], qn[:, c, :], ACT.Identity, scale=ks.scale[:, c:c + 1],
                                         bias=ks.shift[:, c:c + 1]).then_inc(qn_ready, 1)

            def take(o, b, name, kb=None):
                kind = name[0]
                wait_made(act, o, b, name)
                src = ps_m[o.bank(name)]
                if kind == "s":
                    _, j, c = name
                    if j >= 2 and c == 0:
                        act.wait_ge(listed, 2 * (XT * kb + j - 1))
                    ins = nc.scalar.copy(scores[:, j % 2, 4 * c:4 * c + 4, :].rearrange("p l k -> p (l k)"), src[:])
                elif kind == "accT":
                    ins = nc.scalar.copy(accT[:, name[1] % 2, :], src[:, 0:P])
                elif kind == "xT":
                    ins = nc.scalar.copy(xT[:, name[2], :], src[:])
                elif kind == "k":
                    _, m, h = name
                    ins = nc.scalar.activation(kp[:, m, h * HALF:(h + 1) * HALF], src[:], ACT.Relu, bias=bk[:, m:m + 1])
                elif kind == "q":
                    ins = nc.scalar.activation(qp[:, name[1], :], src[:], ACT.Relu, bias=bq[:, name[1]:name[1] + 1],
                                               scale=1.0 / 16.0)
                else:
                    ins = nc.scalar.copy(gatesT[:], src[0:MOE, :])
                ins.then_inc(misc_out[o.bank(name)], 1)

            def exponentials(kb):
                act.wait_ge(diffs, kb + 1)
                p = prob[:].rearrange("p h k -> p (h k)")
                nc.scalar.activation(p, p, ACT.Exp).then_inc(exps, 1)

            def gelu(kb, u):
                act.wait_ge(dotted, HALVES * kb + u + 1)
                nc.scalar.activation(acts[:, u % 2, :], dots[:, u % 2, :], ACT.Gelu).then_inc(gelued, 1)

            def batch(b, o):
                keys = o is LOOP
                if keys:
                    queries(b + 1)
                for name in o.names[:o.no[("v", 0)]]:
                    take(o, b, name, b + 1)
                for n in range(KT // 2):
                    wait_out(act, o, b, ("v", n))
                    v = vp[:, 2 * n:2 * n + 2, :].rearrange("p t n -> p (t n)")
                    nc.scalar.activation(v, v, ACT.Relu).then_inc(relued, 1)
                if keys:
                    exponentials(b + 1)
                act.wait_ge(av_ready, KT * (b + 1))
                nc.scalar.activation(attn, ps_o[:].rearrange("p j n -> p (j n)"), ACT.Relu).then_inc(attn_out, 1)
                for c in range(DC):
                    take(o, b, ("xT", 1, c))
                wait_out(act, o, b, ("router",))
                nc.scalar.activation(sig[:], rs[:], ACT.Sigmoid).then_inc(sig_ready, 1)
                for n in range(BLOCKS + TAIL):
                    if n == FT:
                        take(o, b, ("gatesT",))
                    if n < BLOCKS:
                        act.wait_ge(a_ready, b * BLOCKS + n + 1)
                        if n >= 2:
                            act.wait_ge(h_ready, b * BLOCKS + n - 1)
                        nc.scalar.activation(act_in[:, n % 2, :], ps_a[n % 2][:], ACT.Silu).then_inc(a_out, 1)
                    if keys and (half := half_step(n)) and half[1] == 1:
                        gelu(b + 1, half[0])
                    if keys and (j := tile_at(n, 1)) is not None:
                        take(o, b, ("accT", j))

            queries(0)
            for name in FIRST.names[:XT * QC]:
                take(FIRST, 0, name, 0)
            exponentials(0)
            for u in range(HALVES):
                gelu(0, u)
                if u % 2:
                    take(FIRST, 0, ("accT", u // 2))
            with act.Fori(0, BATCH - 1) as b:
                batch(b, LOOP)
            batch(BATCH - 1, LAST)

        @block.vector
        def _(dve):
            nc.vector.memset(subkeys[:], 0.0).then_inc(zeroed, 1)
            nc.vector.tensor_scalar(gate4[:], gate[:, 2:3], 1.0 / KEY_HEADS, None, ALU.mult)
            dve.wait_ge(consts, 2)
            dve.wait_ge(loaded, 16 * N_LOADS)
            CHOICE_STEPS, ROUTE_STEPS = 11, 4

            def lists(o, b, kb, j):
                wait_out(dve, o, b, ("s", j, 0))
                dve.sem_inc(passed, 1)
                stop_until(dve, misc_out[o.bank(("s", j, 1))], o.out(b, ("s", j, 1)))
                for n in range(LISTS):
                    ins = nc.vector.max(best[:, j, n, :], scores[:, j % 2, n, :])
                ins.then_inc(listed, 1)
                stop_until(dve, listed, 2 * (XT * kb + j) + 1)
                for n in range(LISTS):
                    ins = nc.vector.max_index(best_at[:, j, n, :], best[:, j, n, :], scores[:, j % 2, n, :])
                ins.then_inc(listed, 1)

            def choose(kb, piece):
                def step(n, ins):
                    ins.then_inc(steps, 1)
                    stop_until(dve, steps, kb * CHOICE_STEPS + n)

                if piece == 0:
                    stop_until(dve, listed, 2 * XT * (kb + 1))
                    halves = best[:].rearrange("p j (h s) k -> p (j h) s k", s=2)
                    step(1, nc.vector.tensor_tensor(
                        pair[:], halves[:, :, 0, :].unsqueeze(3).to_broadcast([P, GROUPS, TOP, TOP]),
                        halves[:, :, 1, :].unsqueeze(2).to_broadcast([P, GROUPS, TOP, TOP]), ALU.add))
                elif piece == 1:
                    for g in range(GROUPS):
                        ins = nc.vector.max(top[:, g, :], pair[:, g].rearrange("p a b -> p (a b)"))
                    step(2, ins)
                elif piece == 2:
                    for g in range(GROUPS):
                        ins = nc.vector.max_index(top_at[:, g, :], top[:, g, :], pair[:, g].rearrange("p a b -> p (a b)"))
                    nc.vector.tensor_tensor(prob[:], top[:], top[:, :, 0:1].to_broadcast([P, GROUPS, TOP]),
                                            ALU.subtract).then_inc(diffs, 1)
                    step(3, ins)
                elif piece == 3:
                    nc.vector.tensor_scalar(digit[:, :, 0, :], top_at[:], 3, None, ALU.logical_shift_right)
                    step(4, nc.vector.tensor_scalar(digit[:, :, 1, :], top_at[:], 7, None, ALU.bitwise_and))
                    flat = digit[:].rearrange("p g s k -> p (g s k)")
                    step(5, nc.vector.tensor_tensor(pick, flat.unsqueeze(2).to_broadcast([P, 2 * GROUPS * TOP, TOP]),
                                                    digits[:].unsqueeze(1).to_broadcast([P, 2 * GROUPS * TOP, TOP]),
                                                    ALU.is_equal))
                elif piece == 4:
                    pick4 = pick.rearrange("p (l k) a -> p l k a", k=TOP)
                    at = best_at[:].rearrange("p j l a -> p (j l) a").unsqueeze(2).to_broadcast([P, 2 * GROUPS, TOP, TOP])
                    step(6, nc.vector.tensor_tensor(pick4, pick4, at, ALU.mult))
                elif piece == 5:
                    step(7, nc.vector.tensor_reduce(part[:].rearrange("p g s k -> p (g s k)"), pick, AX.X, ALU.add))
                elif piece == 6:
                    step(8, nc.vector.scalar_tensor_tensor(expert[:], part[:, :, 0, :], float(SUBKEYS),
                                                           part[:, :, 1, :], ALU.mult, ALU.add))
                    nc.vector.tensor_scalar(expert_at[:], expert[:].rearrange("p g k -> p (g k)"),
                                            float(EXPERTS - 1), None, ALU.min).then_inc(experts, 1)
                else:
                    dve.wait_ge(exps, kb + 1)
                    step(9, nc.vector.tensor_reduce(prob_sum[:], prob[:], AX.X, ALU.add))
                    step(10, nc.vector.reciprocal(prob_sum[:], prob_sum[:]))
                    step(11, nc.vector.tensor_tensor(
                        prob[:], prob[:], prob_sum[:].unsqueeze(2).to_broadcast([P, GROUPS, TOP]), ALU.mult))

            def combine(kb, u, quarter):
                n, done = u % 2, (HALVES * kb + u) * 3
                r = rows[:, n]
                if quarter == 0:
                    dve.wait_ge(gathered[n], 16 * HP * (HALVES // 2 * kb + u // 2 + 1))
                    nc.vector.tensor_tensor(prod[:].rearrange("p (k f) -> p k f", f=D_HIDDEN), r,
                                            proj[:, u // 2, :].unsqueeze(1).to_broadcast([P, HP, D_HIDDEN]),
                                            ALU.mult).then_inc(weighed, 1)
                elif quarter == 1:
                    dve.wait_ge(weighed, done + 1)
                    nc.vector.tensor_reduce(dots[:, n, :], prod[:].rearrange("p (k f) -> p k f", f=D_HIDDEN), AX.X,
                                            ALU.add).then_inc(dotted, 1)
                elif quarter == 2:
                    dve.wait_ge(gelued, HALVES * kb + u + 1)
                    w = prob[:].rearrange("p g k -> p (g k)")[:, u * HP:(u + 1) * HP]
                    nc.vector.tensor_tensor(dots[:, n, :], acts[:, n, :], w, ALU.mult).then_inc(weighed, 1)
                    dve.wait_ge(weighed, done + 2)
                    nc.vector.tensor_tensor(r, r, dots[:, n, :].unsqueeze(2).to_broadcast([P, HP, D_HIDDEN]),
                                            ALU.mult).then_inc(weighed, 1)
                else:
                    dve.wait_ge(weighed, done + 3)
                    nc.vector.tensor_reduce(acc[:, u % 4, :], r.rearrange("p k f -> p f k"), AX.X,
                                            ALU.add).then_inc(used, 1)

            def add_keys(o, b, kb, j):
                name = ("keys", j)
                wait_made(dve, o, b, name)
                x = x_res[:, kb, j, :]
                nc.vector.scalar_tensor_tensor(x, ps_m[o.bank(name)][:, 0:DIM], gate4[:], x, ALU.mult,
                                               ALU.add).then_inc(misc_out[o.bank(name)], 1)

            def route(o, b):
                def step(n, ins):
                    ins.then_inc(route_steps, 1)
                    stop_until(dve, route_steps, b * ROUTE_STEPS + n)

                name = ("router",)
                k = o.bank(name)
                wait_made(dve, o, b, name)
                nc.vector.tensor_copy(rs[:].rearrange("p j e -> p (j e)"), ps_m[k][:, 0:XT * MOE])\
                    .then_inc(misc_out[k], 1)
                stop_until(dve, misc_out[k], o.out(b, name))
                for j in range(XT):
                    ins = nc.vector.max(rs_top[:, j, :], rs[:, j, :])
                step(1, ins)
                for j in range(XT):
                    ins = nc.vector.max_index(rs_at[:, j, :], rs_top[:, j, :], rs[:, j, :])
                step(2, ins)
                every = digits[:].unsqueeze(1).to_broadcast([P, XT, MOE])
                nc.vector.tensor_tensor(gates[:], every, rs_at[:, :, 0:1].to_broadcast([P, XT, MOE]), ALU.is_equal)
                step(3, nc.vector.tensor_tensor(second[:], every, rs_at[:, :, 1:2].to_broadcast([P, XT, MOE]),
                                                ALU.is_equal))
                step(4, nc.vector.tensor_tensor(gates[:], gates[:], second[:], ALU.add))
                dve.wait_ge(sig_ready, b + 1)
                nc.vector.tensor_tensor(gates[:], gates[:], sig[:], ALU.mult).then_inc(gates_ready, 1)

            def gated(b, e):
                dve.wait_ge(gates_in[e % 2], 16 * (MOE // 2 * b + e // 2 + 1))
                nc.vector.tensor_tensor(xg[:, e % 2], xT[:], gates_all[:, e % 2, :].unsqueeze(1)
                                        .to_broadcast([P, DC, SEQ]), ALU.mult).then_inc(xg_ready, 1)

            def batch(b, o, before, b_before):
                keys = o is LOOP
                stop_until(dve, misc_out[before.bank(("keys", XT - 1))], before.out(b_before, ("keys", XT - 1)))
                norm.statistics(dve, 2 * b, b)
                norm.apply(dve, 2 * b, b)
                if keys:
                    for j in range(XT):
                        lists(o, b, b + 1, j)
                for n in range(KT // 2):
                    name = ("v", n)
                    wait_made(dve, o, b, name)
                    nc.vector.tensor_tensor(vp[:, 2 * n:2 * n + 2, :].rearrange("p t n -> p (t n)"),
                                            ps_m[o.bank(name)][:], bv[:].rearrange("p t n -> p (t n)"),
                                            ALU.add).then_inc(misc_out[o.bank(name)], 1)
                for kt in range(KT):
                    dve.wait_ge(s_ready, KT * b + kt + 1)
                    if kt >= LOGIT_SLOTS:
                        dve.wait_ge(av_ready, KT * b + kt - LOGIT_SLOTS + 1)
                    nc.vector.scalar_tensor_tensor(logits[:, kt % LOGIT_SLOTS, :], ps_a[kt % 2][:], 0.0,
                                                   maskT[:, kt, :], ALU.max, ALU.add).then_inc(s_out, 1)
                    if keys:
                        choose(b + 1, kt)
                dve.wait_ge(attn_out, b + 1)
                x = x_res[:, b].rearrange("p j n -> p (j n)")
                nc.vector.scalar_tensor_tensor(x, attn, gate[:, 1:2], x, ALU.mult, ALU.add).then_inc(x_done, 1)
                stop_until(dve, x_done, b + 1)
                norm.statistics(dve, 2 * b + 1, b)
                norm.apply(dve, 2 * b + 1, b)
                route(o, b)
                for n in range(BLOCKS + TAIL):
                    if n < BLOCKS:
                        e, f = divmod(n, FT)
                        if f == 2 and e < MOE:
                            gated(b, e)
                        dve.wait_ge(a_out, b * BLOCKS + n + 1)
                        if n >= 2:
                            dve.wait_ge(h_used, b * BLOCKS + n - 1)
                        nc.vector.tensor_tensor(hid[:, n % 2, :], act_in[:, n % 2, :], ps_b[n % 2][:],
                                                ALU.mult).then_inc(h_ready, 1)
                    elif n == BLOCKS:
                        dve.wait_ge(h_used, (b + 1) * BLOCKS)
                        nc.vector.scalar_tensor_tensor(x, ps_o[:].rearrange("p j n -> p (j n)"), gate[:, 3:4], x,
                                                       ALU.mult, ALU.add).then_inc(moe_out, 1)
                    if keys and (half := half_step(n)):
                        combine(b + 1, *half)
                    if keys and (j := tile_at(n, 2)) is not None:
                        add_keys(o, b, b + 1, j)

            for j in range(XT):
                lists(FIRST, 0, 0, j)
            for piece in range(8):
                choose(0, piece)
            for u in range(HALVES):
                for quarter in range(4):
                    combine(0, u, quarter)
                if u % 2:
                    add_keys(FIRST, 0, 0, u // 2)
            batch(0, LOOP, FIRST, 0)
            with dve.Fori(1, BATCH - 1) as b:
                batch(b, LOOP, LOOP, b - 1)
            batch(BATCH - 1, LAST, LOOP, BATCH - 2)

        @block.tensor
        def _(pe):
            pe.wait_ge(loaded, 16 * N_LOADS)

            def make(o, b, name, kb=None):
                kind, k = name[0], o.bank(name)
                pe.wait_ge(misc_out[k], o.free(b, name))
                out = ps_m[k]
                if kind == "s":
                    _, j, c = name
                    if (j, c) == (0, 0):
                        pe.wait_ge(qn_ready, QC * (kb + 1))
                    ins = nc.tensor.matmul(out[:], qn[:, c, j * P:(j + 1) * P], subkeys[:], start=True, stop=True)
                elif kind == "accT":
                    j = name[1]
                    pe.wait_ge(used, HALVES * kb + 2 * j + 2)
                    for h in range(2):
                        ins = nc.tensor.matmul(out[:, 0:P], acc[:, (2 * j + h) % 4, :], ident[:], start=h == 0,
                                               stop=h == 1)
                elif kind == "keys":
                    j = name[1]
                    wait_out(pe, o, b, ("accT", j))
                    ins = nc.tensor.matmul(out[:, 0:DIM], accT[:, j % 2, :], wkeys[:], start=True, stop=True)
                elif kind == "xT":
                    for j in range(XT):
                        ins = nc.tensor.transpose(out[:, j * P:(j + 1) * P],
                                                  norm.out[:, j, name[2] * P:(name[2] + 1) * P], ident[:])
                elif kind == "k":
                    _, m, h = name
                    for c in range(DC):
                        ins = nc.tensor.matmul(out[:], wk[:, c, m * P:(m + 1) * P], ctxT[:, c, h * HALF:(h + 1) * HALF],
                                               start=c == 0, stop=c == DC - 1)
                elif kind == "q":
                    m = name[1]
                    for c in range(DC):
                        ins = nc.tensor.matmul(out[:], wq[:, c, m * P:(m + 1) * P], xT[:, c, :], start=c == 0,
                                               stop=c == DC - 1)
                elif kind == "v":
                    for t in range(2):
                        kt = 2 * name[1] + t
                        for c in range(DC):
                            ins = nc.tensor.matmul(out[:, t * DIM:(t + 1) * DIM], ctxT[:, c, kt * P:(kt + 1) * P],
                                                   wv[:, c, :], start=c == 0, stop=c == DC - 1)
                elif kind == "router":
                    for j in range(XT):
                        for c in range(DC):
                            ins = nc.tensor.matmul(out[:, j * MOE:(j + 1) * MOE], xT[:, c, j * P:(j + 1) * P],
                                                   router[:, c, :], start=c == 0, stop=c == DC - 1)
                else:
                    pe.wait_ge(gates_ready, b + 1)
                    for j in range(XT):
                        ins = nc.tensor.transpose(out[0:MOE, j * P:(j + 1) * P], gates[:, j, :], ident[:])
                ins.then_inc(misc_made, 1)

            def summed(lhsT, rhs, n, last):
                for j in range(XT):
                    ins = nc.tensor.matmul(ps_o[:, j, :], lhsT(j), rhs, start=n == 0 and j % 2 == 0, stop=n == last,
                                           skip_group_check=True)
                return ins

            def expert_products(b, n):
                e, f = divmod(n, FT)
                slot = 2 if e == 0 else (e - 1) % 2
                if f == 0 and e >= 1:
                    pe.wait_ge(expert_in[slot], 48 * (MOE // 2 * b + (e - 1) // 2 + 1))
                    pe.wait_ge(xg_ready, MOE * b + e)
                if n >= 2:
                    pe.wait_ge(h_ready, b * BLOCKS + n - 1)
                src = xT[:] if e == 0 else xg[:, slot]
                for w, out in ((w_in, ps_a[n % 2]), (w_sw, ps_b[n % 2])):
                    for c in range(DC):
                        ins = nc.tensor.matmul(out[:], w[:, slot, c, f * P:(f + 1) * P], src[:, c, :], start=c == 0,
                                               stop=c == DC - 1)
                ins.then_inc(a_ready, 1)

            def expert_sums(b, n):
                e, f = divmod(n, FT)
                slot = 2 if e == 0 else (e - 1) % 2
                pe.wait_ge(h_ready, b * BLOCKS + n + 1)
                summed(lambda j: hid[:, n % 2, j * P:(j + 1) * P], w_out[:, slot, f, :], n,
                       BLOCKS - 1).then_inc(h_used, 1)

            def batch(b, o):
                keys = o is LOOP
                for name in o.names[:o.no[("xT", 1, 0)]]:
                    if name == ("xT", 0, 0):
                        pe.wait_ge(norm.ready, 2 * b + 1)
                    if name == ("k", 0, 0):
                        pe.wait_ge(ctx_loaded, 16 * (b + 1))
                    if name[0] == "q":
                        wait_out(pe, o, b, ("k", DC - 1, o.bank(name)))
                    make(o, b, name, b + 1)
                for kt in range(KT + 1):
                    if kt < KT:
                        if kt >= 2:
                            pe.wait_ge(s_out, KT * b + kt - 1)
                        for c in range(DC):
                            ins = nc.tensor.matmul(ps_a[kt % 2][:], kp[:, c, kt * P:(kt + 1) * P], qp[:, c, :],
                                                   start=c == 0, stop=c == DC - 1)
                        ins.then_inc(s_ready, 1)
                    if kt >= 1:
                        k = kt - 1
                        pe.wait_ge(relued, KT // 2 * b + k // 2 + 1)
                        pe.wait_ge(s_out, KT * b + k + 1)
                        summed(lambda j: logits[:, k % LOGIT_SLOTS, j * P:(j + 1) * P], vp[:, k, :], k,
                               KT - 1).then_inc(av_ready, 1)
                pe.wait_ge(norm.ready, 2 * b + 2)
                for c in range(DC):
                    make(o, b, ("xT", 1, c))
                for c in range(DC):
                    wait_out(pe, o, b, ("xT", 1, c))
                make(o, b, ("router",))
                for n in range(BLOCKS + TAIL):
                    if n == FT - 1:
                        make(o, b, ("gatesT",))
                    if n < BLOCKS:
                        expert_products(b, n)
                    if 1 <= n <= BLOCKS:
                        expert_sums(b, n - 1)
                    if keys and (j := tile_at(n, 1)) is not None:
                        make(o, b, ("accT", j), b + 1)
                    if keys and (j := tile_at(n, 2)) is not None:
                        make(o, b, ("keys", j))

            for name in FIRST.names:
                make(FIRST, 0, name, 0)
            with pe.Fori(0, BATCH - 1) as b:
                batch(b, LOOP)
            batch(BATCH - 1, LAST)


def program(nc, d):
    with ExitStack() as ctx:
        def sem(name):
            return ctx.enter_context(nc.semaphore(name))

        d["table"] = nc.dram_tensor("hidden_table", [EXPERTS, D_HIDDEN], F32).ap()
        d["q_dram"] = nc.dram_tensor("keys_queries", [BATCH, P, QC, SEQ], F32).ap()
        d["proj_dram"] = nc.dram_tensor("keys_projections", [BATCH, P, XT, D_HIDDEN], F32).ap()
        d["gates_dram"] = nc.dram_tensor("gates_by_expert", [MOE, SEQ], F32).ap()
        sh = Shared(nc, ctx)
        rope_attention(nc, sh, d)
        ks = KeyState(nc, ctx)
        key_queries(nc, sh, ks, d, sem)
        keys_and_layer1(nc, sh, ks, d, sem)



def tokens(a):
    b, s, f = a.shape
    return np.ascontiguousarray(a.reshape(b, s // P, P, f).transpose(0, 2, 1, 3))


def columns(a):
    return np.ascontiguousarray(a.reshape(-1, P).T)


def layout(a):
    x0, f0, x1, f1 = "L0_xattn_", "L0_ffn_", "L1_xattn_", "L1_ffn_"
    w2 = a[f0 + "W2"]
    ctx = a["ctx_1024"]
    return {
        "x": tokens(a["x"]),
        "ctx": tokens(ctx),
        "ctxT": ctx.transpose(0, 2, 1).reshape(BATCH, DC, P, CTX).transpose(0, 2, 1, 3),
        "gates": np.concatenate([a["g_xattn"], a["g_ffn"]])[None, :],
        "wq": a[x0 + "Wq"], "wkv": a[x0 + "Wkv"], "wo": a[x0 + "Wo"], "bo": a[x0 + "bo"][None, :],
        "cosT": np.tile(a[x0 + "cos"].T, (P // (DHEAD // 2), 1)),
        "sinT": np.tile(a[x0 + "sin"].T, (P // (DHEAD // 2), 1)),
        "lat_g": columns(a[x0 + "ln_lat_g"]), "lat_b": columns(a[x0 + "ln_lat_b"]),
        "ctx_g": columns(a[x0 + "ln_ctx_g"]), "ctx_b": columns(a[x0 + "ln_ctx_b"]),
        "keys_wqT": a[f0 + "Wq"].reshape(QC * P, DIM).T,
        "keys_bq": columns(a[f0 + "bq"]), "keys_gamma": columns(a[f0 + "gamma"]),
        "keys_beta": columns(a[f0 + "beta"]),
        "sk1T": a[f0 + "sk1"].T, "sk2T": a[f0 + "sk2"].T,
        "latentsT": a[f0 + "latents"].T, "w1": a[f0 + "W1"],
        "w2xT": w2[:, :DIM].T, "w2v": w2[:, DIM:],
        "l1_wq": a[x1 + "kernel_q"][0, 0], "l1_wk": a[x1 + "kernel_k"][0, 0], "l1_wv": a[x1 + "kernel_v"][0, 0],
        "l1_bq": columns(a[x1 + "bias_q"]), "l1_bk": columns(a[x1 + "bias_k"]), "l1_bv": a[x1 + "bias_v"][None, :],
        "maskT": a["mask_1xSxS2_ff0"][0].T,
        "router": a[f1 + "router_DE"],
        "w_in_shared": a[f1 + "w_in_shared_FD"].T, "w_sw_shared": a[f1 + "w_swiglu_FD"].T,
        "w_out_shared": a[f1 + "w_out_shared_DF"].T,
        "w_in": a[f1 + "w_in_eDF"], "w_sw": a[f1 + "w_swiglu_eDF"], "w_out": a[f1 + "w_out_eFD"],
    }


def kernel(**inputs):
    import concourse.bacc as bacc
    from concourse.bass_utils import run_bass_kernel_spmd

    nc = bacc.Bacc("TRN2", target_bir_lowering=False, num_devices=1)
    arrays, d = {}, {}
    for name, a in layout({k: np.asarray(v) for k, v in inputs.items()}).items():
        a = np.ascontiguousarray(a)
        arrays["in_" + name] = a
        d[name] = nc.dram_tensor("in_" + name, a.shape, mybir.dt.from_np(a.dtype), kind="ExternalInput").ap()
    d["out"] = nc.dram_tensor("out", (BATCH, P, XT, DIM), F32, kind="ExternalOutput").ap()
    program(nc, d)
    out = run_bass_kernel_spmd(nc, [arrays], core_ids=[0]).results[0]["out"]
    return np.ascontiguousarray(out.transpose(0, 2, 1, 3)).reshape(BATCH, SEQ, DIM)
```

```python
from contextlib import ExitStack

import numpy as np

import concourse.bass as bass
import concourse.mybir as mybir
from concourse.alu_op_type import AluOpType as ALU

F32 = mybir.dt.float32
U32 = mybir.dt.uint32
F32R = mybir.dt.float32r
ACT = mybir.ActivationFunctionType
AX = mybir.AxisListType

P = 128
BATCH, SEQ, DIM, CTX = 8, 512, 256, 1024
HEADS, DHEAD = 16, 64
INNER = HEADS * DHEAD
DC = DIM // P
XT = SEQ // P
KT = CTX // P
PAIRS = HEADS // 2
HALF = 512
EPS = 1e-5
CLIP, SCALE = 11.0, DHEAD ** -0.5


class Shared:

    def __init__(self, nc, ctx):
        self.gate = ctx.enter_context(nc.sbuf_tensor("gate", [P, 4], F32))
        self.ident = ctx.enter_context(nc.sbuf_tensor("ident", [P, P], F32))
        self.eps = ctx.enter_context(nc.sbuf_tensor("epsilon", [P, 16], F32))
        self.mhalf = ctx.enter_context(nc.sbuf_tensor("minus_half", [P, 16], F32))



UNITS = PAIRS * KT
SCORE_SLOTS, PROB_SLOTS = 2, 4
ADD_LAG = 2
AV_LAG = 2
POOL_TILES = 5
DEN_AT, K_AT, V_AT = 2, 6, (5, 7)
RECIP_AT = (3, 4, 5, 6)
K_HI_AT, K_LO_AT = (2, 1), (2, 1)


def attention_extras(i):
    t, kt = divmod(i, KT)
    out = []
    if t + 2 < PAIRS and kt == K_AT:
        out += [("k", t + 2, h) for h in range(2)]
    if t + 1 < PAIRS and kt == 2:
        out.append(("q", t + 1))
    if kt == DEN_AT and t >= 1:
        out.append(("den", t - 1))
    if t < 4 and kt in V_AT:
        out.append(("v", 2 * t + V_AT.index(kt), 1))
    return out


def attention_lead(i):
    return {UNITS - 4: [("ctxT", 0, 0)], UNITS - 3: [("ctxT", 1, 0), ("ctxT", 0, 1)],
            UNITS - 2: [("ctxT", 1, 1), ("latT", 0), ("latT", 1)],
            UNITS - 1: [("k", 0, 0), ("k", 0, 1), ("q", 0)]}.get(i, [])


LEAD_V = [("v", kt, 0) for kt in range(KT)]
BOUNDARY = LEAD_V[:3] + [("den", PAIRS - 1)] + LEAD_V[3:] + [("o", m) for m in range(XT // 2)]
BOUNDARY += [("k", 1, h) for h in range(2)]
BATCH_TAIL = [("den", PAIRS - 1)] + [("o", m) for m in range(XT // 2)]


def attention_misc():
    order = [name for i in range(UNITS) for name in attention_lead(i)] + BOUNDARY
    order += [name for i in range(UNITS) for name in attention_extras(i)]
    assert len(order) % 2 == 0
    return {name: n for n, name in enumerate(order)}


def rope_attention(nc, sh, d):
    MISC = attention_misc()
    NM = len(MISC)
    with ExitStack() as ctx:
        def sb(name, shape, dtype=F32):
            return ctx.enter_context(nc.sbuf_tensor("s1_" + name, shape, dtype))

        def sem(name):
            return ctx.enter_context(nc.semaphore(name))

        gate, ident, mhalf, eps = sh.gate, sh.ident, sh.mhalf, sh.eps
        wq, wkv, wo = sb("wq", [P, DC, INNER]), sb("wkv", [P, DC, 2 * INNER]), sb("wo", [P, PAIRS, DIM])
        cosT, sinT = sb("cosT", [P, CTX]), sb("sinT", [P, CTX])
        affine = sb("affine", [P, 4, DC])
        bo = sb("bo", [P, DIM])
        context = sb("context", [P, KT, DIM])
        ctxT = sb("ctxT", [P, DC, CTX])
        x_in, x_acc = sb("x_in", [P, XT, DIM]), sb("x_acc", [P, XT, DIM])
        lat, latT = sb("lat", [P, XT, DIM]), sb("latT", [P, DC, SEQ])
        v = sb("v", [P, KT, INNER])
        kraw, kswap, krope = sb("kraw", [P, CTX]), sb("kswap", [P, CTX]), sb("krope", [P, CTX])
        ksplit = sb("k_split", [P, 2, 2, CTX], F32R)
        klo = sb("k_lo", [P, CTX], F32R)
        qsplit = sb("q_split", [P, 2, 2, 2, SEQ], F32R)
        probs = sb("probs", [P, PROB_SLOTS, 2 * SEQ])
        pool_sum, psum = sb("pool_prob_sum", [P, 2 * SEQ]), sb("prob_sum", [P, 2 * SEQ])
        ones = sb("ones", [P, DHEAD])
        recip = sb("recip", [P, SEQ])
        oT = sb("oT", [P, PAIRS, SEQ])
        cst = sb("ctx_stats_sb", [P, KT, 6])
        cmv = sb("ctx_meanvar", [P, KT, 2])
        crs = sb("ctx_rstd_sb", [P, KT])
        xst = sb("x_stats_sb", [P, XT, 6])
        xmv = sb("x_meanvar", [P, XT, 2])
        xrs = sb("x_rstd_sb", [P, XT])

        ps_s = [ctx.enter_context(nc.psum_tensor(f"ps_scores{i}", [P, 2 * SEQ], F32)) for i in range(SCORE_SLOTS)]
        ps_av = [ctx.enter_context(nc.psum_tensor(f"ps_av{i}", [P, SEQ], F32)) for i in range(2)]
        ps_m = [ctx.enter_context(nc.psum_tensor(f"ps_misc{i}", [P, HALF], F32)) for i in range(2)]

        loaded = sem("weights_loaded")
        gates_in = sem("gates_in")
        zeroed = sem("pool_constants")
        ident_ready = sem("ident_ready")
        gates_ready = sem("gates_ready")
        tables_ready = sem("tables_ready")
        ctx_loaded, x_loaded = sem("ctx_loaded"), sem("x_loaded")
        ctx_stats, ctx_eps, ctx_rstd = sem("ctx_stats"), sem("ctx_eps"), sem("ctx_rstd")
        ctx_normed = sem("ctx_normed")
        x_sums, x_eps, x_rstd = sem("x_stats"), sem("x_eps"), sem("x_rstd")
        x_normed = sem("x_normed")
        x_biased = sem("x_biased")
        x_stored = sem("x_stored")
        prep_seq = sem("prep_seq")
        misc_ready = sem("misc_ready")
        misc_evicted = [sem("misc_evicted0"), sem("misc_evicted1")]
        kswap_ready = sem("kswap_ready")
        rope_parts = sem("rope_parts")
        krope_ready = sem("krope_ready")
        k_hi_ready = sem("k_hi_ready")
        k_second_ready = sem("k_second_ready")
        k_lo_ready = sem("k_lo_ready")
        k_stacked = sem("k_stacked")
        q_hi_ready = sem("q_hi_ready")
        q_second, q_first = sem("q_second_head"), sem("q_first_head")
        scores_ready = sem("scores_ready")
        clipped = sem("scores_clipped")
        exp_done = sem("exp_done")
        pool_added = sem("pool_probs_added")
        added = sem("probs_added")
        probs_used = sem("probs_used")
        inverted = sem("inverted")
        recip_ready = sem("recip_ready")
        passed = sem("waits_passed")

        block = ctx.enter_context(nc.Block())
        N_LOADS = 10
        MB = NM // 2

        def stop_until(eng, s, value):
            eng.wait_ge(s, value)
            eng.sem_inc(passed, 1)

        def made(b, name):
            return (b + (name in BATCH_TAIL)) * NM + MISC[name] + 1

        def wait_evicted(eng, b, name):
            n = MISC[name]
            eng.wait_ge(misc_evicted[n % 2], (b + (name in BATCH_TAIL)) * MB + n // 2 + 2)

        def added_count(b, i):
            t, kt = divmod(i, KT)
            if kt < POOL_TILES:
                return pool_added, (b * PAIRS + t) * POOL_TILES + kt + 1
            return added, (b * PAIRS + t) * (KT - POOL_TILES) + kt - POOL_TILES + 1

        @block.sync
        def _(sp):
            sp.dma_start(wkv[:], d["wkv"].rearrange("(c p) n -> p c n", p=P)).then_inc(loaded, 16)
            for n, name in enumerate(("lat_g", "lat_b", "ctx_g", "ctx_b")):
                sp.dma_start(affine[:, n, :], d[name]).then_inc(loaded, 16)
            sp.dma_start(wq[:], d["wq"].rearrange("(c p) n -> p c n", p=P)).then_inc(loaded, 16)
            sp.dma_start(cosT[:], d["cosT"]).then_inc(loaded, 16)
            sp.dma_start(sinT[:], d["sinT"]).then_inc(loaded, 16)
            sp.dma_start(wo[:], d["wo"].rearrange("(t p) n -> p t n", p=P)).then_inc(loaded, 16)
            sp.dma_start(bo[:], d["bo"].to_broadcast([P, DIM])).then_inc(loaded, 16)

            def pair(b, t):
                g = b * PAIRS + t
                for h in range(2):
                    wait_evicted(sp, b, ("k", t, h))
                    sp.sem_inc(passed, 1)
                for q in range(4):
                    sp.dma_start(kswap[32 * q:32 * q + 32, :],
                                 kraw[32 * (q ^ 1):32 * (q ^ 1) + 32, :]).then_inc(kswap_ready, 16)
                wait_evicted(sp, b, ("q", t))
                sp.sem_inc(passed, 1)
                slot = qsplit[:, t % 2].bitcast(F32)
                for half in range(2):
                    sp.dma_start(slot[DHEAD * half:DHEAD * (half + 1), 1], slot[DHEAD:P, 0]).then_inc(q_second, 16)
                sp.wait_ge(k_lo_ready, g + 1)
                sp.sem_inc(passed, 1)
                kslot, lo = ksplit[:, t % 2].bitcast(F32), klo[:].bitcast(F32)
                sp.dma_start(kslot[DHEAD:P, 0], lo[0:DHEAD]).then_inc(k_stacked, 16)
                sp.dma_start(kslot[0:DHEAD, 1], lo[DHEAD:P]).then_inc(k_stacked, 16)
                sp.wait_ge(q_second, 32 * (g + 1))
                sp.sem_inc(passed, 1)
                sp.dma_start(slot[DHEAD:P, 0], slot[0:DHEAD, 0]).then_inc(q_first, 16)

            def store(b):
                for m in range(XT // 2):
                    wait_evicted(sp, b, ("o", m))
                    sp.sem_inc(passed, 1)
                sp.dma_start(d["x_dram"][b], x_acc[:]).then_inc(x_stored, 16)

            pair(0, 0)
            with sp.Fori(0, BATCH - 1) as b:
                for t in range(1, PAIRS):
                    pair(b, t)
                pair(b + 1, 0)
                store(b)
            for t in range(1, PAIRS):
                pair(BATCH - 1, t)
            store(BATCH - 1)
            sp.wait_ge(x_stored, 16 * (BATCH + 1))

        @block.gpsimd
        def _(pool):
            pool.sem_inc(x_stored, 16)
            nc.gpsimd.dma_start(context[:], d["ctx"][0]).then_inc(ctx_loaded, 16)
            nc.gpsimd.dma_start(x_in[:], d["x"][0]).then_inc(x_loaded, 16)
            nc.gpsimd.memset(ident[:], 0.0).then_inc(zeroed, 1)
            nc.gpsimd.memset(eps[:], EPS).then_inc(zeroed, 1)
            nc.gpsimd.memset(mhalf[:], -0.5).then_inc(zeroed, 1)
            pool.wait_ge(zeroed, 3)
            nc.gpsimd.affine_select(out=ident[:], in_=ident[:], compare_op=ALU.not_equal, fill=1.0, base=0,
                                    pattern=[[-1, P]], channel_multiplier=1).then_inc(ident_ready, 1)

            def ctx_power(b):
                pool.wait_ge(ctx_stats, b + 1)
                nc.gpsimd.tensor_tensor(crs[:], cmv[:, :, 1], eps[:, 0:KT], ALU.add).then_inc(ctx_eps, 1)
                pool.wait_ge(ctx_eps, b + 1)
                nc.gpsimd.tensor_tensor(crs[:], crs[:], mhalf[:, 0:KT], ALU.pow).then_inc(ctx_rstd, 1)

            def x_power(b, n):
                pool.wait_ge(x_sums, 2 * b + n + 1)
                nc.gpsimd.tensor_tensor(xrs[:], xmv[:, :, 1], eps[:, 0:XT], ALU.add).then_inc(x_eps, 1)
                pool.wait_ge(x_eps, 2 * b + n + 1)
                nc.gpsimd.tensor_tensor(xrs[:], xrs[:], mhalf[:, 0:XT], ALU.pow).then_inc(x_rstd, 1)

            def rope_cos(b, t):
                for h in range(2):
                    wait_evicted(pool, b, ("k", t, h))
                nc.gpsimd.tensor_tensor(krope[:], kraw[:], cosT[:], ALU.mult).then_inc(rope_parts, 1)

            def rope_sin(b, t):
                pool.wait_ge(kswap_ready, 64 * (b * PAIRS + t + 1))
                nc.gpsimd.tensor_tensor(kswap[:], kswap[:], sinT[:], ALU.mult).then_inc(rope_parts, 1)
                pool.wait_ge(rope_parts, 2 * (b * PAIRS + t + 1))
                nc.gpsimd.tensor_tensor(krope[:], krope[:], kswap[:], ALU.add).then_inc(krope_ready, 1)

            def k_lo(b, t):
                pool.wait_ge(k_hi_ready, b * PAIRS + t + 1)
                nc.gpsimd.tensor_tensor(klo[:], krope[:], ksplit[:, t % 2, 0, :], ALU.subtract).then_inc(k_lo_ready, 1)

            def add(b, t, kt):
                count = (b * PAIRS + t) * POOL_TILES
                p = probs[:, (t * KT + kt) % PROB_SLOTS, :]
                pool.wait_ge(exp_done, b * UNITS + t * KT + kt + 1)
                if kt == 1:
                    if t >= 1:
                        pool.wait_ge(added, (b * PAIRS + t - 1) * (KT - POOL_TILES) + 1)
                    nc.gpsimd.tensor_tensor(pool_sum[:], probs[:, t * KT % PROB_SLOTS, :], p, ALU.add)\
                        .then_inc(pool_added, 2)
                else:
                    pool.wait_ge(pool_added, count + kt)
                    nc.gpsimd.tensor_tensor(pool_sum[:], pool_sum[:], p, ALU.add).then_inc(pool_added, 1)

            def batch(b, last):
                if not last:
                    stop_until(pool, misc_ready, made(b, ("ctxT", 1, 1)))
                    nc.gpsimd.dma_start(context[:], d["ctx"][b + 1]).then_inc(ctx_loaded, 16)
                for t in range(PAIRS):
                    for kt in range(1, POOL_TILES):
                        add(b, t, kt)
                        if kt == K_LO_AT[t > 0] and t + 1 < PAIRS:
                            k_lo(b, t + 1)
                    if t + 2 < PAIRS:
                        rope_cos(b, t + 2)
                        rope_sin(b, t + 2)
                    if t == 0:
                        pool.wait_ge(x_stored, 16 * b + 16)
                        pool.wait_ge(x_normed, 2 * b + 1)
                        for j in range(XT):
                            ins = nc.gpsimd.tensor_tensor(x_acc[:, j, :], x_in[:, j, :], bo[:], ALU.add)
                        ins.then_inc(x_biased, 1)
                        if not last:
                            stop_until(pool, x_biased, b + 1)
                            nc.gpsimd.dma_start(x_in[:], d["x"][b + 1]).then_inc(x_loaded, 16)
                    if not last:
                        if t == 1:
                            ctx_power(b + 1)
                        elif t == 2:
                            x_power(b + 1, 0)
                        elif t == 4:
                            x_power(b + 1, 1)
                if not last:
                    for t in range(2):
                        rope_cos(b + 1, t)
                        rope_sin(b + 1, t)
                        if t == 0:
                            k_lo(b + 1, 0)

            ctx_power(0)
            x_power(0, 0)
            x_power(0, 1)
            pool.wait_ge(tables_ready, 1)
            for t in range(2):
                rope_cos(0, t)
                rope_sin(0, t)
                if t == 0:
                    k_lo(0, 0)
            with pool.Fori(0, BATCH - 1) as b:
                batch(b, False)
            batch(BATCH - 1, True)

        @block.scalar
        def _(act):
            nc.scalar.dma_start(gate[:], d["gates"].to_broadcast([P, 4])).then_inc(gates_in, 16)
            act.wait_ge(gates_in, 16)
            nc.scalar.activation(gate[:], gate[:], ACT.Tanh).then_inc(gates_ready, 1)
            act.wait_ge(loaded, 16 * N_LOADS)

            def evict(b, name):
                n = MISC[name]
                act.wait_ge(misc_ready, made(b, name))
                src, kind = ps_m[n % 2], name[0]
                if kind == "ctxT":
                    _, c, h = name
                    ins = nc.scalar.activation(ctxT[:, c, h * HALF:(h + 1) * HALF], src[:], ACT.Identity,
                                               scale=affine[:, 2, c:c + 1], bias=affine[:, 3, c:c + 1])
                elif kind == "latT":
                    c = name[1]
                    ins = nc.scalar.activation(latT[:, c, :], src[:], ACT.Identity,
                                               scale=affine[:, 0, c:c + 1], bias=affine[:, 1, c:c + 1])
                elif kind == "v":
                    _, kt, h = name
                    ins = nc.scalar.copy(v[:, kt, h * HALF:(h + 1) * HALF], src[:])
                elif kind == "den":
                    t = name[1]
                    if t >= 1:
                        act.wait_ge(recip_ready, b * PAIRS + t)
                    ins = nc.scalar.copy(recip[:], src[:])
                elif kind == "k":
                    ins = nc.scalar.copy(kraw[:, name[2] * HALF:(name[2] + 1) * HALF], src[:])
                else:
                    nc.scalar.copy(qsplit[:, name[1] % 2, 0, 0, :], src[:]).then_inc(q_hi_ready, 1)
                    return
                ins.then_inc(misc_evicted[n % 2], 1)

            def k_hi(b, t):
                act.wait_ge(krope_ready, b * PAIRS + t + 1)
                nc.scalar.copy(ksplit[:, t % 2, 0, :], krope[:]).then_inc(k_hi_ready, 1)
                nc.scalar.copy(ksplit[DHEAD:P, t % 2, 1, :], krope[DHEAD:P, :]).then_inc(k_second_ready, 1)

            def boundary(b, first=False):
                for name in BOUNDARY:
                    if name[0] == "den" and not first:
                        evict(b - 1, name)
                    if name == ("k", 1, 0):
                        act.wait_ge(k_lo_ready, b * PAIRS + 1)
                    if name not in BATCH_TAIL:
                        evict(b, name)
                    if name == LEAD_V[-1]:
                        k_hi(b, 0)

            def batch(b, last):
                for i in range(UNITS):
                    t, kt = divmod(i, KT)
                    act.wait_ge(clipped, b * UNITS + i + 1)
                    p = probs[:, i % PROB_SLOTS, :]
                    nc.scalar.activation(p, p, ACT.Exp, scale=SCALE).then_inc(exp_done, 1)
                    for name in attention_extras(i):
                        if name[0] == "k":
                            act.wait_ge(k_lo_ready, b * PAIRS + t + 2)
                        evict(b, name)
                    if t + 1 < PAIRS and kt == K_HI_AT[t > 0]:
                        k_hi(b, t + 1)
                    if not last:
                        for name in attention_lead(i):
                            if name[0] == "k":
                                act.wait_ge(k_lo_ready, (b + 1) * PAIRS)
                            evict(b + 1, name)
                if last:
                    evict(b, ("den", PAIRS - 1))
                else:
                    boundary(b + 1)

            for i in range(UNITS):
                for name in attention_lead(i):
                    evict(0, name)
            boundary(0, first=True)
            with act.Fori(0, BATCH - 1) as b:
                batch(b, False)
            batch(BATCH - 1, True)

        @block.vector
        def _(dve):
            for s in misc_evicted:
                dve.sem_inc(s, 1)
            nc.vector.memset(ones[:], 1.0)

            def ctx_tile_stats(b, kt):
                if kt == 0:
                    dve.wait_ge(ctx_loaded, 16 * b + 16)
                nc.vector.bn_stats(cst[:, kt, :], context[:, kt, :]).then_inc(prep_seq, 1)
                if kt == KT - 1:
                    stop_until(dve, prep_seq, b * PREP + KT)
                    for k in range(KT):
                        ins = nc.vector.bn_aggr(cmv[:, k, :], cst[:, k, :])
                    ins.then_inc(ctx_stats, 1)

            def ctx_tile_norm(b, kt):
                if kt == 0:
                    dve.wait_ge(ctx_rstd, b + 1)
                ins = nc.vector.tensor_scalar(context[:, kt, :], context[:, kt, :], cmv[:, kt, 0:1],
                                              crs[:, kt:kt + 1], ALU.subtract, ALU.mult)
                if kt == KT - 1:
                    ins.then_inc(ctx_normed, 1)

            def x_stats(b, n):
                if n == 0:
                    dve.wait_ge(x_loaded, 16 * b + 16)
                for j in range(XT):
                    src = lat[:, j, :] if n else x_in[:, j, :]
                    nc.vector.bn_stats(xst[:, j, :], src).then_inc(prep_seq, 1)
                stop_until(dve, prep_seq, b * PREP + KT + (n + 1) * XT)
                for j in range(XT):
                    ins = nc.vector.bn_aggr(xmv[:, j, :], xst[:, j, :])
                ins.then_inc(x_sums, 1)

            def x_norm(b, n):
                dve.wait_ge(x_rstd, 2 * b + n + 1)
                for j in range(XT):
                    src = lat[:, j, :] if n else x_in[:, j, :]
                    ins = nc.vector.tensor_scalar(lat[:, j, :], src, xmv[:, j, 0:1], xrs[:, j:j + 1],
                                                  ALU.subtract, ALU.mult)
                ins.then_inc(x_normed, 1)

            PREP = KT + 2 * XT

            def prepare_slot(b, i):
                t, kt = divmod(i, KT)
                if t == 1:
                    ctx_tile_stats(b, kt)
                elif t == 3:
                    ctx_tile_norm(b, kt)
                elif (t, kt) == (2, 2):
                    x_stats(b, 0)
                elif (t, kt) == (4, 2):
                    x_norm(b, 0)
                elif (t, kt) == (4, 6):
                    dve.wait_ge(x_normed, 2 * b + 1)
                    x_stats(b, 1)
                elif (t, kt) == (6, 1):
                    x_norm(b, 1)

            def q_lo(b, t):
                n = MISC[("q", t)]
                dve.wait_ge(q_hi_ready, b * PAIRS + t + 1)
                slot = qsplit[:, t % 2, 0]
                nc.vector.tensor_tensor(slot[:, 1, :], ps_m[n % 2][:], slot[:, 0, :],
                                        ALU.subtract).then_inc(misc_evicted[n % 2], 1)

            def add(b, i):
                t, kt = divmod(i, KT)
                if kt < POOL_TILES:
                    return
                first = kt == POOL_TILES
                dve.wait_ge(exp_done, b * UNITS + i + 1)
                dve.wait_ge(*added_count(b, i - 1))
                nc.vector.tensor_tensor(psum[:], pool_sum[:] if first else psum[:],
                                        probs[:, i % PROB_SLOTS, :], ALU.add).then_inc(added, 1)

            def reciprocals(b, t, part):
                n = SEQ // len(RECIP_AT)
                c = slice(n * part, n * (part + 1))
                if part == 0:
                    wait_evicted(dve, b, ("den", t))
                ins = nc.vector.reciprocal(recip[:, c], recip[:, c])
                if part == len(RECIP_AT) - 1:
                    ins.then_inc(inverted, 1)

            def normalise(b, t):
                dve.wait_ge(inverted, b * PAIRS + t + 1)
                dve.wait_ge(probs_used, b * UNITS + (t + 1) * KT)
                nc.vector.tensor_tensor(oT[:, t, :], ps_av[t % 2][:], recip[:], ALU.mult).then_inc(recip_ready, 1)

            def batch(b, last):
                for i in range(UNITS + ADD_LAG):
                    t, kt = divmod(i, KT)
                    if i < UNITS:
                        dve.wait_ge(scores_ready, b * UNITS + i + 1)
                        if i >= PROB_SLOTS:
                            dve.wait_ge(probs_used, b * UNITS + i - PROB_SLOTS + 1)
                            dve.wait_ge(*added_count(b, i - PROB_SLOTS))
                        nc.vector.tensor_scalar(probs[:, i % PROB_SLOTS, :], ps_s[i % SCORE_SLOTS][:],
                                                CLIP / SCALE, -CLIP / SCALE, ALU.min, ALU.max).then_inc(clipped, 1)
                    if i >= ADD_LAG:
                        add(b, i - ADD_LAG)
                    if i < UNITS and t + 1 < PAIRS and kt == 3:
                        q_lo(b, t + 1)
                    if i < UNITS and t >= 1:
                        if kt in RECIP_AT:
                            reciprocals(b, t - 1, RECIP_AT.index(kt))
                        if kt == 7:
                            normalise(b, t - 1)
                    if i < UNITS and not last:
                        prepare_slot(b + 1, i)
                if not last:
                    q_lo(b + 1, 0)
                for part in range(len(RECIP_AT)):
                    reciprocals(b, PAIRS - 1, part)
                normalise(b, PAIRS - 1)
                dve.wait_ge(x_biased, b + 1)
                for m in range(XT // 2):
                    n = MISC[("o", m)]
                    dve.wait_ge(misc_ready, made(b, ("o", m)))
                    x = x_acc[:, 2 * m:2 * m + 2, :].rearrange("p j n -> p (j n)")
                    nc.vector.scalar_tensor_tensor(x, ps_m[n % 2][:], gate[:, 0:1], x, ALU.mult,
                                                   ALU.add).then_inc(misc_evicted[n % 2], 1)

            for kt in range(KT):
                ctx_tile_stats(0, kt)
            x_stats(0, 0)
            for kt in range(KT):
                ctx_tile_norm(0, kt)
            x_norm(0, 0)
            dve.wait_ge(x_normed, 1)
            x_stats(0, 1)
            x_norm(0, 1)
            dve.wait_ge(loaded, 16 * N_LOADS)
            for q in (0, 2):
                nc.vector.tensor_scalar(sinT[32 * q:32 * q + 32, :], sinT[32 * q:32 * q + 32, :], -1.0, None,
                                        ALU.mult)
            dve.wait_ge(gates_ready, 1)
            nc.vector.tensor_scalar(bo[:], bo[:], gate[:, 0:1], None, ALU.mult).then_inc(tables_ready, 1)
            q_lo(0, 0)
            with dve.Fori(0, BATCH - 1) as b:
                batch(b, False)
            batch(BATCH - 1, True)

        @block.tensor
        def _(pe):
            pe.wait_ge(loaded, 16 * N_LOADS)
            pe.wait_ge(ident_ready, 1)

            def extra(b, name):
                kind = name[0]
                n = MISC[name]
                pe.wait_ge(misc_evicted[n % 2], (b + (name in BATCH_TAIL)) * MB + n // 2 + 1)
                out = ps_m[n % 2]
                if kind == "ctxT":
                    _, c, h = name
                    if (c, h) == (0, 0):
                        pe.wait_ge(ctx_normed, b + 1)
                    for j in range(4):
                        ins = nc.tensor.transpose(out[:, j * P:(j + 1) * P],
                                                  context[:, 4 * h + j, c * P:(c + 1) * P], ident[:])
                elif kind == "latT":
                    c = name[1]
                    if c == 0:
                        pe.wait_ge(x_normed, 2 * b + 2)
                    for j in range(XT):
                        ins = nc.tensor.transpose(out[:, j * P:(j + 1) * P], lat[:, j, c * P:(c + 1) * P], ident[:])
                elif kind == "v":
                    _, kt, h = name
                    for c in range(DC):
                        ins = nc.tensor.matmul(out[:], ctxT[:, c, kt * P:(kt + 1) * P],
                                               wkv[:, c, INNER + h * HALF:INNER + (h + 1) * HALF],
                                               start=c == 0, stop=c == DC - 1)
                elif kind == "k":
                    _, t, h = name
                    if (t, h) == (0, 0):
                        for c in range(DC):
                            wait_evicted(pe, b, ("latT", c))
                    for c in range(DC):
                        ins = nc.tensor.matmul(out[:], wkv[:, c, t * P:(t + 1) * P],
                                               ctxT[:, c, h * HALF:(h + 1) * HALF], start=c == 0, stop=c == DC - 1)
                elif kind == "q":
                    t = name[1]
                    for c in range(DC):
                        ins = nc.tensor.matmul(out[:], wq[:, c, t * P:(t + 1) * P], latT[:, c, :],
                                               start=c == 0, stop=c == DC - 1)
                elif kind == "den":
                    t = name[1]
                    pe.wait_ge(*added_count(b, t * KT + KT - 1))
                    for a in range(2):
                        ins = nc.tensor.matmul(out[DHEAD * a:DHEAD * (a + 1), :], ones[:],
                                               psum[:, a * SEQ:(a + 1) * SEQ], start=True, stop=True)
                else:
                    m = name[1]
                    if m == 0:
                        pe.wait_ge(recip_ready, (b + 1) * PAIRS)
                    for j in range(2):
                        for t in range(PAIRS):
                            ins = nc.tensor.matmul(out[:, j * DIM:(j + 1) * DIM],
                                                   oT[:, t, (2 * m + j) * P:(2 * m + j + 1) * P], wo[:, t, :],
                                                   start=t == 0, stop=t == PAIRS - 1)
                ins.then_inc(misc_ready, 1)

            def skip(b, name):
                n = MISC[name]
                pe.wait_ge(misc_evicted[n % 2], (b + (name in BATCH_TAIL)) * MB + n // 2 + 1)
                pe.sem_inc(misc_evicted[n % 2], 1)
                pe.wait_ge(misc_ready, (b + (name in BATCH_TAIL)) * NM + n)
                pe.sem_inc(misc_ready, 1)

            def scores(b, i):
                t, kt = divmod(i, KT)
                if kt == 0:
                    pe.wait_ge(k_second_ready, b * PAIRS + t + 1)
                    pe.wait_ge(k_stacked, 32 * (b * PAIRS + t + 1))
                    pe.wait_ge(q_first, 16 * (b * PAIRS + t + 1))
                if i >= SCORE_SLOTS:
                    pe.wait_ge(clipped, b * UNITS + i - SCORE_SLOTS + 1)
                for a in range(2):
                    for part in range(2):
                        ins = nc.tensor.matmul(ps_s[i % SCORE_SLOTS][:, a * SEQ:(a + 1) * SEQ],
                                               ksplit[:, t % 2, a, kt * P:(kt + 1) * P],
                                               qsplit[:, t % 2, a, part, :], start=part == 0, stop=part == 1)
                ins.then_inc(scores_ready, 1)

            def values(b, i):
                t, kt = divmod(i, KT)
                pe.wait_ge(exp_done, b * UNITS + i + 1)
                if t % 4 == 0:
                    wait_evicted(pe, b, ("v", kt, t // 4))
                if kt == 0 and t >= 2:
                    pe.wait_ge(recip_ready, b * PAIRS + t - 1)
                for a in range(2):
                    col = (2 * t + a) * DHEAD
                    ins = nc.tensor.matmul(ps_av[t % 2][DHEAD * a:DHEAD * (a + 1), :], v[:, kt, col:col + DHEAD],
                                           probs[:, i % PROB_SLOTS, a * SEQ:(a + 1) * SEQ],
                                           start=kt == 0, stop=kt == KT - 1)
                ins.then_inc(probs_used, 1)

            def batch(b, last):
                for i in range(UNITS + AV_LAG):
                    if i < UNITS:
                        scores(b, i)
                        for name in attention_extras(i):
                            extra(b, name)
                        for name in attention_lead(i):
                            if last:
                                skip(b + 1, name)
                            else:
                                extra(b + 1, name)
                    if i >= AV_LAG:
                        values(b, i - AV_LAG)
                for name in BOUNDARY:
                    if name in BATCH_TAIL:
                        extra(b, name)
                    elif not last:
                        extra(b + 1, name)
                    else:
                        skip(b + 1, name)

            for i in range(UNITS):
                for name in attention_lead(i):
                    extra(0, name)
            for name in BOUNDARY:
                if name in BATCH_TAIL:
                    skip(-1, name)
                else:
                    extra(0, name)
            pe.wait_ge(tables_ready, 1)
            with pe.Fori(0, BATCH - 1) as b:
                batch(b, False)
            batch(BATCH - 1, True)



class RowNorm:

    def __init__(self, nc, ctx, sh, name, sem):
        def sb(part, shape):
            return ctx.enter_context(nc.sbuf_tensor(f"{name}_{part}", shape, F32))

        self.nc, self.sh = nc, sh
        self.out = sb("normed", [P, XT, DIM])
        self.sums, self.meanvar, self.rstd = sb("sums", [P, XT, 6]), sb("meanvar", [P, XT, 2]), sb("rstd", [P, XT])
        self.summed = sem(name + "_summed")
        self.stats = sem(name + "_stats")
        self.eps_added, self.rstd_ready = sem(name + "_eps_added"), sem(name + "_rstd_ready")
        self.ready = sem(name + "_ready")
        self.passed = sem(name + "_passed")

    def statistics(self, dve, turn, x):
        for j in range(XT):
            self.nc.vector.bn_stats(self.sums[:, j, :], x[:, j, :]).then_inc(self.summed, 1)
        dve.wait_ge(self.summed, XT * turn + XT)
        dve.sem_inc(self.passed, 1)
        for j in range(XT):
            ins = self.nc.vector.bn_aggr(self.meanvar[:, j, :], self.sums[:, j, :])
        ins.then_inc(self.stats, 1)

    def power(self, pool, turn):
        pool.wait_ge(self.stats, turn + 1)
        self.nc.gpsimd.tensor_tensor(self.rstd[:], self.meanvar[:, :, 1], self.sh.eps[:, 0:XT],
                                     ALU.add).then_inc(self.eps_added, 1)
        pool.wait_ge(self.eps_added, turn + 1)
        self.nc.gpsimd.tensor_tensor(self.rstd[:], self.rstd[:], self.sh.mhalf[:, 0:XT],
                                     ALU.pow).then_inc(self.rstd_ready, 1)

    def apply(self, dve, turn, x):
        dve.wait_ge(self.rstd_ready, turn + 1)
        for j in range(XT):
            ins = self.nc.vector.tensor_scalar(self.out[:, j, :], x[:, j, :], self.meanvar[:, j, 0:1],
                                               self.rstd[:, j:j + 1], ALU.subtract, ALU.mult)
        ins.then_inc(self.ready, 1)



KEY_HEADS, D_QUERY, SUBKEYS, D_LATENT, D_HIDDEN = 4, 64, 128, 64, 128
EXPERTS = 4096
TOP = 8
PICKS = KEY_HEADS * TOP
QC = KEY_HEADS * D_QUERY // P
ET = EXPERTS // P


class KeyState:

    def __init__(self, nc, ctx):
        self.scale = ctx.enter_context(nc.sbuf_tensor("keys_scale", [P, QC], F32))
        self.shift = ctx.enter_context(nc.sbuf_tensor("keys_shift", [P, QC], F32))


def key_queries(nc, sh, ks, d, sem):
    with ExitStack() as ctx:
        def sb(name, shape):
            return ctx.enter_context(nc.sbuf_tensor("s2_" + name, shape, F32))

        ident = sh.ident
        norm = RowNorm(nc, ctx, sh, "s2_norm", sem)
        x_all = sb("x", [P, BATCH, XT, DIM])
        wq, wx = sb("wq", [P, DC, QC * P]), sb("wx", [P, DC, D_HIDDEN])
        cols = sb("cols", [P, 3, QC])
        latT, w1 = sb("latentsT", [D_LATENT, EXPERTS]), sb("w1", [D_LATENT, D_HIDDEN])
        hidden = sb("hidden", [P, 2, 4, D_HIDDEN])
        xT = sb("xT", [P, DC, SEQ])
        qT, proj = sb("qT", [P, BATCH, QC, SEQ]), sb("proj", [P, BATCH, XT, D_HIDDEN])
        qsums, qmv = sb("q_sums", [P, QC, BATCH, 6]), sb("q_meanvar", [P, QC, 2])
        qrs = sb("q_rstd", [P, QC])
        ps_t = [ctx.enter_context(nc.psum_tensor(f"s2_ps_t{c}", [P, HALF], F32)) for c in range(DC)]
        ps_q = [ctx.enter_context(nc.psum_tensor(f"s2_ps_q{c}", [P, HALF], F32)) for c in range(QC)]
        ps_x = ctx.enter_context(nc.psum_tensor("s2_ps_x", [P, XT, D_HIDDEN], F32))
        ps_h = [ctx.enter_context(nc.psum_tensor(f"s2_ps_h{c}", [P, 4, D_HIDDEN], F32)) for c in range(2)]

        table_in = sem("s2_table_inputs")
        loaded, hid_ready, hid_done, hid_out = sem("s2_loaded"), sem("hidden_ready"), sem("hidden_done"), \
            [sem("hidden_out0"), sem("hidden_out1")]
        t_ready, t_out = sem("s2_transposed"), sem("s2_xT_out")
        q_ready, q_out = sem("s2_q_ready"), sem("s2_q_out")
        p_ready, p_out = sem("s2_proj_ready"), sem("s2_proj_out")
        q_summed, q_eps, q_rstd, steps = sem("s2_q_summed"), sem("s2_q_eps"), sem("s2_q_rstd"), sem("s2_steps")
        q_stats, passed = sem("s2_q_stats"), sem("s2_passed")
        q_stored = sem("s2_stored")
        x_first, x_rest = sem("x_first_loaded"), sem("x_rest_loaded")
        N_LOADS = 5
        block = ctx.enter_context(nc.Block())

        @block.sync
        def _(sp):
            sp.dma_start(w1[:], d["w1"]).then_inc(table_in, 16)
            sp.dma_start(latT[:], d["latentsT"]).then_inc(table_in, 16)
            sp.dma_start(x_all[:, 0], d["x_dram"][0]).then_inc(x_first, 16)
            sp.dma_start(wq[:], d["keys_wqT"].rearrange("(c p) n -> p c n", p=P)).then_inc(loaded, 16)
            sp.dma_start(wx[:], d["w2xT"].rearrange("(c p) n -> p c n", p=P)).then_inc(loaded, 16)
            for n, name in enumerate(("keys_bq", "keys_gamma", "keys_beta")):
                sp.dma_start(cols[:, n, :], d[name]).then_inc(loaded, 16)
            for b in range(1, BATCH):
                sp.dma_start(x_all[:, b], d["x_dram"][b]).then_inc(x_rest, 16)
            for n in range(ET // 4):
                sp.wait_ge(hid_done, n + 1)
                sp.dma_start(d["table"][4 * n * P:4 * (n + 1) * P, :].rearrange("(j p) f -> p j f", p=P),
                             hidden[:, n % 2]).then_inc(hid_out[n % 2], 16)
            for s in hid_out:
                sp.wait_ge(s, 16 * ET // 8)
            with sp.Fori(0, BATCH) as b:
                sp.wait_ge(q_out, QC * (b + 1))
                sp.sem_inc(passed, 1)
                sp.dma_start(d["q_dram"][b], qT[:, b]).then_inc(q_stored, 16)
                sp.wait_ge(p_out, b + 1)
                sp.sem_inc(passed, 1)
                sp.dma_start(d["proj_dram"][b], proj[:, b]).then_inc(q_stored, 16)
            sp.wait_ge(q_stored, 32 * BATCH)

        @block.gpsimd
        def _(pool):
            with pool.Fori(0, BATCH) as b:
                norm.power(pool, b)
            pool.wait_ge(q_stats, 1)
            nc.gpsimd.tensor_tensor(qrs[:], qmv[:, :, 1], sh.eps[:, 0:QC], ALU.add).then_inc(q_eps, 1)
            pool.wait_ge(q_eps, 1)
            nc.gpsimd.tensor_tensor(qrs[:], qrs[:], sh.mhalf[:, 0:QC], ALU.pow).then_inc(q_rstd, 1)

        @block.scalar
        def _(act):
            for n in range(ET // 4):
                act.wait_ge(hid_ready, n + 1)
                if n >= 2:
                    act.wait_ge(hid_out[n % 2], 16 * (n // 2))
                nc.scalar.activation(hidden[:, n % 2].rearrange("p j f -> p (j f)"),
                                     ps_h[n % 2][:].rearrange("p j f -> p (j f)"), ACT.Gelu).then_inc(hid_done, 1)
            act.wait_ge(loaded, 16 * N_LOADS)
            with act.Fori(0, BATCH) as b:
                for c in range(DC):
                    act.wait_ge(t_ready, DC * b + c + 1)
                    nc.scalar.copy(xT[:, c, :], ps_t[c][:]).then_inc(t_out, 1)
                for c in range(QC):
                    act.wait_ge(q_ready, QC * b + c + 1)
                    nc.scalar.activation(qT[:, b, c, :], ps_q[c][:], ACT.Identity,
                                         bias=cols[:, 0, c:c + 1]).then_inc(q_out, 1)
                act.wait_ge(p_ready, b + 1)
                nc.scalar.copy(proj[:, b].rearrange("p j f -> p (j f)"),
                               ps_x[:].rearrange("p j f -> p (j f)")).then_inc(p_out, 1)

        @block.vector
        def _(dve):
            def query_sums(b):
                for c in range(QC):
                    dve.wait_ge(q_out, QC * b + c + 1)
                    nc.vector.bn_stats(qsums[:, c, b, :], qT[:, b, c, :]).then_inc(q_summed, 1)

            dve.wait_ge(x_first, 16)
            dve.sem_inc(passed, 1)
            norm.statistics(dve, 0, x_all[:, 0])
            norm.apply(dve, 0, x_all[:, 0])
            dve.wait_ge(x_rest, 16 * (BATCH - 1))
            dve.sem_inc(passed, 1)
            with dve.Fori(0, BATCH - 1) as b:
                norm.statistics(dve, b + 1, x_all[:, b + 1])
                dve.wait_ge(t_ready, DC * b + DC)
                dve.sem_inc(passed, 1)
                norm.apply(dve, b + 1, x_all[:, b + 1])
                query_sums(b)
            query_sums(BATCH - 1)
            dve.wait_ge(q_summed, QC * BATCH)
            for c in range(QC):
                ins = nc.vector.bn_aggr(qmv[:, c, :], qsums[:, c].rearrange("p b s -> p (b s)"))
            ins.then_inc(q_stats, 1)
            dve.wait_ge(q_rstd, 1)
            dve.wait_ge(loaded, 16 * N_LOADS)
            nc.vector.tensor_tensor(ks.scale[:], qrs[:], cols[:, 1, :], ALU.mult).then_inc(steps, 1)
            dve.wait_ge(steps, 1)
            nc.vector.tensor_tensor(ks.shift[:], qmv[:, :, 0], ks.scale[:], ALU.mult).then_inc(steps, 1)
            dve.wait_ge(steps, 2)
            nc.vector.tensor_tensor(ks.shift[:], cols[:, 2, :], ks.shift[:], ALU.subtract).then_inc(steps, 1)

        @block.tensor
        def _(pe):
            pe.wait_ge(table_in, 32)
            for n in range(ET // 4):
                if n >= 2:
                    pe.wait_ge(hid_done, n - 1)
                for j in range(4):
                    ins = nc.tensor.matmul(ps_h[n % 2][:, j, :], latT[:, (4 * n + j) * P:(4 * n + j + 1) * P], w1[:],
                                           start=True, stop=True)
                ins.then_inc(hid_ready, 1)

            def body(b, first):
                if first:
                    pe.wait_ge(loaded, 16 * N_LOADS)
                pe.wait_ge(norm.ready, b + 1)
                for c in range(DC):
                    if not first and c == 0:
                        pe.wait_ge(t_out, DC * b)
                    for j in range(XT):
                        ins = nc.tensor.transpose(ps_t[c][:, j * P:(j + 1) * P], norm.out[:, j, c * P:(c + 1) * P],
                                                  ident[:])
                    ins.then_inc(t_ready, 1)
                pe.wait_ge(t_out, DC * (b + 1))
                for m in range(QC):
                    if not first and m == 0:
                        pe.wait_ge(q_out, QC * b)
                    for c in range(DC):
                        ins = nc.tensor.matmul(ps_q[m][:], wq[:, c, m * P:(m + 1) * P], xT[:, c, :],
                                               start=c == 0, stop=c == DC - 1)
                    ins.then_inc(q_ready, 1)
                if not first:
                    pe.wait_ge(p_out, b)
                for j in range(XT):
                    for c in range(DC):
                        ins = nc.tensor.matmul(ps_x[:, j, :], xT[:, c, j * P:(j + 1) * P], wx[:, c, :],
                                               start=c == 0, stop=c == DC - 1)
                ins.then_inc(p_ready, 1)

            body(0, True)
            with pe.Fori(1, BATCH) as b:
                body(b, False)



LISTS = 2 * KEY_HEADS
GROUPS = XT * KEY_HEADS
HALVES = 2 * XT
HP = PICKS // 2
MOE, FF = 8, 512
FT = FF // P
BLOCKS = (MOE + 1) * FT
LOGIT_SLOTS = 4
FIRST_HALF = 2


def half_step(n):
    u, step = divmod(n - FIRST_HALF, 4)
    return (u, step) if 0 <= u < HALVES else None


def tile_at(n, lag):
    j, r = divmod(n - lag - FIRST_HALF - 7, 8)
    return j if r == 0 and 0 <= j < XT else None


GATES_AT = 2
TAIL = 4


class Order:

    def __init__(self, names, before):
        assert len(names) % 2 == 0 and before % 2 == 0
        self.names, self.before, self.no = names, before, {name: n for n, name in enumerate(names)}

    def made(self, b, name):
        return self.before + self.turn * b + self.no[name] + 1

    def bank(self, name):
        return self.no[name] % 2

    def free(self, b, name):
        return (self.before + self.turn * b) // 2 + self.no[name] // 2 + 1 if isinstance(b, int) else \
            b * (self.turn // 2) + self.before // 2 + self.no[name] // 2 + 1

    def out(self, b, name):
        return self.free(b, name) + 1


def orders():
    s = [[("s", j, c) for c in range(QC)] for j in range(XT)]
    keys_of_context = [("k", m, h) for m in range(DC) for h in range(2)]
    first = sum(s, []) + keys_of_context + [x for j in range(XT) for x in (("accT", j), ("keys", j))]

    def turn(with_keys):
        s_ = s if with_keys else [[]] * XT
        names = s_[0] + s_[1] + [("v", 0), ("v", 1)] + [("xT", 0, c) for c in range(DC)] + [("v", 2), ("v", 3)]
        names += [("q", c) for c in range(DC)] + s_[2] + s_[3]
        if with_keys:
            names += keys_of_context
        names += [("xT", 1, c) for c in range(DC)] + [("router",), ("gatesT",)]
        if with_keys:
            names += [x for j in range(XT) for x in (("accT", j), ("keys", j))]
        return names

    Order.turn = len(turn(True))
    return Order(first, 0), Order(turn(True), len(first)), Order(turn(False), len(first))


def keys_and_layer1(nc, sh, ks, d, sem):
    with ExitStack() as ctx:
        def sb(name, shape, dt=F32):
            return ctx.enter_context(nc.sbuf_tensor("s3_" + name, shape, dt))

        gate, ident = sh.gate, sh.ident
        x_next, x_now = sb("x_next", [P, XT, DIM]), sb("x_now", [P, XT, DIM])
        subkeys = sb("subkeys", [P, 4, SUBKEYS])
        wkeys = sb("wkeys", [D_HIDDEN, DIM])
        gate4 = sb("gate4", [P, 1])
        digits_i, digits = sb("digits_i", [P, TOP], mybir.dt.int32), sb("digits", [P, TOP])
        qn, proj = sb("qn", [P, QC, SEQ]), sb("proj", [P, XT, D_HIDDEN])
        scores = sb("scores", [P, 2, LISTS, SUBKEYS])
        best, best_at = sb("best", [P, XT, LISTS, TOP]), sb("best_at", [P, XT, LISTS, TOP], U32)
        pair = sb("pair_sums", [P, GROUPS, TOP, TOP])
        top, top_at = sb("top", [P, GROUPS, TOP]), sb("top_at", [P, GROUPS, TOP], U32)
        digit = sb("digit", [P, GROUPS, 2, TOP], U32)
        prod = sb("prod", [P, HP * D_HIDDEN])
        pick = prod[:].rearrange("p (n a) -> p n a", a=TOP)
        part = sb("part", [P, GROUPS, 2, TOP])
        expert, expert_at = sb("expert", [P, GROUPS, TOP]), sb("expert_at", [P, XT * PICKS], U32)
        prob, prob_sum = sb("prob", [P, GROUPS, TOP]), sb("prob_sum", [P, GROUPS])
        rows = sb("rows", [P, 2, HP, D_HIDDEN])
        dots, acts = sb("dots", [P, 2, HP]), sb("acts", [P, 2, HP])
        acc, accT = sb("acc", [P, 4, D_HIDDEN]), sb("accT", [P, 2, P])
        norm = RowNorm(nc, ctx, sh, "s3_norm", sem)
        wq, wk, wv = sb("wq", [P, DC, DIM]), sb("wk", [P, DC, DIM]), sb("wv", [P, DC, DIM])
        bq, bk, bv = sb("bq", [P, DC]), sb("bk", [P, DC]), sb("bv", [P, 2, DIM])
        maskT = sb("maskT", [P, KT, SEQ])
        ctxT = sb("ctxT", [P, DC, CTX])
        kp, vp, qp = sb("kp", [P, DC, CTX]), sb("vp", [P, KT, DIM]), sb("qp", [P, DC, SEQ])
        logits = sb("logits", [P, LOGIT_SLOTS, SEQ])
        act_in, hid = logits[:, 0:2, :], logits[:, 2:4, :]
        xT = sb("xT", [P, DC, SEQ])
        router = sb("router", [P, DC, MOE])
        w_in, w_sw = sb("w_in", [P, 3, DC, FF]), sb("w_sw", [P, 3, DC, FF])
        w_out = sb("w_out", [P, 3, FT, DIM])
        rs, rs_top = sb("router_scores", [P, XT, MOE]), sb("router_top", [P, XT, TOP])
        rs_at = sb("router_at", [P, XT, TOP], U32)
        second, gates, sig = sb("second", [P, XT, MOE]), sb("gates", [P, XT, MOE]), sb("sigmoids", [P, XT, MOE])
        gatesT = sb("gatesT", [MOE, SEQ])
        gates_all = sb("gates_all", [P, 2, SEQ])
        xg = sb("xg", [P, 2, DC, SEQ])
        attn = xg[:, 0].rearrange("p c q -> p (c q)")

        ps_m = [ctx.enter_context(nc.psum_tensor(f"s3_ps_m{c}", [P, HALF], F32)) for c in range(2)]
        ps_o = ctx.enter_context(nc.psum_tensor("s3_ps_o", [P, XT, DIM], F32))
        ps_a = [ctx.enter_context(nc.psum_tensor(f"s3_ps_a{c}", [P, HALF], F32)) for c in range(2)]
        ps_b = [ctx.enter_context(nc.psum_tensor(f"s3_ps_b{c}", [P, HALF], F32)) for c in range(2)]

        keys_loaded = sem("s3_keys_loaded")
        loaded, consts, bias_scaled = sem("s3_loaded"), sem("s3_consts"), sem("s3_bias_scaled")
        zeroed = sem("s3_zeroed")
        misc_made, misc_out = sem("misc_made"), [sem("misc_out0"), sem("misc_out1")]
        q_loaded, qn_ready = sem("q_loaded"), sem("qn_ready")
        listed = sem("listed")
        steps = sem("choice_steps")
        diffs, exps = sem("prob_diffs"), sem("prob_exps")
        experts = sem("experts_known")
        gathered = [sem("rows_gathered0"), sem("rows_gathered1")]
        weighed = sem("rows_weighed")
        dotted, gelued = sem("rows_dotted"), sem("dots_gelued")
        used = sem("rows_used")
        x_loaded = sem("s3_x_loaded")
        ctx_loaded, expert_in = sem("l1_ctx_loaded"), [sem("expert_in0"), sem("expert_in1")]
        relued = sem("v_relued")
        s_ready, s_out = sem("l1_scores"), sem("l1_logits")
        av_ready, attn_out, x_done = sem("l1_av"), sem("l1_attn_out"), sem("l1_x_attended")
        route_steps, sig_ready, gates_ready = sem("route_steps"), sem("sigmoids_ready"), sem("gates_chosen")
        gates_stored, gates_in = sem("gates_stored"), [sem("gates_in0"), sem("gates_in1")]
        xg_ready = sem("rows_gated")
        a_ready, a_out, h_ready, h_used = sem("first_ready"), sem("silu_out"), sem("hidden_ready_l1"), sem("hidden_used")
        moe_out, stored = sem("moe_added"), sem("out_stored")
        passed = sem("s3_waits_passed")
        N_LOADS, N_KEY_LOADS = 11, 5
        FIRST, LOOP, LAST = orders()
        block = ctx.enter_context(nc.Block())

        def stop_until(eng, s, value):
            eng.wait_ge(s, value)
            eng.sem_inc(passed, 1)

        def wait_made(eng, o, b, name):
            eng.wait_ge(misc_made, o.made(b, name))

        def wait_out(eng, o, b, name):
            eng.wait_ge(misc_out[o.bank(name)], o.out(b, name))

        def choices(kb, tile):
            return tile if tile is not None else kb + XT - 1

        def groups(tile):
            return slice(KEY_HEADS * tile, KEY_HEADS * (tile + 1)) if tile is not None else slice(0, GROUPS)

        @block.sync
        def _(sp):
            sp.dma_start(qn[:], d["q_dram"][0]).then_inc(q_loaded, 16)
            sp.dma_start(proj[:], d["proj_dram"][0]).then_inc(q_loaded, 16)
            sp.dma_start(x_next[:], d["x_dram"][0]).then_inc(x_loaded, 16)
            sp.dma_start(wkeys[:], d["w2v"]).then_inc(keys_loaded, 16)
            sp.wait_ge(zeroed, 1)
            for n in range(4):
                sp.dma_start(subkeys[32 * n:32 * n + 32, n, :], d[f"sk{n % 2 + 1}T"]).then_inc(keys_loaded, 16)
            sp.dma_start(ctxT[:], d["ctxT"][0]).then_inc(ctx_loaded, 16)
            for t, name in ((wk, "l1_wk"), (wq, "l1_wq"), (wv, "l1_wv"), (router, "router")):
                sp.dma_start(t[:], d[name].rearrange("(c p) n -> p c n", p=P)).then_inc(loaded, 16)
            sp.dma_start(bq[:], d["l1_bq"]).then_inc(loaded, 16)
            sp.dma_start(bk[:], d["l1_bk"]).then_inc(loaded, 16)
            sp.dma_start(bv[:], d["l1_bv"].unsqueeze(1).to_broadcast([P, 2, DIM])).then_inc(loaded, 16)
            sp.dma_start(w_in[:, 2], d["w_in_shared"].rearrange("(c p) n -> p c n", p=P)).then_inc(loaded, 16)
            sp.dma_start(w_sw[:, 2], d["w_sw_shared"].rearrange("(c p) n -> p c n", p=P)).then_inc(loaded, 16)
            sp.dma_start(w_out[:, 2], d["w_out_shared"].rearrange("(f p) n -> p f n", p=P)).then_inc(loaded, 16)
            sp.dma_start(maskT[:], d["maskT"].rearrange("(t p) q -> p t q", p=P)).then_inc(loaded, 16)

            def expert_weights(b, e, first):
                if not first:
                    stop_until(sp, h_used, b * BLOCKS + (e if e >= 2 else e - 1) * FT)
                s = e % 2
                sp.dma_start(w_in[:, s], d["w_in"][e].rearrange("(c p) n -> p c n", p=P)).then_inc(expert_in[s], 16)
                sp.dma_start(w_sw[:, s], d["w_sw"][e].rearrange("(c p) n -> p c n", p=P)).then_inc(expert_in[s], 16)
                sp.dma_start(w_out[:, s], d["w_out"][e].rearrange("(f p) n -> p f n", p=P)).then_inc(expert_in[s], 16)

            def batch(b, o, first):
                if o is LOOP:
                    stop_until(sp, used, HALVES * (b + 1))
                    sp.dma_start(qn[:], d["q_dram"][b + 1]).then_inc(q_loaded, 16)
                    sp.dma_start(proj[:], d["proj_dram"][b + 1]).then_inc(q_loaded, 16)
                for e in range(2):
                    expert_weights(b, e, first)
                if not first:
                    stop_until(sp, moe_out, b)
                    sp.dma_start(d["out"][b - 1], x_now[:]).then_inc(stored, 16)
                if o is LOOP:
                    stop_until(sp, misc_made, o.made(b, ("v", KT // 2 - 1)))
                    sp.dma_start(ctxT[:], d["ctxT"][b + 1]).then_inc(ctx_loaded, 16)
                    stop_until(sp, x_done, b + 1)
                    sp.dma_start(x_next[:], d["x_dram"][b + 1]).then_inc(x_loaded, 16)
                wait_out(sp, o, b, ("gatesT",))
                sp.sem_inc(passed, 1)
                sp.dma_start(d["gates_dram"], gatesT[:]).then_inc(gates_stored, 16)
                stop_until(sp, gates_stored, 16 * (b + 1))
                for e in range(MOE):
                    if e >= 2:
                        stop_until(sp, xg_ready, MOE * b + e - 1)
                    sp.dma_start(gates_all[:, e % 2, :],
                                 d["gates_dram"][e:e + 1, :].to_broadcast([P, SEQ])).then_inc(gates_in[e % 2], 16)
                    if e >= 2:
                        expert_weights(b, e, False)

            batch(0, LOOP, True)
            with sp.Fori(1, BATCH - 1) as b:
                batch(b, LOOP, False)
            batch(BATCH - 1, LAST, False)
            sp.wait_ge(moe_out, BATCH)
            sp.dma_start(d["out"][BATCH - 1], x_now[:]).then_inc(stored, 16)
            sp.wait_ge(stored, 16 * BATCH)

        @block.gpsimd
        def _(pool):
            nc.gpsimd.iota(digits_i[:], pattern=[[1, TOP]], base=0, channel_multiplier=0).then_inc(consts, 1)
            pool.wait_ge(consts, 1)
            nc.gpsimd.tensor_copy(digits[:], digits_i[:]).then_inc(consts, 1)

            def gather(b, first=False):
                for u in range(HALVES):
                    if first:
                        pool.wait_ge(experts, u // 2 + 1)
                    if not (first and u < 2):
                        stop_until(pool, used, HALVES * b + u - 1)
                    for k in range(HP):
                        at = u * HP + k
                        nc.gpsimd.indirect_dma_start(
                            out=rows[:, u % 2, k, :], out_offset=None, in_=d["table"],
                            in_offset=bass.IndirectOffsetOnAxis(ap=expert_at[:, at:at + 1], axis=0),
                        ).then_inc(gathered[u % 2], 16)

            gather(0, True)
            with pool.Fori(0, BATCH - 1) as b:
                for n in range(2):
                    norm.power(pool, 2 * b + n)
                pool.wait_ge(experts, choices(b + 1, None) + 1)
                gather(b + 1)
            for n in range(2):
                norm.power(pool, 2 * (BATCH - 1) + n)

        @block.scalar
        def _(act):
            for s in misc_out:
                act.sem_inc(s, 1)

            def queries(kb):
                act.wait_ge(q_loaded, 32 * (kb + 1))
                for c in range(QC):
                    nc.scalar.activation(qn[:, c, :], qn[:, c, :], ACT.Identity, scale=ks.scale[:, c:c + 1],
                                         bias=ks.shift[:, c:c + 1]).then_inc(qn_ready, 1)

            def take(o, b, name, kb=None):
                kind = name[0]
                wait_made(act, o, b, name)
                src = ps_m[o.bank(name)]
                if kind == "s":
                    _, j, c = name
                    if j >= 2 and c == 0:
                        act.wait_ge(listed, 2 * (XT * kb + j - 1))
                    ins = nc.scalar.copy(scores[:, j % 2, 4 * c:4 * c + 4, :].rearrange("p l k -> p (l k)"), src[:])
                elif kind == "accT":
                    ins = nc.scalar.copy(accT[:, name[1] % 2, :], src[:, 0:P])
                elif kind == "xT":
                    ins = nc.scalar.copy(xT[:, name[2], :], src[:])
                elif kind == "k":
                    _, m, h = name
                    ins = nc.scalar.activation(kp[:, m, h * HALF:(h + 1) * HALF], src[:], ACT.Relu, bias=bk[:, m:m + 1])
                elif kind == "q":
                    ins = nc.scalar.activation(qp[:, name[1], :], src[:], ACT.Relu, bias=bq[:, name[1]:name[1] + 1],
                                               scale=1.0 / 16.0)
                else:
                    ins = nc.scalar.copy(gatesT[:], src[0:MOE, :])
                ins.then_inc(misc_out[o.bank(name)], 1)

            def exponentials(kb, tile=None):
                act.wait_ge(diffs, choices(kb, tile) + 1)
                p = prob[:, groups(tile)].rearrange("p h k -> p (h k)")
                nc.scalar.activation(p, p, ACT.Exp).then_inc(exps, 1)

            def gelu(kb, u):
                act.wait_ge(dotted, HALVES * kb + u + 1)
                nc.scalar.activation(acts[:, u % 2, :], dots[:, u % 2, :], ACT.Gelu).then_inc(gelued, 1)

            def batch(b, o):
                keys = o is LOOP
                if keys:
                    queries(b + 1)
                for name in o.names[:o.no[("q", DC - 1)] + 1 + (2 * QC if keys else 0)]:
                    if name[0] != "v":
                        take(o, b, name, b + 1)
                    if name == ("q", DC - 1):
                        for n in range(KT // 2):
                            wait_out(act, o, b, ("v", n))
                            v = vp[:, 2 * n:2 * n + 2, :].rearrange("p t n -> p (t n)")
                            nc.scalar.activation(v, v, ACT.Relu).then_inc(relued, 1)
                act.wait_ge(av_ready, KT * (b + 1))
                nc.scalar.activation(attn, ps_o[:].rearrange("p j n -> p (j n)"), ACT.Relu).then_inc(attn_out, 1)
                if keys:
                    for m in range(DC):
                        for h in range(2):
                            take(o, b, ("k", m, h))
                    exponentials(b + 1)
                for c in range(DC):
                    take(o, b, ("xT", 1, c))
                wait_out(act, o, b, ("router",))
                nc.scalar.activation(sig[:], rs[:], ACT.Sigmoid).then_inc(sig_ready, 1)
                for n in range(BLOCKS + TAIL):
                    if n == GATES_AT:
                        take(o, b, ("gatesT",))
                    if n < BLOCKS:
                        act.wait_ge(a_ready, b * BLOCKS + n + 1)
                        if n >= 2:
                            act.wait_ge(h_ready, b * BLOCKS + n - 1)
                        nc.scalar.activation(act_in[:, n % 2, :], ps_a[n % 2][:], ACT.Silu).then_inc(a_out, 1)
                    if keys and (half := half_step(n)) and half[1] == 1:
                        gelu(b + 1, half[0])
                    if keys and (j := tile_at(n, 1)) is not None:
                        take(o, b, ("accT", j))

            queries(0)
            for j in range(XT):
                for c in range(QC):
                    take(FIRST, 0, ("s", j, c), 0)
                if j >= 1:
                    exponentials(0, j - 1)
            exponentials(0, XT - 1)
            act.wait_ge(loaded, 16 * N_LOADS)
            nc.scalar.mul(bq[:], bq[:], 1.0 / 16.0).then_inc(bias_scaled, 1)
            act.wait_ge(bias_scaled, 1)
            for m in range(DC):
                for h in range(2):
                    take(FIRST, 0, ("k", m, h))
            for u in range(HALVES):
                gelu(0, u)
                if u % 2:
                    take(FIRST, 0, ("accT", u // 2))
            with act.Fori(0, BATCH - 1) as b:
                batch(b, LOOP)
            batch(BATCH - 1, LAST)

        @block.vector
        def _(dve):
            nc.vector.memset(subkeys[:], 0.0).then_inc(zeroed, 1)
            nc.vector.tensor_scalar(gate4[:], gate[:, 2:3], 1.0 / KEY_HEADS, None, ALU.mult)
            dve.wait_ge(consts, 2)
            CHOICE_STEPS, ROUTE_STEPS = 11, 4

            def lists(o, b, kb, j):
                wait_out(dve, o, b, ("s", j, 0))
                dve.sem_inc(passed, 1)
                stop_until(dve, misc_out[o.bank(("s", j, 1))], o.out(b, ("s", j, 1)))
                for n in range(LISTS):
                    ins = nc.vector.max(best[:, j, n, :], scores[:, j % 2, n, :])
                ins.then_inc(listed, 1)
                stop_until(dve, listed, 2 * (XT * kb + j) + 1)
                for n in range(LISTS):
                    ins = nc.vector.max_index(best_at[:, j, n, :], best[:, j, n, :], scores[:, j % 2, n, :])
                ins.then_inc(listed, 1)

            def choose(kb, piece, tile=None):
                gs = groups(tile)
                n_g = gs.stop - gs.start
                js = slice(gs.start // KEY_HEADS, gs.stop // KEY_HEADS)
                picks = slice(gs.start * TOP, gs.stop * TOP)
                place = pick[:, 0:2 * n_g * TOP, :]

                def step(n, ins):
                    ins.then_inc(steps, 1)
                    stop_until(dve, steps, choices(kb, tile) * CHOICE_STEPS + n)

                if piece == 0:
                    stop_until(dve, listed, 2 * (XT * kb + js.stop))
                    halves = best[:, js].rearrange("p j (h s) k -> p (j h) s k", s=2)
                    step(1, nc.vector.tensor_tensor(
                        pair[:, gs], halves[:, :, 0, :].unsqueeze(3).to_broadcast([P, n_g, TOP, TOP]),
                        halves[:, :, 1, :].unsqueeze(2).to_broadcast([P, n_g, TOP, TOP]), ALU.add))
                elif piece == 1:
                    for g in range(gs.start, gs.stop):
                        ins = nc.vector.max(top[:, g, :], pair[:, g].rearrange("p a b -> p (a b)"))
                    step(2, ins)
                elif piece == 2:
                    for g in range(gs.start, gs.stop):
                        ins = nc.vector.max_index(top_at[:, g, :], top[:, g, :], pair[:, g].rearrange("p a b -> p (a b)"))
                    nc.vector.tensor_tensor(prob[:, gs], top[:, gs], top[:, gs, 0:1].to_broadcast([P, n_g, TOP]),
                                            ALU.subtract).then_inc(diffs, 1)
                    step(3, ins)
                elif piece == 3:
                    nc.vector.tensor_scalar(digit[:, gs, 0, :], top_at[:, gs], 3, None, ALU.logical_shift_right)
                    step(4, nc.vector.tensor_scalar(digit[:, gs, 1, :], top_at[:, gs], 7, None, ALU.bitwise_and))
                    flat = digit[:, gs].rearrange("p g s k -> p (g s k)")
                    step(5, nc.vector.tensor_tensor(place, flat.unsqueeze(2).to_broadcast([P, 2 * n_g * TOP, TOP]),
                                                    digits[:].unsqueeze(1).to_broadcast([P, 2 * n_g * TOP, TOP]),
                                                    ALU.is_equal))
                elif piece == 4:
                    place4 = place.rearrange("p (l k) a -> p l k a", k=TOP)
                    at = best_at[:, js].rearrange("p j l a -> p (j l) a").unsqueeze(2)\
                        .to_broadcast([P, 2 * n_g, TOP, TOP])
                    step(6, nc.vector.tensor_tensor(place4, place4, at, ALU.mult))
                elif piece == 5:
                    step(7, nc.vector.tensor_reduce(part[:, gs].rearrange("p g s k -> p (g s k)"), place, AX.X, ALU.add))
                elif piece == 6:
                    step(8, nc.vector.scalar_tensor_tensor(expert[:, gs], part[:, gs, 0, :], float(SUBKEYS),
                                                           part[:, gs, 1, :], ALU.mult, ALU.add))
                    nc.vector.tensor_scalar(expert_at[:, picks], expert[:, gs].rearrange("p g k -> p (g k)"),
                                            float(EXPERTS - 1), None, ALU.min).then_inc(experts, 1)
                else:
                    dve.wait_ge(exps, choices(kb, tile) + 1)
                    step(9, nc.vector.tensor_reduce(prob_sum[:, gs], prob[:, gs], AX.X, ALU.add))
                    step(10, nc.vector.reciprocal(prob_sum[:, gs], prob_sum[:, gs]))
                    step(11, nc.vector.tensor_tensor(
                        prob[:, gs], prob[:, gs], prob_sum[:, gs].unsqueeze(2).to_broadcast([P, n_g, TOP]), ALU.mult))

            def combine(kb, u, quarter):
                n, done = u % 2, (HALVES * kb + u) * 3
                r = rows[:, n]
                if quarter == 0:
                    dve.wait_ge(gathered[n], 16 * HP * (HALVES // 2 * kb + u // 2 + 1))
                    nc.vector.tensor_tensor(prod[:].rearrange("p (k f) -> p k f", f=D_HIDDEN), r,
                                            proj[:, u // 2, :].unsqueeze(1).to_broadcast([P, HP, D_HIDDEN]),
                                            ALU.mult).then_inc(weighed, 1)
                elif quarter == 1:
                    dve.wait_ge(weighed, done + 1)
                    nc.vector.tensor_reduce(dots[:, n, :], prod[:].rearrange("p (k f) -> p k f", f=D_HIDDEN), AX.X,
                                            ALU.add).then_inc(dotted, 1)
                elif quarter == 2:
                    dve.wait_ge(gelued, HALVES * kb + u + 1)
                    w = prob[:].rearrange("p g k -> p (g k)")[:, u * HP:(u + 1) * HP]
                    nc.vector.tensor_tensor(dots[:, n, :], acts[:, n, :], w, ALU.mult).then_inc(weighed, 1)
                    dve.wait_ge(weighed, done + 2)
                    nc.vector.tensor_tensor(r, r, dots[:, n, :].unsqueeze(2).to_broadcast([P, HP, D_HIDDEN]),
                                            ALU.mult).then_inc(weighed, 1)
                else:
                    dve.wait_ge(weighed, done + 3)
                    nc.vector.tensor_reduce(acc[:, u % 4, :], r.rearrange("p k f -> p f k"), AX.X,
                                            ALU.add).then_inc(used, 1)

            def add_keys(o, b, kb, j):
                name = ("keys", j)
                wait_made(dve, o, b, name)
                if j == 0:
                    dve.wait_ge(x_loaded, 16 * (kb + 1))
                x = x_next[:, j, :]
                nc.vector.scalar_tensor_tensor(x, ps_m[o.bank(name)][:, 0:DIM], gate4[:], x, ALU.mult,
                                               ALU.add).then_inc(misc_out[o.bank(name)], 1)

            def route(o, b):
                def step(n, ins):
                    ins.then_inc(route_steps, 1)
                    stop_until(dve, route_steps, b * ROUTE_STEPS + n)

                name = ("router",)
                k = o.bank(name)
                wait_made(dve, o, b, name)
                nc.vector.tensor_copy(rs[:].rearrange("p j e -> p (j e)"), ps_m[k][:, 0:XT * MOE])\
                    .then_inc(misc_out[k], 1)
                stop_until(dve, misc_out[k], o.out(b, name))
                for j in range(XT):
                    ins = nc.vector.max(rs_top[:, j, :], rs[:, j, :])
                step(1, ins)
                for j in range(XT):
                    ins = nc.vector.max_index(rs_at[:, j, :], rs_top[:, j, :], rs[:, j, :])
                step(2, ins)
                every = digits[:].unsqueeze(1).to_broadcast([P, XT, MOE])
                nc.vector.tensor_tensor(gates[:], every, rs_at[:, :, 0:1].to_broadcast([P, XT, MOE]), ALU.is_equal)
                step(3, nc.vector.tensor_tensor(second[:], every, rs_at[:, :, 1:2].to_broadcast([P, XT, MOE]),
                                                ALU.is_equal))
                step(4, nc.vector.tensor_tensor(gates[:], gates[:], second[:], ALU.add))
                dve.wait_ge(sig_ready, b + 1)
                nc.vector.tensor_tensor(gates[:], gates[:], sig[:], ALU.mult).then_inc(gates_ready, 1)

            def gated(b, e):
                dve.wait_ge(gates_in[e % 2], 16 * (MOE // 2 * b + e // 2 + 1))
                nc.vector.tensor_tensor(xg[:, e % 2], xT[:], gates_all[:, e % 2, :].unsqueeze(1)
                                        .to_broadcast([P, DC, SEQ]), ALU.mult).then_inc(xg_ready, 1)

            def add_v_bias(o, b, n):
                name = ("v", n)
                wait_made(dve, o, b, name)
                nc.vector.tensor_tensor(vp[:, 2 * n:2 * n + 2, :].rearrange("p t n -> p (t n)"),
                                        ps_m[o.bank(name)][:], bv[:].rearrange("p t n -> p (t n)"),
                                        ALU.add).then_inc(misc_out[o.bank(name)], 1)

            def batch(b, o, before, b_before):
                keys = o is LOOP
                stop_until(dve, misc_out[before.bank(("keys", XT - 1))], before.out(b_before, ("keys", XT - 1)))
                norm.statistics(dve, 2 * b, x_next)
                if isinstance(b, int) and b == 0:
                    dve.wait_ge(loaded, 16 * N_LOADS)
                for n in range(2):
                    add_v_bias(o, b, n)
                norm.apply(dve, 2 * b, x_next)
                for n in range(2, KT // 2):
                    add_v_bias(o, b, n)
                if keys:
                    for j in range(2):
                        lists(o, b, b + 1, j)
                for kt in range(KT):
                    dve.wait_ge(s_ready, KT * b + kt + 1)
                    if kt >= LOGIT_SLOTS:
                        dve.wait_ge(av_ready, KT * b + kt - LOGIT_SLOTS + 1)
                    nc.vector.scalar_tensor_tensor(logits[:, kt % LOGIT_SLOTS, :], ps_a[kt % 2][:], 0.0,
                                                   maskT[:, kt, :], ALU.max, ALU.add).then_inc(s_out, 1)
                    if keys and kt < 2:
                        lists(o, b, b + 1, 2 + kt)
                    elif keys:
                        choose(b + 1, kt - 2)
                dve.wait_ge(attn_out, b + 1)
                x = x_now[:].rearrange("p j n -> p (j n)")
                if not (isinstance(b, int) and b == 0):
                    dve.wait_ge(stored, 16 * b)
                nc.vector.scalar_tensor_tensor(x, attn, gate[:, 1:2], x_next[:].rearrange("p j n -> p (j n)"),
                                               ALU.mult, ALU.add).then_inc(x_done, 1)
                stop_until(dve, x_done, b + 1)
                norm.statistics(dve, 2 * b + 1, x_now)
                if keys:
                    choose(b + 1, 6)
                norm.apply(dve, 2 * b + 1, x_now)
                route(o, b)
                if keys:
                    choose(b + 1, 7)
                for n in range(BLOCKS + TAIL):
                    if n < BLOCKS:
                        e, f = divmod(n, FT)
                        if f == 2 and e < MOE:
                            gated(b, e)
                        dve.wait_ge(a_out, b * BLOCKS + n + 1)
                        if n >= 2:
                            dve.wait_ge(h_used, b * BLOCKS + n - 1)
                        nc.vector.tensor_tensor(hid[:, n % 2, :], act_in[:, n % 2, :], ps_b[n % 2][:],
                                                ALU.mult).then_inc(h_ready, 1)
                    elif n == BLOCKS:
                        dve.wait_ge(h_used, (b + 1) * BLOCKS)
                        nc.vector.scalar_tensor_tensor(x, ps_o[:].rearrange("p j n -> p (j n)"), gate[:, 3:4], x,
                                                       ALU.mult, ALU.add).then_inc(moe_out, 1)
                    if keys and (half := half_step(n)):
                        combine(b + 1, *half)
                    if keys and (j := tile_at(n, 2)) is not None:
                        add_keys(o, b, b + 1, j)

            for j in range(XT):
                lists(FIRST, 0, 0, j)
                for piece in range(8):
                    choose(0, piece, j)
            for u in range(HALVES):
                for quarter in range(4):
                    combine(0, u, quarter)
                if u % 2:
                    add_keys(FIRST, 0, 0, u // 2)
            batch(0, LOOP, FIRST, 0)
            with dve.Fori(1, BATCH - 1) as b:
                batch(b, LOOP, LOOP, b - 1)
            batch(BATCH - 1, LAST, LOOP, BATCH - 2)

        @block.tensor
        def _(pe):
            def make(o, b, name, kb=None):
                kind, k = name[0], o.bank(name)
                pe.wait_ge(misc_out[k], o.free(b, name))
                out = ps_m[k]
                if kind == "s":
                    _, j, c = name
                    if (j, c) == (0, 0):
                        pe.wait_ge(qn_ready, QC * (kb + 1))
                    ins = nc.tensor.matmul(out[:], qn[:, c, j * P:(j + 1) * P], subkeys[:], start=True, stop=True)
                elif kind == "accT":
                    j = name[1]
                    pe.wait_ge(used, HALVES * kb + 2 * j + 2)
                    for h in range(2):
                        ins = nc.tensor.matmul(out[:, 0:P], acc[:, (2 * j + h) % 4, :], ident[:], start=h == 0,
                                               stop=h == 1)
                elif kind == "keys":
                    j = name[1]
                    wait_out(pe, o, b, ("accT", j))
                    ins = nc.tensor.matmul(out[:, 0:DIM], accT[:, j % 2, :], wkeys[:], start=True, stop=True)
                elif kind == "xT":
                    for j in range(XT):
                        ins = nc.tensor.transpose(out[:, j * P:(j + 1) * P],
                                                  norm.out[:, j, name[2] * P:(name[2] + 1) * P], ident[:])
                elif kind == "k":
                    _, m, h = name
                    for c in range(DC):
                        ins = nc.tensor.matmul(out[:], wk[:, c, m * P:(m + 1) * P], ctxT[:, c, h * HALF:(h + 1) * HALF],
                                               start=c == 0, stop=c == DC - 1)
                elif kind == "q":
                    m = name[1]
                    for c in range(DC):
                        ins = nc.tensor.matmul(out[:], wq[:, c, m * P:(m + 1) * P], xT[:, c, :], start=c == 0,
                                               stop=c == DC - 1)
                elif kind == "v":
                    for t in range(2):
                        kt = 2 * name[1] + t
                        for c in range(DC):
                            ins = nc.tensor.matmul(out[:, t * DIM:(t + 1) * DIM], ctxT[:, c, kt * P:(kt + 1) * P],
                                                   wv[:, c, :], start=c == 0, stop=c == DC - 1)
                elif kind == "router":
                    for j in range(XT):
                        for c in range(DC):
                            ins = nc.tensor.matmul(out[:, j * MOE:(j + 1) * MOE], xT[:, c, j * P:(j + 1) * P],
                                                   router[:, c, :], start=c == 0, stop=c == DC - 1)
                else:
                    pe.wait_ge(gates_ready, b + 1)
                    for j in range(XT):
                        ins = nc.tensor.transpose(out[0:MOE, j * P:(j + 1) * P], gates[:, j, :], ident[:])
                ins.then_inc(misc_made, 1)

            def summed(lhsT, rhs, n, last):
                for j in range(XT):
                    ins = nc.tensor.matmul(ps_o[:, j, :], lhsT(j), rhs, start=n == 0 and j % 2 == 0, stop=n == last,
                                           skip_group_check=True)
                return ins

            def expert_products(b, n):
                e, f = divmod(n, FT)
                slot = 2 if e == 0 else (e - 1) % 2
                if f == 0 and e >= 1:
                    pe.wait_ge(expert_in[slot], 48 * (MOE // 2 * b + (e - 1) // 2 + 1))
                    pe.wait_ge(xg_ready, MOE * b + e)
                if n >= 2:
                    pe.wait_ge(h_ready, b * BLOCKS + n - 1)
                src = xT[:] if e == 0 else xg[:, slot]
                for w, out in ((w_in, ps_a[n % 2]), (w_sw, ps_b[n % 2])):
                    for c in range(DC):
                        ins = nc.tensor.matmul(out[:], w[:, slot, c, f * P:(f + 1) * P], src[:, c, :], start=c == 0,
                                               stop=c == DC - 1)
                ins.then_inc(a_ready, 1)

            def expert_sums(b, n):
                e, f = divmod(n, FT)
                slot = 2 if e == 0 else (e - 1) % 2
                pe.wait_ge(h_ready, b * BLOCKS + n + 1)
                summed(lambda j: hid[:, n % 2, j * P:(j + 1) * P], w_out[:, slot, f, :], n,
                       BLOCKS - 1).then_inc(h_used, 1)

            def batch(b, o):
                keys = o is LOOP
                for name in o.names[:o.no[("q", DC - 1)] + 1 + (2 * QC if keys else 0)]:
                    if name == ("xT", 0, 0):
                        pe.wait_ge(norm.ready, 2 * b + 1)
                    if name == ("q", 0):
                        for n in (2, 3):
                            wait_out(pe, o, b, ("v", n))
                    make(o, b, name, b + 1)
                for c in range(DC):
                    wait_out(pe, o, b, ("q", c))
                for kt in range(KT + 1):
                    if kt < KT:
                        if kt >= 2:
                            pe.wait_ge(s_out, KT * b + kt - 1)
                        for c in range(DC):
                            ins = nc.tensor.matmul(ps_a[kt % 2][:], kp[:, c, kt * P:(kt + 1) * P], qp[:, c, :],
                                                   start=c == 0, stop=c == DC - 1)
                        ins.then_inc(s_ready, 1)
                    if kt >= 1:
                        k = kt - 1
                        pe.wait_ge(relued, KT // 2 * b + k // 2 + 1)
                        pe.wait_ge(s_out, KT * b + k + 1)
                        summed(lambda j: logits[:, k % LOGIT_SLOTS, j * P:(j + 1) * P], vp[:, k, :], k,
                               KT - 1).then_inc(av_ready, 1)
                if keys:
                    pe.wait_ge(ctx_loaded, 16 * (b + 2))
                    for m in range(DC):
                        for h in range(2):
                            make(o, b, ("k", m, h))
                pe.wait_ge(norm.ready, 2 * b + 2)
                for c in range(DC):
                    make(o, b, ("xT", 1, c))
                for c in range(DC):
                    wait_out(pe, o, b, ("xT", 1, c))
                make(o, b, ("router",))
                for n in range(BLOCKS + TAIL):
                    if n == GATES_AT:
                        make(o, b, ("gatesT",))
                    if n < BLOCKS:
                        expert_products(b, n)
                    if 1 <= n <= BLOCKS:
                        expert_sums(b, n - 1)
                    if keys and (j := tile_at(n, 1)) is not None:
                        make(o, b, ("accT", j), b + 1)
                    if keys and (j := tile_at(n, 2)) is not None:
                        make(o, b, ("keys", j))

            pe.wait_ge(keys_loaded, 16 * N_KEY_LOADS)
            for name in FIRST.names:
                if name == ("k", 0, 0):
                    pe.wait_ge(loaded, 16 * N_LOADS)
                    pe.wait_ge(ctx_loaded, 16)
                make(FIRST, 0, name, 0)
            with pe.Fori(0, BATCH - 1) as b:
                batch(b, LOOP)
            batch(BATCH - 1, LAST)


def program(nc, d):
    with ExitStack() as ctx:
        def sem(name):
            return ctx.enter_context(nc.semaphore(name))

        d["x_dram"] = nc.dram_tensor("x_after_attention", [BATCH, P, XT, DIM], F32).ap()
        d["table"] = nc.dram_tensor("hidden_table", [EXPERTS, D_HIDDEN], F32).ap()
        d["q_dram"] = nc.dram_tensor("keys_queries", [BATCH, P, QC, SEQ], F32).ap()
        d["proj_dram"] = nc.dram_tensor("keys_projections", [BATCH, P, XT, D_HIDDEN], F32).ap()
        d["gates_dram"] = nc.dram_tensor("gates_by_expert", [MOE, SEQ], F32).ap()
        sh = Shared(nc, ctx)
        rope_attention(nc, sh, d)
        ks = KeyState(nc, ctx)
        key_queries(nc, sh, ks, d, sem)
        keys_and_layer1(nc, sh, ks, d, sem)



def tokens(a):
    b, s, f = a.shape
    return np.ascontiguousarray(a.reshape(b, s // P, P, f).transpose(0, 2, 1, 3))


def columns(a):
    return np.ascontiguousarray(a.reshape(-1, P).T)


def layout(a):
    x0, f0, x1, f1 = "L0_xattn_", "L0_ffn_", "L1_xattn_", "L1_ffn_"
    w2 = a[f0 + "W2"]
    ctx = a["ctx_1024"]
    return {
        "x": tokens(a["x"]),
        "ctx": tokens(ctx),
        "ctxT": ctx.transpose(0, 2, 1).reshape(BATCH, DC, P, CTX).transpose(0, 2, 1, 3),
        "gates": np.concatenate([a["g_xattn"], a["g_ffn"]])[None, :],
        "wq": a[x0 + "Wq"], "wkv": a[x0 + "Wkv"], "wo": a[x0 + "Wo"], "bo": a[x0 + "bo"][None, :],
        "cosT": np.tile(a[x0 + "cos"].T, (P // (DHEAD // 2), 1)),
        "sinT": np.tile(a[x0 + "sin"].T, (P // (DHEAD // 2), 1)),
        "lat_g": columns(a[x0 + "ln_lat_g"]), "lat_b": columns(a[x0 + "ln_lat_b"]),
        "ctx_g": columns(a[x0 + "ln_ctx_g"]), "ctx_b": columns(a[x0 + "ln_ctx_b"]),
        "keys_wqT": a[f0 + "Wq"].reshape(QC * P, DIM).T,
        "keys_bq": columns(a[f0 + "bq"]), "keys_gamma": columns(a[f0 + "gamma"]),
        "keys_beta": columns(a[f0 + "beta"]),
        "sk1T": a[f0 + "sk1"].T, "sk2T": a[f0 + "sk2"].T,
        "latentsT": a[f0 + "latents"].T, "w1": a[f0 + "W1"],
        "w2xT": w2[:, :DIM].T, "w2v": w2[:, DIM:],
        "l1_wq": a[x1 + "kernel_q"][0, 0], "l1_wk": a[x1 + "kernel_k"][0, 0], "l1_wv": a[x1 + "kernel_v"][0, 0],
        "l1_bq": columns(a[x1 + "bias_q"]), "l1_bk": columns(a[x1 + "bias_k"]), "l1_bv": a[x1 + "bias_v"][None, :],
        "maskT": a["mask_1xSxS2_ff0"][0].T,
        "router": a[f1 + "router_DE"],
        "w_in_shared": a[f1 + "w_in_shared_FD"].T, "w_sw_shared": a[f1 + "w_swiglu_FD"].T,
        "w_out_shared": a[f1 + "w_out_shared_DF"].T,
        "w_in": a[f1 + "w_in_eDF"], "w_sw": a[f1 + "w_swiglu_eDF"], "w_out": a[f1 + "w_out_eFD"],
    }


def kernel(**inputs):
    import concourse.bacc as bacc
    from concourse.bass_utils import run_bass_kernel_spmd

    nc = bacc.Bacc("TRN2", target_bir_lowering=False, num_devices=1)
    arrays, d = {}, {}
    for name, a in layout({k: np.asarray(v) for k, v in inputs.items()}).items():
        a = np.ascontiguousarray(a)
        arrays["in_" + name] = a
        d[name] = nc.dram_tensor("in_" + name, a.shape, mybir.dt.from_np(a.dtype), kind="ExternalInput").ap()
    d["out"] = nc.dram_tensor("out", (BATCH, P, XT, DIM), F32, kind="ExternalOutput").ap()
    program(nc, d)
    out = run_bass_kernel_spmd(nc, [arrays], core_ids=[0]).results[0]["out"]
    return np.ascontiguousarray(out.transpose(0, 2, 1, 3)).reshape(BATCH, SEQ, DIM)
```
